# Optimizing a Trainium2 kernel written in Bass

```python
import numpy as np
import jax
import jax.numpy as jnp

def _softmax(x, axis=-1):
    return jax.nn.softmax(x, axis=axis)

def _gelu(x):
    return jax.nn.gelu(x, approximate=True)

def _silu(x):
    return jax.nn.silu(x)

def _sigmoid(x):
    return jax.nn.sigmoid(x)

def _layernorm(x, axis=-1, eps=1e-05):
    m = jnp.mean(x, axis=axis, keepdims=True)
    v = jnp.var(x, axis=axis, keepdims=True)
    return (x - m) / jnp.sqrt(v + eps)

def _scatter_add(tgt, idx, src, axis=0):
    return tgt.at[idx].add(src)

def _segment_sum(src, seg, n):
    return jax.ops.segment_sum(src, seg, n)
kernel_name = 'mk_seq_preln_d1_jaxref_r8_f56290'

def setup_inputs(seed: int=0):
    np.random.seed(seed)
    _w = jnp.asarray

    def _L0_attn_setup():
        import math
        import jax, jax.numpy as jnp
        import numpy as np
        DIM = 128
        N_HEADS = 16
        HEAD_DIM = DIM // N_HEADS
        SEQ_LEN = 256
        BASE = 10000.0
        EPS = 1e-05

        def rope_cache(seq_len, dim):
            pos = jnp.arange(seq_len, dtype=jnp.float32)[:, None]
            di = jnp.arange(0, dim, 2, dtype=jnp.float32) / dim
            theta = pos * jnp.exp(-di * math.log(BASE))
            cos = jnp.repeat(jnp.cos(theta), 2, axis=1)
            sin = jnp.repeat(jnp.sin(theta), 2, axis=1)
            return (cos, sin)

        def rotate_half(x):
            x1 = x[..., ::2]
            x2 = x[..., 1::2]
            return jnp.concatenate((-x2, x1), axis=-1)

        def layernorm(x, gamma, beta):
            mu = jnp.mean(x, axis=-1, keepdims=True)
            var = jnp.var(x, axis=-1, keepdims=True)
            return (x - mu) * jax.lax.rsqrt(var + EPS) * gamma + beta
        key = jax.random.key(seed)
        ks = jax.random.split(key, 7)
        s = 1.0 / math.sqrt(DIM)
        return {'x': jax.random.normal(ks[0], (2, SEQ_LEN, DIM), dtype=jnp.float32), 'Wq': jax.random.normal(ks[1], (DIM, DIM), dtype=jnp.float32) * s, 'Wk': jax.random.normal(ks[2], (DIM, DIM), dtype=jnp.float32) * s, 'Wv': jax.random.normal(ks[3], (DIM, DIM), dtype=jnp.float32) * s, 'q_gamma': jnp.ones((HEAD_DIM,), jnp.float32), 'q_beta': jnp.zeros((HEAD_DIM,), jnp.float32), 'k_gamma': jnp.ones((HEAD_DIM,), jnp.float32), 'k_beta': jnp.zeros((HEAD_DIM,), jnp.float32), 'Wo': jax.random.normal(ks[4], (DIM, DIM), dtype=jnp.float32) * s, 'bo': jnp.zeros((DIM,), jnp.float32)}
    _L0_attn_in = _L0_attn_setup()

    def _L0_ffn_setup():
        import jax, jax.numpy as jnp
        import numpy as np
        DIM = 128
        E = 16
        TOPK = 2
        G = 4
        TOPK_G = 2
        INTER = 64
        N_SHARED = 2
        ROUTE_SCALE = 1.0

        def _gate(xf, gate_w, gate_b):
            scores = xf @ gate_w.T
            scores = jax.nn.softmax(scores.astype(jnp.float32), axis=-1)
            orig = scores
            scores = scores + gate_b
            T = xf.shape[0]
            sg = scores.reshape(T, G, E // G)
            group_scores = jax.lax.top_k(sg, 2)[0].sum(-1)
            _, gidx = jax.lax.top_k(group_scores, TOPK_G)
            keep = jax.nn.one_hot(gidx, G).sum(axis=1) > 0
            sg = jnp.where(keep[:, :, None], sg, -jnp.inf)
            scores = sg.reshape(T, E)
            _, idx = jax.lax.top_k(scores, TOPK)
            weights = jnp.take_along_axis(orig, idx, axis=1)
            weights = (weights * ROUTE_SCALE).astype(xf.dtype)
            return (weights, idx)
        key = jax.random.key(seed)
        ks = jax.random.split(key, 16)
        s = lambda fan_in: 1.0 / np.sqrt(fan_in)
        inp = {'x': jax.random.normal(ks[0], (4, 128, DIM), dtype=jnp.float32), 'gate_w': jax.random.normal(ks[1], (E, DIM), dtype=jnp.float32) * s(DIM), 'gate_b': jnp.zeros((E,), dtype=jnp.float32), 'We1': jax.random.normal(ks[2], (E, DIM, INTER), dtype=jnp.float32) * s(DIM), 'be1': jnp.zeros((E, INTER), dtype=jnp.float32), 'We2': jax.random.normal(ks[3], (E, INTER, DIM), dtype=jnp.float32) * s(INTER), 'be2': jnp.zeros((E, DIM), dtype=jnp.float32), 'We3': jax.random.normal(ks[4], (E, DIM, INTER), dtype=jnp.float32) * s(DIM), 'be3': jnp.zeros((E, INTER), dtype=jnp.float32), 'ws1': jax.random.normal(ks[5], (DIM, N_SHARED * INTER), dtype=jnp.float32) * s(DIM), 'bs1': jnp.zeros((N_SHARED * INTER,), dtype=jnp.float32), 'ws2': jax.random.normal(ks[6], (N_SHARED * INTER, DIM), dtype=jnp.float32) * s(N_SHARED * INTER), 'bs2': jnp.zeros((DIM,), dtype=jnp.float32), 'ws3': jax.random.normal(ks[7], (DIM, N_SHARED * INTER), dtype=jnp.float32) * s(DIM), 'bs3': jnp.zeros((N_SHARED * INTER,), dtype=jnp.float32)}
        return inp
    _L0_ffn_in = _L0_ffn_setup()
    _d = {'L0_attn_x': _L0_attn_in['x'], 'L0_attn_Wq': _L0_attn_in['Wq'], 'L0_attn_Wk': _L0_attn_in['Wk'], 'L0_attn_Wv': _L0_attn_in['Wv'], 'L0_attn_q_gamma': _L0_attn_in['q_gamma'], 'L0_attn_q_beta': _L0_attn_in['q_beta'], 'L0_attn_k_gamma': _L0_attn_in['k_gamma'], 'L0_attn_k_beta': _L0_attn_in['k_beta'], 'L0_attn_Wo': _L0_attn_in['Wo'], 'L0_attn_bo': _L0_attn_in['bo'], 'L0_ffn_gate_w': _L0_ffn_in['gate_w'], 'L0_ffn_gate_b': _L0_ffn_in['gate_b'], 'L0_ffn_We1': _L0_ffn_in['We1'], 'L0_ffn_be1': _L0_ffn_in['be1'], 'L0_ffn_We2': _L0_ffn_in['We2'], 'L0_ffn_be2': _L0_ffn_in['be2'], 'L0_ffn_We3': _L0_ffn_in['We3'], 'L0_ffn_be3': _L0_ffn_in['be3'], 'L0_ffn_ws1': _L0_ffn_in['ws1'], 'L0_ffn_bs1': _L0_ffn_in['bs1'], 'L0_ffn_ws2': _L0_ffn_in['ws2'], 'L0_ffn_bs2': _L0_ffn_in['bs2'], 'L0_ffn_ws3': _L0_ffn_in['ws3'], 'L0_ffn_bs3': _L0_ffn_in['bs3']}
    _x0 = _d['L0_attn_x']
    _d['L0_attn_x'] = jax.random.normal(jax.random.fold_in(jax.random.key(seed), 1), (2, 1024, 128), dtype=_x0.dtype)
    del _x0
    return _d

def reference(L0_attn_x, L0_attn_Wq, L0_attn_Wk, L0_attn_Wv, L0_attn_q_gamma, L0_attn_q_beta, L0_attn_k_gamma, L0_attn_k_beta, L0_attn_Wo, L0_attn_bo, L0_ffn_gate_w, L0_ffn_gate_b, L0_ffn_We1, L0_ffn_be1, L0_ffn_We2, L0_ffn_be2, L0_ffn_We3, L0_ffn_be3, L0_ffn_ws1, L0_ffn_bs1, L0_ffn_ws2, L0_ffn_bs2, L0_ffn_ws3, L0_ffn_bs3):

    def _L0_attn_ref(x, Wq, Wk, Wv, q_gamma, q_beta, k_gamma, k_beta, Wo, bo):
        import math
        import jax, jax.numpy as jnp
        import numpy as np
        DIM = 128
        N_HEADS = 16
        HEAD_DIM = DIM // N_HEADS
        SEQ_LEN = 256
        BASE = 10000.0
        EPS = 1e-05

        def rope_cache(seq_len, dim):
            pos = jnp.arange(seq_len, dtype=jnp.float32)[:, None]
            di = jnp.arange(0, dim, 2, dtype=jnp.float32) / dim
            theta = pos * jnp.exp(-di * math.log(BASE))
            cos = jnp.repeat(jnp.cos(theta), 2, axis=1)
            sin = jnp.repeat(jnp.sin(theta), 2, axis=1)
            return (cos, sin)

        def rotate_half(x):
            x1 = x[..., ::2]
            x2 = x[..., 1::2]
            return jnp.concatenate((-x2, x1), axis=-1)

        def layernorm(x, gamma, beta):
            mu = jnp.mean(x, axis=-1, keepdims=True)
            var = jnp.var(x, axis=-1, keepdims=True)
            return (x - mu) * jax.lax.rsqrt(var + EPS) * gamma + beta
        B, S, D = x.shape
        H, hd = (N_HEADS, HEAD_DIM)
        q = (x @ Wq.T).reshape(B, S, H, hd).transpose(0, 2, 1, 3)
        k = (x @ Wk.T).reshape(B, S, H, hd).transpose(0, 2, 1, 3)
        v = (x @ Wv.T).reshape(B, S, H, hd).transpose(0, 2, 1, 3)
        q = layernorm(q, q_gamma, q_beta)
        k = layernorm(k, k_gamma, k_beta)
        cos, sin = rope_cache(S, hd)
        cos = cos[None, None]
        sin = sin[None, None]
        q = q * cos + rotate_half(q) * sin
        k = k * cos + rotate_half(k) * sin
        scale = 1.0 / math.sqrt(hd)
        scores = scale * jnp.einsum('bhqd,bhkd->bhqk', q, k)
        mask = jnp.tril(jnp.ones((S, S), dtype=bool))
        scores = jnp.where(mask, scores, -jnp.inf)
        attn = jax.nn.softmax(scores, axis=-1)
        out = jnp.einsum('bhqk,bhkd->bhqd', attn, v)
        out = out.transpose(0, 2, 1, 3).reshape(B, S, D)
        return out @ Wo.T + bo

    def _L0_ffn_ref(x, gate_w, gate_b, We1, be1, We2, be2, We3, be3, ws1, bs1, ws2, bs2, ws3, bs3):
        import jax, jax.numpy as jnp
        import numpy as np
        DIM = 128
        E = 16
        TOPK = 2
        G = 4
        TOPK_G = 2
        INTER = 64
        N_SHARED = 2
        ROUTE_SCALE = 1.0

        def _gate(xf, gate_w, gate_b):
            scores = xf @ gate_w.T
            scores = jax.nn.softmax(scores.astype(jnp.float32), axis=-1)
            orig = scores
            scores = scores + gate_b
            T = xf.shape[0]
            sg = scores.reshape(T, G, E // G)
            group_scores = jax.lax.top_k(sg, 2)[0].sum(-1)
            _, gidx = jax.lax.top_k(group_scores, TOPK_G)
            keep = jax.nn.one_hot(gidx, G).sum(axis=1) > 0
            sg = jnp.where(keep[:, :, None], sg, -jnp.inf)
            scores = sg.reshape(T, E)
            _, idx = jax.lax.top_k(scores, TOPK)
            weights = jnp.take_along_axis(orig, idx, axis=1)
            weights = (weights * ROUTE_SCALE).astype(xf.dtype)
            return (weights, idx)
        shape = x.shape
        xf = x.reshape(-1, DIM)
        weights, idx = _gate(xf, gate_w, gate_b)
        combine = (jax.nn.one_hot(idx, E, dtype=xf.dtype) * weights[..., None]).sum(1)
        h1 = jnp.einsum('td,edi->tei', xf, We1) + be1
        h3 = jnp.einsum('td,edi->tei', xf, We3) + be3
        h = jax.nn.silu(h1) * h3
        yo = jnp.einsum('tei,eid->ted', h, We2) + be2
        y = jnp.einsum('te,ted->td', combine, yo)
        z = jax.nn.silu(xf @ ws1 + bs1) * (xf @ ws3 + bs3) @ ws2 + bs2
        return (y + z).reshape(shape)
    x = L0_attn_x
    x = x + _L0_attn_ref(_layernorm(x, axis=-1), L0_attn_Wq, L0_attn_Wk, L0_attn_Wv, L0_attn_q_gamma, L0_attn_q_beta, L0_attn_k_gamma, L0_attn_k_beta, L0_attn_Wo, L0_attn_bo)
    x = x + _L0_ffn_ref(_layernorm(x, axis=-1), L0_ffn_gate_w, L0_ffn_gate_b, L0_ffn_We1, L0_ffn_be1, L0_ffn_We2, L0_ffn_be2, L0_ffn_We3, L0_ffn_be3, L0_ffn_ws1, L0_ffn_bs1, L0_ffn_ws2, L0_ffn_bs2, L0_ffn_ws3, L0_ffn_bs3)
    return x

_drawn_inputs = setup_inputs


def setup_inputs(seed=0):
    import zlib

    import numpy as np

    out = dict(_drawn_inputs(seed))
    spreads = {'L0_attn_q_gamma': (1.0, 0.2),
     'L0_attn_q_beta': (0.0, 0.423),
     'L0_attn_k_gamma': (1.0, 0.2),
     'L0_attn_k_beta': (0.0, 0.483),
     'L0_attn_bo': (0.0, 0.1),
     'L0_ffn_gate_b': (0.0, 0.1),
     'L0_ffn_be1': (0.0, 0.551),
     'L0_ffn_be2': (0.0, 0.349),
     'L0_ffn_be3': (0.0, 0.562),
     'L0_ffn_bs1': (0.0, 0.1),
     'L0_ffn_bs2': (0.0, 0.1),
     'L0_ffn_bs3': (0.0, 0.1)}
    factors = {}
    for name, (base, spread) in spreads.items():
        noise = np.random.default_rng([zlib.crc32(name.encode()), seed]).standard_normal(out[name].shape)
        drawn = base * np.exp(spread * noise) if base else spread * noise
        out[name] = jnp.asarray(drawn.astype(out[name].dtype))
    for name, factor in factors.items():
        out[name] = (out[name] * factor).astype(out[name].dtype)
    return out
```

```python
from contextlib import ExitStack

import numpy as np
import concourse.bass as bass
from concourse import mybir

F32 = mybir.dt.float32
BF16 = mybir.dt.bfloat16
ALU = mybir.AluOpType
ACT = mybir.ActivationFunctionType
AX = mybir.AxisListType

P = 128
B, S, D = 2, 1024, 128
H, HD = 16, 8
E, INTER, NGRP = 16, 64, 4
CH = 512
NX = B * S // CH
TPC = CH // P
KT = S // P
G = 4
NG = H // G
NA = NX * NG
PAIRS = E // 2
UNITS = PAIRS + 1
HALF = CH // 2
SCALE = float(HD) ** -0.5
EPS = 1e-5
TERMS_Q = [0, 0, 1, 1, 0, 2]
TERMS_K = [0, 1, 0, 1, 2, 0]
KR = 8 * len(TERMS_Q)
KM = KR + 2
VC = 16
MASKED = -1e30
TWO_ONES = float(np.array([0x3F803F80], np.uint32).view(np.float32)[0])
ST_RING, P_RING, MAX_RING = 3, 12, 2
ST_BANK, ACC_BANK, MAX_BANK, WORK_BANK, Y_BANK = 0, 3, 4, 6, 7


def bursts_of(c):
    out = [[([(j, kt, 0, CH, 0)], None) for j in range(G)] for kt in range(4 * c)]
    out.append([([(j, 4 * c, 0, CH, 0)], slice(0, 1)) for j in range(G)])
    out.append([([(j, 4 * c + 1, 0, 384, 128), (j, 4 * c + 3, 384, 128, 384)], slice(0, 4, 3)) for j in range(G)])
    out.append([([(j, 4 * c + 2, 0, 256, 256), (j + 2, 4 * c + 2, 256, 256, 256)], slice(0, 4, 2)) for j in range(2)])
    return out


def max_units_of(c):
    units = [("full", qt, [j], 512) for qt in range(TPC) for j in range(G)] if c else []
    for qt in range(TPC):
        keys = P * (qt + 1)
        for j in range(2):
            units += [("diag", qt, [j, j + 2], keys)] if qt < 2 else [("diag", qt, [j], keys), ("diag", qt, [j + 2], keys)]
    return units


def plan():
    bursts = [(a, k) for a in range(NA) for k in range(len(bursts_of(a // NG % 2)))]
    first = {a: min(s for s, (q, _) in enumerate(bursts) if q == a) for a in range(NA)}
    first[NA] = len(bursts)
    side = {s: [] for s in range(len(bursts))}

    def spread(pieces, start, end):
        for n, piece in enumerate(pieces):
            side[start + n * (end - start) // len(pieces)].append(piece)

    def prep(x):
        return [("norm", x), ("xT", x)] + [("qkv", TPC * x + t) for t in range(TPC)] + [
            ("headnorm", x), ("rope", x), ("qT", x), ("kT", x)]

    def epilogue(x):
        return [(n, x) for n in ("onT", "proj", "norm2", "x2T", "gate", "cT")]

    def moe(x):
        return [("moe", (x, n)) for n in range(2 * UNITS + 1)] + [("final", x)]

    spread(prep(1), 0, first[2])
    spread(prep(2), first[3], first[5])
    spread(prep(3), first[7], first[9])
    spread(epilogue(0), first[4] + 3, first[5] + 3)
    spread(moe(0), first[5] + 3, first[8])
    spread(epilogue(1), first[8] + 2, first[11])
    spread(moe(1), first[11], first[13])
    spread(epilogue(2), first[12] + 3, first[13] + 3)
    spread(moe(2), first[13] + 3, first[16])

    order = [("weights", 0), ("weights2", 0)] + prep(0)
    for a in (0, 1):
        order += [("max", (a, u)) for u in range(len(max_units_of(0)))] + [("mfin", a)]
    for s, (a, k) in enumerate(bursts):
        banks = bursts_of(a // NG % 2)[k]
        ahead = []
        if a + 2 < NA:
            n, m = len(max_units_of((a + 2) // NG % 2)), first[a + 1] - first[a]
            ahead = [("max", (a + 2, u)) for u in range(n * k // m, n * (k + 1) // m)]
            if k == m - 1:
                ahead.append(("mfin", a + 2))
        late = [("pv", s - 2)] if s >= 2 else []
        if s >= 2 and bursts[s - 2][0] != bursts[s - 1][0]:
            late.append(("oT", bursts[s - 2][0]))
        fill = ahead + side[s]
        for i in range(len(banks)):
            order.append(("scores", (s, i)))
            order += fill[i * len(fill) // len(banks):(i + 1) * len(fill) // len(banks)]
            if i == 1:
                order += late[:1]
        order += late[1:]
    n = len(bursts)
    order += [("pv", n - 2), ("pv", n - 1), ("oT", NA - 1)] + epilogue(NX - 1) + moe(NX - 1)
    return bursts, order


BURSTS, SCHEDULE = plan()
BANKS = {key: n for n, key in enumerate(arg for kind, arg in SCHEDULE if kind == "scores")}
BANKS_TO = {s: max(n for (q, _), n in BANKS.items() if q == s) + 1 for s in range(len(BURSTS))}
MASKS_TO = {}
for _s in range(len(BURSTS)):
    MASKS_TO[_s] = sum(bank[1] is not None for q in range(_s + 1)
                       for bank in bursts_of(BURSTS[q][0] // NG % 2)[BURSTS[q][1]])
MAXES = {arg: n for n, arg in enumerate(arg for kind, arg in SCHEDULE if kind == "max")}
LAST_READER = {"weights": "act", "weights2": "act", "xT": "act", "qkv": "act", "qT": "dve", "kT": "dve",
               "mfin": "dve", "oT": "dve", "onT": "act", "proj": "dve", "x2T": "act", "gate": "dve",
               "cT": "dve", "moe": "experts"}
FILLS = [(kind, arg) for kind, arg in SCHEDULE
         if kind in LAST_READER and not (kind == "moe" and arg[1] == 2 * UNITS)]
FILL = {key: n for n, key in enumerate(FILLS)}
LAST_MAX = max(n for n, (kind, _) in enumerate(SCHEDULE) if kind == "max")
EARLY = FILL["kT", 0] + 1
LATE = min(n for n, key in enumerate(FILLS) if SCHEDULE.index(key) > LAST_MAX)
FILL_BANK = [WORK_BANK if EARLY <= n < LATE else (WORK_BANK, MAX_BANK, MAX_BANK + 1)[n % 3]
             for n in range(len(FILLS))]


def banks_before(a):
    return sum(BURSTS[s][0] < a for s, _ in BANKS)


def frees(reader, upto):
    return sum(LAST_READER[FILLS[n][0]] == reader for n in range(upto))


def layer_kernel(nc, x, Wq, Wk, Wv, q_gamma, q_beta, k_gamma, k_beta, Wo, bo, gate_w, gate_b,
                 We1, be1, We2, be2, We3, be3, ws1, bs1, ws2, bs2, ws3, bs3,
                 c_ident, c_center, c_causal, c_rope, c_rank, out):
    x_v = x.rearrange("b (h t p) d -> (b h) p t d", p=P, t=TPC)
    out_v = out.rearrange("b (h t p) d -> (b h) p t d", p=P, t=TPC)
    combine_dram = nc.dram_tensor("combine_scratch", [NX, E, CH], F32, kind="Internal").ap()

    with ExitStack() as ctx:
        def sb(name, shape, dt=F32):
            return ctx.enter_context(nc.sbuf_tensor(name, shape, dt))

        def sem(name):
            return ctx.enter_context(nc.semaphore(name))

        psum = ctx.enter_context(nc.psum_tensor("psum", [P, 8, 512], F32))

        ident = sb("ident", [P, P])
        ident_bf = sb("ident_bf", [P, P], BF16)
        center = sb("center", [P, P])
        causal = sb("causal", [P, P])
        causal_bf = sb("causal_bf", [P, P], BF16)
        rope = sb("rope", [P, KT, 2, HD])
        rank = sb("rank", [P, E])
        w_raw = sb("w_raw", [P, 4, P])
        gate_raw = sb("gate_raw", [E, P])
        w_qkv = sb("w_qkv", [P, 3 * P])
        w_o = sb("w_o", [P, P + E])
        gb = sb("gb", [P, 4, HD])
        gb_rot = sb("gb_rot", [P, 4, HD])
        g_cos = sb("g_cos", [P, 2, KT, HD])
        g_sin = sb("g_sin", [P, 2, KT, HD])
        g_add = sb("g_add", [P, 2, KT, HD])
        g_tmp = sb("g_tmp", [P, 2, KT, HD])
        bo_b = sb("bo_b", [P, P])
        gate_bb = sb("gate_bb", [P, E])
        w1 = sb("w1", [P, UNITS, P])
        w3 = sb("w3", [P, UNITS, P])
        w2 = sb("w2", [P, UNITS, P])
        b1 = sb("b1", [P, UNITS])
        b1h = sb("b1h", [P, UNITS])
        b3 = sb("b3", [P, UNITS])
        b2 = sb("b2", [E + 1, P])
        expo = sb("expo", [P, P])
        xs = sb("xs", [P, NX, TPC, P])
        xn = sb("xn", [P, TPC, P])
        xnT = sb("xnT", [P, CH])
        stats = sb("stats", [P, TPC, 6])
        mv = sb("mv", [P, TPC, 2])
        veps = sb("veps", [P, TPC])
        rstd = sb("rstd", [P, TPC])
        qk = sb("qk", [P, 2, TPC, H, HD])
        sq = sb("sq", [P, 2, TPC, H, HD])
        ssum = sb("ssum", [P, 2 * TPC * H])
        hvar = sb("hvar", [P, 2 * TPC * H])
        hrstd = sb("hrstd", [P, 2 * TPC * H])
        rot = sb("rot", [P, 2, TPC, H, HD])
        roped = sb("roped", [P, 2, TPC, 2, HD, H // 2])
        parts = sb("parts", [P, 2, 3, CH], BF16)
        resid = sb("resid", [P, 2, CH])
        q_st = sb("q_st", [P, 2, H // 2, CH], BF16)
        k_st = sb("k_st", [P, B, H // 2, S], BF16)
        v_ones = sb("v_ones", [P, B, KT, H, VC])
        mx_full = sb("mx_full", [P, TPC, 2, 2])
        mx_diag = sb("mx_diag", [P, TPC, 2, 2])
        mx = sb("mx", [P, TPC * 2, 2])
        negmax = sb("negmax", [P, TPC * 2, 2, 2], BF16)
        maxT = sb("maxT", [8, 2, CH], BF16)
        probs = sb("probs", [P, P_RING, CH])
        o_raw = sb("o_raw", [P, CH])
        rden = sb("rden", [P, TPC, G, 1])
        o_norm = sb("o_norm", [P, TPC, P])
        o_normT = sb("o_normT", [P, CH])
        x2T = sb("x2T", [P, 2, CH])
        lg = sb("lg", [P, 12, TPC, E])
        gsm = sb("gsm", [P, 16, TPC, NGRP])
        pair_sums = sb("pair_sums", [P, TPC * NGRP, 6])
        red = sb("red", [P, 8, TPC])
        combT = sb("combT", [E + 1, CH])
        comb_b = sb("comb_b", [P, PAIRS, CH])
        mu = sb("mu", [P, 2, HALF])
        mt = sb("mt", [P, 2, HALF])
        mw = sb("mw", [P, HALF])
        mh = sb("mh", [P, 2, HALF])
        mhc = sb("mhc", [P, 2, HALF])
        fin = sb("fin", [P, TPC, P])

        ld_x = [sem(f"ld_x{i}") for i in range(NX)]
        ld_attn = sem("ld_attn")
        ld_rope = sem("ld_rope")
        ld_moe = sem("ld_moe")
        ld_combine = sem("ld_combine")
        st_combine = sem("st_combine")
        stacked = [sem(f"stacked{i}") for i in range(NX)]
        maxrow_in = [sem(f"maxrow_in{i}") for i in range(2)]
        stored = sem("stored")
        scores_full = sem("scores_full")
        max_full = sem("max_full")
        work_full = sem("work_full")
        pv_done = sem("pv_done")
        y_done = sem("y_done")
        exp_done = sem("exp_done")
        work_read_act = sem("work_read_act")
        part_hi = sem("part_hi")
        gate_exp = sem("gate_exp")
        act_u = sem("act_u")
        act_t = sem("act_t")
        v_set = sem("v_set")
        k_set = sem("k_set")
        masked = sem("masked")
        pool_chain = sem("pool_chain")
        rstd_ready = sem("rstd_ready")
        hrstd_ready = sem("hrstd_ready")
        rope_direct_ready = sem("rope_direct_ready")
        parts_lo = sem("parts_lo")
        xbo_ready = sem("xbo_ready")
        weighted = sem("weighted")
        consts = sem("consts")
        tables_ready = sem("tables_ready")
        rope_a = sem("rope_a")
        chain = sem("chain")
        max_free = sem("max_free")
        work_read_dve = sem("work_read_dve")
        var_ready = sem("var_ready")
        xn_ready = sem("xn_ready")
        hsum_ready = sem("hsum_ready")
        roped_ready = sem("roped_ready")
        neg_ready = sem("neg_ready")
        o_ready = sem("o_ready")
        comb_ready = sem("comb_ready")
        h_ready = sem("h_ready")
        h_used = sem("h_used")
        out_ready = sem("out_ready")

        N_ATTN, N_ROPE, N_MOE = 7, 6, 15

        def bank(n):
            return psum[:, n, :]

        def wbank(kind, arg):
            return bank(FILL_BANK[FILL[kind, arg]])

        def turned(kind, arg):
            return FILL[kind, arg] + 1

        def norm_at(kind, x):
            return [q for q in SCHEDULE if q[0] in ("norm", "norm2")].index((kind, x))

        block = ctx.enter_context(nc.Block())

        @block.sync
        def _(sp):
            for w, dst in ((Wq, 0), (Wk, 1), (Wv, 2), (Wo, 3)):
                sp.dma_start(w_raw[:, dst, :], w).then_inc(ld_attn, 16)
            sp.dma_start(ident[:, :], c_ident).then_inc(ld_attn, 16)
            sp.dma_start(center[:, :], c_center).then_inc(ld_attn, 16)
            sp.dma_start(gate_raw[:, :], gate_w).then_inc(ld_attn, 16)
            sp.dma_start(rope[:, :, :, :], c_rope).then_inc(ld_rope, 16)
            for n, v in enumerate((q_gamma, q_beta, k_gamma, k_beta)):
                sp.dma_start(gb[:, n, :], v.partition_broadcast(P)).then_inc(ld_rope, 16)
            sp.dma_start(bo_b[:, :], bo.partition_broadcast(P)).then_inc(ld_rope, 16)
            for i in range(1, NX):
                sp.dma_start(xs[:, i, :, :], x_v[i]).then_inc(ld_x[i], 16)
            sp.dma_start(causal[:, :], c_causal).then_inc(ld_moe, 16)
            sp.dma_start(rank[:, :], c_rank).then_inc(ld_moe, 16)
            sp.dma_start(gate_bb[:, :], gate_b.partition_broadcast(P)).then_inc(ld_moe, 16)
            for w, dst, shared in ((We1, w1, ws1), (We3, w3, ws3)):
                sp.dma_start(dst[:, 0:PAIRS, :].rearrange("d p (e i) -> d (p e) i", e=2),
                             w.rearrange("e d i -> d e i")).then_inc(ld_moe, 16)
                sp.dma_start(dst[:, PAIRS, :], shared).then_inc(ld_moe, 16)
            sp.dma_start(w2[:, 0:PAIRS, :], We2.rearrange("(p e) i d -> (e i) p d", e=2)).then_inc(ld_moe, 16)
            sp.dma_start(w2[:, PAIRS, :], ws2).then_inc(ld_moe, 16)
            for v, dst, shared in ((be1, b1, bs1), (be3, b3, bs3)):
                sp.dma_start(dst[:, 0:PAIRS], v.rearrange("(p e) i -> (e i) p", e=2),
                             allow_slow_non_contiguous=True).then_inc(ld_moe, 16)
                sp.dma_start(dst[:, PAIRS:UNITS], shared.rearrange("(i o) -> i o", o=1)).then_inc(ld_moe, 16)
            sp.dma_start(b2[0:E, :], be2).then_inc(ld_moe, 16)
            sp.dma_start(b2[E:E + 1, :], bs2.rearrange("(o d) -> o d", o=1)).then_inc(ld_moe, 16)

            def stack(x, which):
                b, c = x // 2, x % 2
                terms = (TERMS_Q, TERMS_K)[which]
                if which == 0 and x >= 2:
                    sp.wait_ge(scores_full, banks_before(NG * (x - 1)))
                for part in range(3):
                    if part == 0:
                        sp.wait_ge(part_hi, 2 * x + which + 1)
                    elif part == 1:
                        sp.wait_ge(parts_lo, 2 * x + which + 1)
                    for t in [t for t, p in enumerate(terms) if p == part]:
                        for par in range(2):
                            rows = slice(64 * par + 8 * t, 64 * par + 8 * t + 8)
                            sp.dma_start(k_st[rows, b, :, c * CH:(c + 1) * CH] if which else q_st[rows, x % 2, :, :],
                                         parts[64 * par:64 * par + 64, which, part, :]).then_inc(stacked[x], 16)

            for kind, arg in SCHEDULE:
                if kind == "qT":
                    stack(arg, 0)
                elif kind == "kT":
                    sp.wait_ge(k_set, arg // 2 + 1)
                    stack(arg, 1)
                elif kind == "mfin":
                    x, g = arg // NG, arg % NG
                    b, c = x // 2, x % 2
                    sp.wait_ge(work_read_dve, frees("dve", FILL["mfin", arg] + 1))
                    for par in range(2):
                        sp.dma_start(q_st[64 * par + KR:64 * par + KM, x % 2, 2 * g:2 * g + 2, :],
                                     maxT[4 * par:4 * par + 4, arg % 2, :]).then_inc(maxrow_in[arg % 2], 16)
                elif kind == "cT":
                    x = arg
                    sp.wait_ge(work_read_dve, frees("dve", FILL["cT", x] + 1))
                    sp.dma_start(combine_dram[x], combT[0:E, :]).then_inc(st_combine, 16)
                    sp.wait_ge(st_combine, 16 * (x + 1))
                    if x >= 1:
                        sp.wait_ge(weighted, 2 * PAIRS * x)
                    for e in range(2):
                        src = combine_dram[x].rearrange("(m e) q -> e m q", e=2)[e]
                        sp.dma_start(comb_b[64 * e:64 * e + 64, :, :], src.partition_broadcast(64)).then_inc(ld_combine, 16)
                elif kind == "final":
                    sp.wait_ge(out_ready, arg + 1)
                    sp.dma_start(out_v[arg], fin[:, :, :]).then_inc(stored, 16)
            sp.wait_ge(stored, 16 * NX)

        @block.tensor
        def _(pe):
            def fill(kind, arg):
                n = FILL[kind, arg]
                before = [m for m in range(n) if FILL_BANK[m] == FILL_BANK[n]]
                if before:
                    last = before[-1]
                    reader = LAST_READER[FILLS[last][0]]
                    read = {"act": work_read_act, "dve": work_read_dve, "experts": h_ready}[reader]
                    pe.wait_ge(read, frees(reader, last + 1))
                if n >= LATE and FILL_BANK[n] != WORK_BANK:
                    pe.wait_ge(max_free, len(MAXES))
                return bank(FILL_BANK[n])

            def weights():
                w = fill("weights", 0)
                pe.wait_ge(ld_attn, 16 * N_ATTN)
                pe.matmul(w[:, 0:P], w_raw[:, 0, :], center[:, :], start=True, stop=True)
                pe.matmul(w[:, P:2 * P], w_raw[:, 1, :], center[:, :], start=True, stop=True)
                pe.transpose(w[:, 2 * P:3 * P], w_raw[:, 2, :], ident[:, :]).then_inc(work_full, 1)

            def weights2():
                w = fill("weights2", 0)
                pe.transpose(w[:, 0:P], w_raw[:, 3, :], ident[:, :])
                pe.transpose(w[:, P:P + E], gate_raw[:, :], ident[0:E, 0:E]).then_inc(work_full, 1)

            def turn(kind, arg, src, tiles=TPC):
                w = fill(kind, arg)
                for t in range(tiles):
                    last = pe.transpose(w[:, t * P:(t + 1) * P], src(t), ident[:, :])
                last.then_inc(work_full, 1)

            def qkv(tile):
                x, t = tile // TPC, tile % TPC
                w = fill("qkv", tile)
                if tile == 0:
                    pe.wait_ge(work_read_act, 1)
                pe.wait_ge(work_read_act, frees("act", FILL["xT", x] + 1))
                pe.matmul(w[:, 0:3 * P], xnT[:, t * P:(t + 1) * P], w_qkv[:, :], start=True, stop=True
                          ).then_inc(work_full, 1)

            def maxima(a, u):
                x, g = a // NG, a % NG
                b, c = x // 2, x % 2
                n = MAXES[a, u]
                what, qt, heads, keys = max_units_of(c)[u]
                w = bank(MAX_BANK + n % MAX_RING)
                if n == 0:
                    pe.wait_ge(consts, 1)
                    pe.wait_ge(work_read_act, frees("act", EARLY))
                    pe.wait_ge(work_read_dve, frees("dve", EARLY))
                if n >= MAX_RING:
                    pe.wait_ge(max_free, n - MAX_RING + 1)
                if u == 0:
                    for y in range(2 * b, x + 1):
                        pe.wait_ge(stacked[y], 16 * 24)
                if what == "diag":
                    nh = len(heads)
                    v = w[:, 0:nh * keys].rearrange("p (h k) -> p h k", h=nh)[:, :, keys - P:keys]
                    pe.matmul(v, ident_bf[:, :], causal_bf[:, :].unsqueeze(1).broadcast_to([P, nh, P]),
                              start=True, stop=False, skip_group_check=True)
                k0 = c * CH if what == "diag" else 0
                for i, j in enumerate(heads):
                    par, m = j % 2, 2 * g + j // 2
                    q0 = qt * P
                    last = pe.matmul(w[:, i * keys:(i + 1) * keys], q_st[64 * par:64 * par + KR, x % 2, m, q0:q0 + P],
                                     k_st[64 * par:64 * par + KR, b, m, k0:k0 + keys],
                                     start=(what == "full"), stop=True, skip_group_check=True)
                last.then_inc(max_full, 1)

            def max_turn(a):
                w = fill("mfin", a)
                pe.wait_ge(neg_ready, a + 1)
                wb = w.bitcast(BF16)
                for qt in range(TPC):
                    src = negmax[:, 2 * qt:2 * qt + 2, :, :].rearrange("p a r m -> p (a r m)")
                    last = pe.transpose(wb[0:8, qt * P:(qt + 1) * P], src, ident_bf[:, :])
                last.then_inc(work_full, 1)

            def scores(s, i):
                a, k = BURSTS[s]
                x, g = a // NG, a % NG
                b, c = x // 2, x % 2
                n = BANKS[s, i]
                w = bank(ST_BANK + n % ST_RING)
                if n >= ST_RING:
                    pe.wait_ge(exp_done, n - ST_RING + 1)
                if k == 0 and i == 0:
                    pe.wait_ge(maxrow_in[a % 2], 32 * (a // 2 + 1))
                for j, kt, col, cols, q0 in bursts_of(c)[k][i][0]:
                    par, m = j % 2, 2 * g + j // 2
                    last = pe.matmul(w[:, col:col + cols], k_st[64 * par:64 * par + KM, b, m, kt * P:(kt + 1) * P],
                                     q_st[64 * par:64 * par + KM, x % 2, m, q0:q0 + cols],
                                     start=True, stop=True)
                last.then_inc(scores_full, 1)

            def pv(s):
                a, k = BURSTS[s]
                x, g = a // NG, a % NG
                b, c = x // 2, x % 2
                acc = bank(ACC_BANK)
                pe.wait_ge(exp_done, BANKS_TO[s])
                if MASKS_TO[s]:
                    pe.wait_ge(masked, MASKS_TO[s])
                if k == 0 and a >= 1:
                    pe.wait_ge(o_ready, a)
                todo = [(r, n) for i, (regions, _) in enumerate(bursts_of(c)[k]) for n in [BANKS[s, i]] for r in regions]
                todo.sort(key=lambda rn: (rn[0][1], rn[0][0]))
                for (j, kt, col, cols, q0), n in todo:
                    last = pe.matmul(acc[32 * j:32 * j + VC, q0:q0 + cols], v_ones[:, b, kt, G * g + j, :],
                                     probs[:, n % P_RING, col:col + cols], start=(kt == 0),
                                     stop=(k == len(bursts_of(c)) - 1), tile_position=(0, 32 * j),
                                     skip_group_check=True)
                last.then_inc(pv_done, 1)

            def project(x):
                w = fill("proj", x)
                pe.wait_ge(work_read_act, frees("act", FILL["onT", x] + 1))
                for t in range(TPC):
                    last = pe.matmul(w[:, t * P:(t + 1) * P], o_normT[:, t * P:(t + 1) * P], w_o[:, 0:P],
                                     start=True, stop=True)
                last.then_inc(work_full, 1)

            def router(x):
                w = fill("gate", x)
                pe.wait_ge(work_read_act, frees("act", FILL["x2T", x] + 1))
                for t in range(TPC):
                    last = pe.matmul(w[:, t * E:(t + 1) * E], x2T[:, x % 2, t * P:(t + 1) * P], w_o[:, P:P + E],
                                     start=True, stop=True)
                last.then_inc(work_full, 1)

            def combine_turn(x):
                w = fill("cT", x)
                pe.wait_ge(comb_ready, x + 1)
                for t in range(TPC):
                    last = pe.transpose(w[0:E, t * P:(t + 1) * P], lg[:, 11, t, :], ident[:, :])
                last.then_inc(work_full, 1)

            def moe(x, n):
                if n == 0 and x == 0:
                    pe.wait_ge(ld_moe, 16 * N_MOE)
                if n < 2 * UNITS:
                    half, u = n // UNITS, n % UNITS
                    w = fill("moe", (x, n))
                    rhs = x2T[:, x % 2, half * HALF:(half + 1) * HALF]
                    pe.matmul(w[:, 0:HALF], w1[:, u, :], rhs, start=True, stop=True)
                    pe.matmul(w[:, HALF:CH], w3[:, u, :], rhs, start=True, stop=True).then_inc(work_full, 1)
                y = bank(Y_BANK)
                if n == 0:
                    if x >= 1:
                        pe.wait_ge(out_ready, x)
                    pe.wait_ge(work_read_dve, frees("dve", FILL["cT", x] + 1))
                    for t in range(TPC):
                        pe.matmul(y[:, t * P:(t + 1) * P], combT[:, t * P:(t + 1) * P], b2[:, :],
                                  start=(t == 0), stop=False, skip_group_check=True)
                else:
                    half, u = (n - 1) // UNITS, (n - 1) % UNITS
                    at = 2 * UNITS * x + n - 1
                    if u < PAIRS:
                        pe.wait_ge(weighted, PAIRS * (2 * x + half) + u + 1)
                    else:
                        pe.wait_ge(h_ready, at + 1)
                    src = mhc if u < PAIRS else mh
                    for t in range(2):
                        tok = 2 * half + t
                        last = pe.matmul(y[:, tok * P:(tok + 1) * P], src[:, at % 2, t * P:(t + 1) * P], w2[:, u, :],
                                         start=False, stop=(u == UNITS - 1), skip_group_check=True)
                    last.then_inc(y_done, 1)

            for kind, arg in SCHEDULE:
                if kind == "weights":
                    weights()
                elif kind == "weights2":
                    weights2()
                elif kind == "xT":
                    pe.wait_ge(xn_ready, norm_at("norm", arg) + 1)
                    turn(kind, arg, lambda t: xn[:, t, :])
                elif kind == "qkv":
                    qkv(arg)
                elif kind in ("qT", "kT"):
                    which = int(kind == "kT")
                    pe.wait_ge(roped_ready, arg + 1)
                    turn(kind, arg, lambda t, w=which: roped[:, w, t, :, :, :].rearrange("p r d m -> p (r d m)"))
                elif kind == "max":
                    maxima(*arg)
                elif kind == "mfin":
                    max_turn(arg)
                elif kind == "scores":
                    scores(*arg)
                elif kind == "pv":
                    pv(arg)
                elif kind == "oT":
                    pe.wait_ge(o_ready, arg + 1)
                    turn(kind, arg, lambda t: o_raw[:, t * P:(t + 1) * P])
                elif kind == "onT":
                    pe.wait_ge(work_read_dve, frees("dve", turned("oT", NG * arg + NG - 1)))
                    turn(kind, arg, lambda t: o_norm[:, t, :])
                elif kind == "proj":
                    project(arg)
                elif kind == "x2T":
                    pe.wait_ge(xn_ready, norm_at("norm2", arg) + 1)
                    turn(kind, arg, lambda t: xn[:, t, :])
                elif kind == "gate":
                    router(arg)
                elif kind == "cT":
                    combine_turn(arg)
                elif kind == "moe":
                    moe(*arg)

        @block.scalar
        def _(act):
            act.dma_start(xs[:, 0, :, :], x_v[0]).then_inc(ld_x[0], 16)

            def exp(s, i):
                n = BANKS[s, i]
                act.wait_ge(scores_full, n + 1)
                if n >= P_RING:
                    old = next(q for q in range(len(BURSTS)) if BANKS_TO[q] > n - P_RING)
                    act.wait_ge(pv_done, old + 1)
                act.activation(probs[:, n % P_RING, :], bank(ST_BANK + n % ST_RING), ACT.Exp,
                               scale=SCALE).then_inc(exp_done, 1)

            def keep(kind, arg, dst, cols):
                act.wait_ge(work_full, turned(kind, arg))
                act.copy(dst, wbank(kind, arg)[:, 0:cols]).then_inc(work_read_act, 1)

            def qkv(tile):
                x, t = tile // TPC, tile % TPC
                b, kt = x // 2, tile % KT
                act.wait_ge(work_full, turned("qkv", tile))
                w = wbank("qkv", tile)
                if x >= 1:
                    act.wait_ge(roped_ready, x)
                both = w[:, 0:2 * P].rearrange("p (w h d) -> p w h d", w=2, h=H)
                act.copy(qk[:, :, t, :, :], both)
                act.activation(sq[:, :, t, :, :], both, ACT.Square)
                if t == 0:
                    act.wait_ge(v_set, b + 1)
                act.copy(v_ones[:, b, kt, :, 0:HD], w[:, 2 * P:3 * P].rearrange("p (h d) -> p h d", h=H)
                         ).then_inc(work_read_act, 1)

            def leading_part(kind, x):
                which = int(kind == "kT")
                act.wait_ge(work_full, turned(kind, x))
                if x >= 1:
                    act.wait_ge(stacked[x - 1], 16 * 24)
                act.copy(parts[:, which, 0, :], wbank(kind, x)).then_inc(part_hi, 1)

            def moe(x, n):
                at, u = 2 * UNITS * x + n, n % UNITS
                act.wait_ge(work_full, turned("moe", (x, n)))
                if x == 0 and n == 0:
                    act.wait_ge(consts, 2)
                if at >= 2:
                    act.wait_ge(h_used, at - 1)
                act.activation(mu[:, at % 2, :], wbank("moe", (x, n))[:, 0:HALF], ACT.Identity,
                               bias=b1h[:, u:u + 1], scale=0.5).then_inc(act_u, 1)
                act.wait_ge(act_u, at + 1)
                act.activation(mt[:, at % 2, :], mu[:, at % 2, :], ACT.Tanh).then_inc(act_t, 1)

            for kind, arg in SCHEDULE:
                if kind == "weights":
                    keep(kind, arg, w_qkv[:, :], 3 * P)
                elif kind == "weights2":
                    keep(kind, arg, w_o[:, :], P + E)
                elif kind == "xT":
                    keep(kind, arg, xnT[:, :], CH)
                elif kind == "qkv":
                    qkv(arg)
                elif kind in ("qT", "kT"):
                    leading_part(kind, arg)
                elif kind == "scores":
                    exp(*arg)
                elif kind == "onT":
                    keep(kind, arg, o_normT[:, :], CH)
                elif kind == "x2T":
                    keep(kind, arg, x2T[:, arg % 2, :], CH)
                elif kind == "gate":
                    act.wait_ge(work_read_dve, frees("dve", turned("gate", arg)))
                    act.activation(lg[:, 1, :, :], lg[:, 0, :, :], ACT.Exp).then_inc(gate_exp, 1)
                elif kind == "moe" and arg[1] < 2 * UNITS:
                    moe(*arg)

        @block.gpsimd
        def _(pool):
            links = [0]

            def link(ins):
                links[0] += 1
                ins.then_inc(pool_chain, 1)
                pool.wait_ge(pool_chain, links[0])

            link(pool.memset(expo[:, :], -0.5))
            for b in range(B):
                pool.memset(k_st[:, b, :, :].rearrange("p m q -> p (m q)").bitcast(F32), TWO_ONES).then_inc(k_set, 1)
                pool.memset(v_ones[:, b, :, :, :], 1.0).then_inc(v_set, 1)

            def rstd_of(kind, x):
                pool.wait_ge(var_ready, norm_at(kind, x) + 1)
                link(pool.tensor_scalar(veps[:, :], mv[:, :, 1], EPS, None, ALU.add))
                pool.tensor_tensor(rstd[:, :], veps[:, :], expo[:, 0:TPC], ALU.pow).then_inc(rstd_ready, 1)

            def rope_direct(x):
                c = x % 2
                if x == 0:
                    pool.wait_ge(tables_ready, 1)
                pool.wait_ge(rope_a, x + 1)
                for w in range(2):
                    for tab, src, op in ((g_cos, sq, ALU.mult), (g_add, qk, ALU.add)):
                        t = tab[:, w, 4 * c:4 * c + 4, :].unsqueeze(2).broadcast_to([P, TPC, H, HD])
                        last = pool.tensor_tensor(qk[:, w, :, :, :], src[:, w, :, :, :], t, op)
                        if op == ALU.mult:
                            link(last)
                last.then_inc(rope_direct_ready, 1)

            def lower_parts(kind, x):
                which = int(kind == "kT")
                pool.wait_ge(work_read_dve, frees("dve", turned(kind, x)))
                if x >= 1:
                    pool.wait_ge(stacked[x - 1], 16 * 24)
                link(pool.tensor_copy(parts[:, which, 1, :], resid[:, which, :]))
                pool.tensor_tensor(parts[:, which, 2, :], resid[:, which, :], parts[:, which, 1, :],
                                   ALU.subtract).then_inc(parts_lo, 1)

            for kind, arg in SCHEDULE:
                if kind in ("norm", "norm2"):
                    rstd_of(kind, arg)
                    if kind == "norm":
                        if arg == 0:
                            pool.wait_ge(ld_rope, 16 * N_ROPE)
                        pool.wait_ge(xn_ready, norm_at(kind, arg) + 1)
                        pool.tensor_tensor(xs[:, arg, :, :], xs[:, arg, :, :],
                                           bo_b[:, :].unsqueeze(1).broadcast_to([P, TPC, P]), ALU.add
                                           ).then_inc(xbo_ready, 1)
                elif kind == "headnorm":
                    pool.wait_ge(hsum_ready, arg + 1)
                    link(pool.tensor_scalar(hvar[:, :], ssum[:, :], 1.0 / HD, EPS, ALU.mult, ALU.add))
                    pool.tensor_tensor(hrstd[:, :], hvar[:, :], expo[:, :], ALU.pow).then_inc(hrstd_ready, 1)
                elif kind == "rope":
                    rope_direct(arg)
                elif kind in ("qT", "kT"):
                    lower_parts(kind, arg)
                elif kind == "scores":
                    s, i = arg
                    a, k = BURSTS[s]
                    blocks = bursts_of(a // NG % 2)[k][i][1]
                    if blocks is not None:
                        n = BANKS[arg]
                        pool.wait_ge(exp_done, n + 1)
                        v = probs[:, n % P_RING, :].rearrange("p (r q) -> p r q", q=P)[:, blocks, :]
                        pool.affine_select(out=v, in_=v, compare_op=ALU.is_ge, fill=0.0, base=0,
                                           pattern=[[0, v.shape[1]], [1, P]], channel_multiplier=-1
                                           ).then_inc(masked, 1)
                elif kind == "moe" and arg[1] < 2 * UNITS and arg[1] % UNITS < PAIRS:
                    x, n = arg
                    at, half, u = 2 * UNITS * x + n, n // UNITS, n % UNITS
                    if n == 0:
                        pool.wait_ge(ld_combine, 32 * (x + 1))
                    pool.wait_ge(h_ready, at + 1)
                    if at >= 2:
                        pool.wait_ge(y_done, at - 1)
                    pool.tensor_tensor(mhc[:, at % 2, :], mh[:, at % 2, :],
                                       comb_b[:, u, half * HALF:(half + 1) * HALF], ALU.mult).then_inc(weighted, 1)

        @block.vector
        def _(dve):
            links = [0]

            def link(ins):
                links[0] += 1
                ins.then_inc(chain, 1)
                dve.wait_ge(chain, links[0])

            def norm(kind, x):
                n = norm_at(kind, x)
                if kind == "norm":
                    dve.wait_ge(ld_x[x], 16)
                else:
                    dve.wait_ge(work_read_dve, frees("dve", turned("proj", x)))
                for t in range(TPC):
                    last = dve.bn_stats(stats[:, t, :], xs[:, x, t, :])
                link(last)
                for t in range(TPC):
                    last = dve.bn_aggr(mv[:, t, :], stats[:, t, :])
                last.then_inc(var_ready, 1)
                dve.wait_ge(var_ready, n + 1)
                dve.wait_ge(rstd_ready, n + 1)
                if n >= 1:
                    k, y = [q for q in SCHEDULE if q[0] in ("norm", "norm2")][n - 1]
                    dve.wait_ge(work_full, turned("xT" if k == "norm" else "x2T", y))
                for t in range(TPC):
                    last = dve.tensor_scalar(xn[:, t, :], xs[:, x, t, :], mv[:, t, 0:1], rstd[:, t:t + 1],
                                             ALU.subtract, ALU.mult)
                last.then_inc(xn_ready, 1)

            def head_sums(x):
                dve.wait_ge(work_read_act, frees("act", turned("qkv", TPC * x + TPC - 1)))
                dve.tensor_reduce(ssum[:, :], sq[:, :, :, :, :].rearrange("p w t h d -> p (w t h) d"), AX.X,
                                  ALU.add).then_inc(hsum_ready, 1)

            def rope_rotated(x):
                c = x % 2
                dve.wait_ge(hrstd_ready, x + 1)
                dve.tensor_tensor(sq[:, :, :, :, :].rearrange("p w t h d -> p (w t h) d"),
                                  qk[:, :, :, :, :].rearrange("p w t h d -> p (w t h) d"),
                                  hrstd[:, :].unsqueeze(2).broadcast_to([P, 2 * TPC * H, HD]),
                                  ALU.mult).then_inc(rope_a, 1)
                dve.wait_ge(rope_a, x + 1)
                for w in range(2):
                    for j in range(2):
                        t = g_sin[:, w, 4 * c:4 * c + 4, 4 * j:4 * j + 4].unsqueeze(2).broadcast_to([P, TPC, H, 4])
                        last = dve.tensor_tensor(rot[:, w, :, :, 4 * j:4 * j + 4], sq[:, w, :, :, 1 - j::2], t, ALU.mult)
                link(last)
                dve.wait_ge(rope_direct_ready, x + 1)
                if x >= 1:
                    dve.wait_ge(work_full, turned("kT", x - 1))
                for w in range(2):
                    for par in range(2):
                        last = dve.tensor_tensor(roped[:, w, :, par, :, :].rearrange("p t d m -> p t m d"),
                                                 qk[:, w, :, par::2, :], rot[:, w, :, par::2, :], ALU.add)
                last.then_inc(roped_ready, 1)

            def remainder(kind, x):
                which = int(kind == "kT")
                dve.wait_ge(part_hi, 2 * x + which + 1)
                if x >= 1:
                    dve.wait_ge(parts_lo, 2 * x)
                dve.tensor_tensor(resid[:, which, :], wbank(kind, x), parts[:, which, 0, :],
                                  ALU.subtract).then_inc(work_read_dve, 1)

            def maxima(a, u):
                n = MAXES[a, u]
                what, qt, heads, keys = max_units_of(a // NG % 2)[u]
                j, nh = heads[0], len(heads)
                w = bank(MAX_BANK + n % MAX_RING)[:, 0:nh * keys].rearrange("p (h k) -> p h k", h=nh)
                dst = mx_full if what == "full" else mx_diag
                dve.wait_ge(max_full, n + 1)
                dve.tensor_reduce(dst[:, qt, j % 2, j // 2:j // 2 + nh], w, AX.X, ALU.max).then_inc(max_free, 1)

            def max_finish(a):
                dve.wait_ge(max_free, MAXES[a, len(max_units_of(a // NG % 2)) - 1] + 1)
                m = mx_diag[:, :, :, :].rearrange("p t r m -> p (t r) m")
                if a // NG % 2:
                    link(dve.tensor_tensor(mx[:, :, :], m, mx_full[:, :, :, :].rearrange("p t r m -> p (t r) m"), ALU.max))
                    m = mx[:, :, :]
                if a >= 1:
                    dve.wait_ge(work_full, turned("mfin", a - 1))
                link(dve.tensor_scalar(negmax[:, :, 0, :], m, -1.0, None, ALU.mult))
                dve.scalar_tensor_tensor(out=negmax[:, :, 1, :], in0=m, scalar=-1.0, in1=negmax[:, :, 0, :],
                                         op0=ALU.mult, op1=ALU.subtract).then_inc(neg_ready, 1)
                dve.wait_ge(work_full, turned("mfin", a))
                if a >= 2:
                    dve.wait_ge(maxrow_in[a % 2], 32 * (a // 2))
                dve.tensor_copy(maxT[:, a % 2, :], wbank("mfin", a).bitcast(BF16)[0:8, 0:CH]).then_inc(work_read_dve, 1)

            def leave(a):
                if a >= 1:
                    dve.wait_ge(work_full, turned("oT", a - 1))
                dve.tensor_copy(o_raw[:, :], bank(ACC_BANK)).then_inc(o_ready, 1)

            def normalise(a):
                g = a % NG
                dve.wait_ge(work_full, turned("oT", a))
                w = wbank("oT", a).rearrange("p (t j v) -> p t j v", t=TPC, j=G)
                link(dve.reciprocal(rden[:, :, :, :], w[:, :, :, HD:HD + 1]))
                dst = o_norm[:, :, G * HD * g:G * HD * (g + 1)].rearrange("p t (j d) -> p t j d", j=G)
                last = dve.tensor_tensor(dst, w[:, :, :, 0:HD], rden[:, :, :, :].broadcast_to([P, TPC, G, HD]), ALU.mult)
                last.then_inc(work_read_dve, 1)

            def two_largest(v, ranks, width, t, small, out_mask):
                def wide(m):
                    return m.unsqueeze(2).broadcast_to([P, TPC, width])
                link(dve.tensor_reduce(small[0], v, AX.X, ALU.max))
                for turn in range(2):
                    link(dve.tensor_tensor(t[0], v if turn == 0 else t[2], wide(small[0]), ALU.is_equal))
                    link(dve.tensor_tensor(t[0], t[0], ranks, ALU.mult))
                    link(dve.tensor_reduce(small[1], t[0], AX.X, ALU.max))
                    link(dve.tensor_tensor(t[1 + 2 * turn], t[0], wide(small[1]), ALU.is_equal))
                    if turn == 0:
                        link(dve.scalar_tensor_tensor(out=t[2], in0=t[1], scalar=3 * MASKED, in1=v,
                                                      op0=ALU.mult, op1=ALU.add))
                        link(dve.tensor_reduce(small[0], t[2], AX.X, ALU.max))
                link(dve.tensor_tensor(out_mask, t[1], t[3], ALU.add))

            def router(x):
                dve.wait_ge(work_full, turned("gate", x))
                w = wbank("gate", x)[:, 0:TPC * E].rearrange("p (t e) -> p t e", t=TPC)

                def wide(m, width=E):
                    return m.unsqueeze(2).broadcast_to([P, m.shape[1], width])

                def grouped(m):
                    return m.rearrange("p t (g e) -> p (t g) e", g=NGRP)

                link(dve.tensor_reduce(red[:, 0, :], w, AX.X, ALU.max))
                dve.tensor_tensor(lg[:, 0, :, :], w, wide(red[:, 0, :]), ALU.subtract).then_inc(work_read_dve, 1)
                dve.wait_ge(gate_exp, x + 1)
                link(dve.tensor_reduce(red[:, 1, :], lg[:, 1, :, :], AX.X, ALU.add))
                link(dve.reciprocal(red[:, 2, :], red[:, 1, :]))
                link(dve.tensor_tensor(lg[:, 2, :, :], lg[:, 1, :, :], wide(red[:, 2, :]), ALU.mult))
                link(dve.tensor_tensor(lg[:, 3, :, :], lg[:, 2, :, :],
                                       gate_bb[:, :].unsqueeze(1).broadcast_to([P, TPC, E]), ALU.add))
                s = grouped(lg[:, 3, :, :])
                dve.tensor_tensor(pair_sums[:, :, 0:3], s[:, :, 0:3], s[:, :, 1:4], ALU.add)
                dve.tensor_tensor(pair_sums[:, :, 3:5], s[:, :, 0:2], s[:, :, 2:4], ALU.add)
                link(dve.tensor_tensor(pair_sums[:, :, 5:6], s[:, :, 0:1], s[:, :, 3:4], ALU.add))
                link(dve.tensor_reduce(gsm[:, 0, :, :].rearrange("p t g -> p (t g)"), pair_sums[:, :, :], AX.X, ALU.max))
                two_largest(gsm[:, 0, :, :], rank[:, E - NGRP:E].unsqueeze(1).broadcast_to([P, TPC, NGRP]), NGRP,
                            [gsm[:, 1 + i, :, :] for i in range(4)], (red[:, 3, :], red[:, 4, :]), gsm[:, 5, :, :])
                link(dve.tensor_scalar(gsm[:, 6, :, :], gsm[:, 5, :, :], -MASKED, MASKED, ALU.mult, ALU.add))
                per = [gsm[:, i, :, :].rearrange("p t g -> p (t g)") for i in (5, 6)]
                link(dve.tensor_tensor(grouped(lg[:, 4, :, :]), s, wide(per[0], E // NGRP), ALU.mult))
                link(dve.tensor_tensor(grouped(lg[:, 5, :, :]), grouped(lg[:, 4, :, :]), wide(per[1], E // NGRP), ALU.add))
                two_largest(lg[:, 5, :, :], rank[:, :].unsqueeze(1).broadcast_to([P, TPC, E]), E,
                            [lg[:, 6 + i, :, :] for i in range(4)], (red[:, 5, :], red[:, 6, :]), lg[:, 10, :, :])
                dve.tensor_tensor(lg[:, 11, :, :], lg[:, 2, :, :], lg[:, 10, :, :], ALU.mult).then_inc(comb_ready, 1)

            def combine_rows(x):
                dve.wait_ge(work_full, turned("cT", x))
                if x >= 1:
                    dve.wait_ge(st_combine, 16 * x)
                    dve.wait_ge(y_done, 2 * UNITS * (x - 1) + 1)
                dve.tensor_copy(combT[0:E, :], wbank("cT", x)[0:E, :]).then_inc(work_read_dve, 1)

            def moe(x, n):
                at, u = 2 * UNITS * x + n, n % UNITS
                dve.wait_ge(act_t, at + 1)
                if at >= 1:
                    dve.wait_ge(h_ready, at)
                dve.scalar_tensor_tensor(out=mw[:, :], in0=mt[:, at % 2, :], scalar=1.0, in1=mu[:, at % 2, :],
                                         op0=ALU.add, op1=ALU.mult).then_inc(h_used, 1)
                dve.wait_ge(h_used, at + 1)
                if at >= 2:
                    dve.wait_ge(y_done, at - 1)
                dve.scalar_tensor_tensor(out=mh[:, at % 2, :], in0=wbank("moe", (x, n))[:, HALF:CH],
                                         scalar=b3[:, u:u + 1], in1=mw[:, :], op0=ALU.add, op1=ALU.mult
                                         ).then_inc(h_ready, 1)

            link(dve.memset(combT[:, :], 1.0))
            dve.memset(bank(ACC_BANK), 0.0)
            norm("norm", 0)
            dve.wait_ge(ld_rope, 16 * N_ROPE)
            dve.tensor_copy(gb_rot[:, :, 0:4], gb[:, :, 1::2])
            link(dve.tensor_copy(gb_rot[:, :, 4:8], gb[:, :, 0::2]))
            for w in range(2):
                def affine(m, i, w=w):
                    return m[:, 2 * w + i, :].unsqueeze(1).broadcast_to([P, KT, HD])
                dve.tensor_tensor(g_cos[:, w, :, :], rope[:, :, 0, :], affine(gb, 0), ALU.mult)
                dve.tensor_tensor(g_sin[:, w, :, :], rope[:, :, 1, :], affine(gb_rot, 0), ALU.mult)
                dve.tensor_tensor(g_add[:, w, :, :], rope[:, :, 0, :], affine(gb, 1), ALU.mult)
                link(dve.tensor_tensor(g_tmp[:, w, :, :], rope[:, :, 1, :], affine(gb_rot, 1), ALU.mult))
            dve.tensor_tensor(g_add[:, :, :, :], g_add[:, :, :, :], g_tmp[:, :, :, :], ALU.add).then_inc(tables_ready, 1)

            for kind, arg in SCHEDULE:
                if kind == "norm" and arg >= 1 or kind == "norm2":
                    norm(kind, arg)
                elif kind == "headnorm":
                    head_sums(arg)
                elif kind == "rope":
                    rope_rotated(arg)
                elif kind in ("qT", "kT"):
                    remainder(kind, arg)
                    if kind == "kT" and arg == 0:
                        dve.wait_ge(ld_moe, 16 * N_MOE)
                        dve.wait_ge(ld_attn, 16 * N_ATTN)
                        dve.tensor_copy(ident_bf[:, :], ident[:, :])
                        dve.tensor_copy(causal_bf[:, :], causal[:, :]).then_inc(consts, 1)
                        dve.tensor_scalar(b1h[:, :], b1[:, :], 0.5, None, ALU.mult).then_inc(consts, 1)
                elif kind == "max":
                    maxima(*arg)
                elif kind == "mfin":
                    max_finish(arg)
                elif kind == "pv":
                    a, k = BURSTS[arg]
                    if k == len(bursts_of(a // NG % 2)) - 1:
                        dve.wait_ge(pv_done, arg + 1)
                        leave(a)
                elif kind == "oT":
                    normalise(arg)
                elif kind == "proj":
                    dve.wait_ge(work_full, turned("proj", arg))
                    dve.wait_ge(xbo_ready, arg + 1)
                    dve.tensor_tensor(xs[:, arg, :, :], wbank("proj", arg).rearrange("p (t d) -> p t d", t=TPC),
                                      xs[:, arg, :, :], ALU.add).then_inc(work_read_dve, 1)
                elif kind == "gate":
                    router(arg)
                elif kind == "cT":
                    combine_rows(arg)
                elif kind == "moe" and arg[1] < 2 * UNITS:
                    moe(*arg)
                elif kind == "final":
                    dve.wait_ge(y_done, 2 * UNITS * (arg + 1))
                    if arg >= 1:
                        dve.wait_ge(stored, 16 * arg)
                    dve.tensor_tensor(fin[:, :, :], bank(Y_BANK).rearrange("p (t d) -> p t d", t=TPC),
                                      xs[:, arg, :, :], ALU.add).then_inc(out_ready, 1)
    return nc


_INS = ["x", "Wq", "Wk", "Wv", "q_gamma", "q_beta", "k_gamma", "k_beta", "Wo", "bo"]
_FFN = ["gate_w", "gate_b", "We1", "be1", "We2", "be2", "We3", "be3", "ws1", "bs1", "ws2", "bs2", "ws3", "bs3"]


def shape_constants():
    f = np.float32
    ident = np.eye(P, dtype=f)
    center = (ident - np.kron(np.eye(H, dtype=f), np.full((HD, HD), 1.0 / HD, f))).astype(f)
    q, k = np.arange(P)[:, None], np.arange(P)[None, :]
    causal = np.where(k > q, f(MASKED), f(0)).astype(f)
    di = np.arange(0, HD, 2, dtype=f) / f(HD)
    theta = np.arange(S, dtype=f)[:, None] * np.exp(-di * f(np.log(10000.0)))
    cos, sin = (np.repeat(fn(theta.astype(f)), 2, axis=1).astype(f) for fn in (np.cos, np.sin))
    sin[:, 0:HD // 2] *= -1
    rope = np.stack([cos, sin], axis=1).reshape(KT, P, 2, HD).transpose(1, 0, 2, 3)
    rank = np.broadcast_to(np.arange(E, 0, -1, dtype=f), (P, E))
    return {"c_ident": ident, "c_center": center, "c_causal": causal, "c_rope": rope, "c_rank": rank}


def kernel(**inputs):
    import concourse.bacc as _bacc
    from concourse.bass_utils import run_bass_kernel_spmd as _run

    nc = _bacc.Bacc("TRN2", target_bir_lowering=False, num_devices=1)
    given = {n: inputs["L0_attn_" + n] for n in _INS} | {n: inputs["L0_ffn_" + n] for n in _FFN} | shape_constants()
    arrays, args = {}, []
    for name, a in given.items():
        a = np.ascontiguousarray(a)
        arrays["in_" + name] = a
        args.append(nc.dram_tensor("in_" + name, a.shape, mybir.dt.from_np(a.dtype), kind="ExternalInput").ap())
    out = nc.dram_tensor("out_0", (B, S, D), F32, kind="ExternalOutput").ap()
    layer_kernel(nc, *args, out)
    r = _run(nc, [arrays], core_ids=[0])
    return r.results[0]["out_0"]
```

```python
from contextlib import ExitStack

import numpy as np
import concourse.bass as bass
from concourse import mybir

F32 = mybir.dt.float32
BF16 = mybir.dt.bfloat16
I32 = mybir.dt.int32
ALU = mybir.AluOpType
ACT = mybir.ActivationFunctionType
AX = mybir.AxisListType

P = 128
B, S, D = 2, 1024, 128
H, HD = 16, 8
E, INTER, NGRP = 16, 64, 4
CH = 512
NX = B * S // CH
TPC = CH // P
KT = S // P
G = 4
NG = H // G
NA = NX * NG
PAIRS = E // 2
UNITS = PAIRS + 1
HALF = CH // 2
SCALE = float(HD) ** -0.5
EPS = 1e-5
TERMS_Q = [0, 0, 1, 1, 0, 2]
TERMS_K = [0, 1, 0, 1, 2, 0]
KR = 8 * len(TERMS_Q)
KM = P - 2
VC = 16
MASKED = -1e30
RSQRT_SEED = 0x5F3759DF
TWO_ONES = float(np.array([0x3F803F80], np.uint32).view(np.float32)[0])
ST_RING, P_RING, MAX_RING, MOE_RING = 3, 10, 2, 3
ST_BANK, ACC_BANK, MAX_BANK, WORK_BANK, Y_BANK = 0, 3, 4, 6, 7


def bursts_of(c):
    out = [[([(j, kt, 0, CH, 0)], None) for j in range(G)] for kt in range(4 * c)]
    out.append([([(j, 4 * c, 0, CH, 0)], slice(0, 1)) for j in range(G)])
    out.append([([(j, 4 * c + 1, 0, 384, 128), (j, 4 * c + 3, 384, 128, 384)], slice(0, 4, 3)) for j in range(G)])
    out.append([([(j, 4 * c + 2, 0, 256, 256), (j + 2, 4 * c + 2, 256, 256, 256)], slice(0, 4, 2)) for j in range(2)])
    return out


def max_units_of(c):
    units = [("full", qt, [j], 512) for qt in range(TPC) for j in range(G)] if c else []
    for qt in range(TPC):
        keys = P * (qt + 1)
        for j in range(2):
            units += [("diag", qt, [j, j + 2], keys)] if qt < 2 else [("diag", qt, [j], keys), ("diag", qt, [j + 2], keys)]
    return units


def unit(n):
    return n // UNITS, (n % UNITS + PAIRS) % UNITS


FILLS_READ = {"weights": ("weights_read", "act"), "weights2": ("weights2_read", "act"), "xT": ("xT_read", "act"),
              "qkv": ("qkv_read", "act"), "qT": ("qT_rest", "dve"), "kT": ("kT_rest", "dve"),
              "mturn": ("mcopy", "dve"), "oT": ("oT_read", "dve"), "onT": ("onT_read", "act"),
              "proj": ("proj_read", "dve"), "x2T": ("x2T_read", "act"), "gate": ("gate_read", "dve"),
              "cT": ("cT_read", "dve"), "moe": ("moe_dve", "experts")}
READS = {stage: reader for stage, reader in FILLS_READ.values()}
LENGTHS = {
    "pe": {"weights": .8, "weights2": .3, "xT": .44, "qkv": .65, "qT": .44, "kT": .44, "scores": .22, "mturn": .25,
           "pv": .92, "oT": .44, "onT": .44, "proj": .87, "x2T": .44, "gate": .87, "cT": .44, "moe": .86,
           "moe_y": .45, "max": .25},
    "act": {"weights_read": .4, "weights2_read": .2, "xT_read": .5, "qkv_read": .72, "qT_lead": .5, "kT_lead": .5,
            "exp": .49, "leave": .5, "onT_read": .5, "x2T_read": .5, "gate_exp": .2, "moe_act": .85},
    "dve": {"norm": 4.8, "tables": 1.85, "headsum": 1.15, "headrstd": 3.65, "headscale": 1.15, "rope": 1.35,
            "rope_sum": 1.35, "qT_rest": 1.1, "kT_rest": 1.1, "maxred": .6, "mneg": .5, "mcopy": .35, "oT_read": .5,
            "proj_read": .6, "norm2": 4.8, "gate_read": .4, "route1": 1.65, "route2": 3.2, "route3": 3.3,
            "cT_read": .6, "moe_dve": .88, "final": .6},
    "pool": {"ones": 5.2, "zero": 6.9, "xbo": 1.3, "rope_pool": 4.9, "qT_low": 1.2, "kT_low": 1.2, "mask": .35, "weight": .75},
    "sp": {"stack": 3.6, "mrow": 1.2, "cstore": .6, "cload": 1.2, "store": .6},
}
ENGINE = {kind: engine for engine, kinds in LENGTHS.items() for kind in kinds}
DMA_DONE = {"stack": 5.8, "mrow": 3.2, "cstore": 2.3, "cload": 6.0, "store": 3.0}
PE_TICK, PE_BUSY = 3.413, 1.3
SIGNAL = 0.12


def plan():
    bursts = [(a, k) for a in range(NA) for k in range(len(bursts_of(a // NG % 2)))]
    first = {a: min(s for s, (q, _) in enumerate(bursts) if q == a) for a in range(NA)}
    first[NA] = len(bursts)
    banks = [(s, i) for s, (a, k) in enumerate(bursts) for i in range(len(bursts_of(a // NG % 2)[k]))]
    units = [(a, u) for a in range(NA) for u in range(len(max_units_of(a // NG % 2)))]
    burst_end = {s: max(n for n, (q, _) in enumerate(banks) if q == s) for s in range(len(bursts))}
    needs, urgency = {}, {}

    def add(kind, arg, key, *after):
        assert (kind, arg) not in needs
        needs[kind, arg] = [q for q in after if q is not None]
        urgency[kind, arg] = key

    def old(kind, arg, ok):
        return (kind, arg) if ok else None

    add("weights", 0, -30)
    add("weights_read", 0, -30, ("weights", 0))
    add("weights2", 0, -29, ("weights", 0))
    add("weights2_read", 0, -29, ("weights2", 0))
    add("tables", 0, -20, ("norm", 0))
    add("ones", 0, -40)
    add("zero", 0, -39)
    add("zero", 1, -12, ("xbo", 0), ("ones", 0))
    add("ones", 1, -11, ("kT_low", 0))

    def window(lo, hi, what):
        return {stage: lo + n * (hi - lo) / len(what) for n, stage in enumerate(what)}

    for x in range(NX):
        lo, hi = PREP_WINDOWS[x](first)
        tiles = range(TPC * x, TPC * x + TPC)
        names = (["norm", "xbo", "xT", "xT_read"] + [n for t in tiles for n in (("qkv", t), ("qkv_read", t))] +
                 ["headsum", "headrstd", "headscale", "rope_pool", "rope", "rope_sum", "qT", "qT_lead", "qT_rest",
                  "qT_low", "kT", "kT_lead", "kT_rest", "kT_low"])
        at = window(lo, hi, names)
        p = x - 1
        add("norm", x, at["norm"], old("xT", p, x))
        add("xbo", x, at["xbo"] + 3, ("norm", x))
        add("xT", x, at["xT"], ("norm", x), ("weights", 0))
        add("xT_read", x, at["xT_read"], ("xT", x), old("qkv", TPC * x - 1, x))
        for t in tiles:
            add("qkv", t, at["qkv", t], ("xT_read", x), ("weights_read", 0), old("qkv", t - 1, t))
            add("qkv_read", t, at["qkv_read", t], ("qkv", t), ("ones", x // 2), old("rope_sum", p, x))
        add("headsum", x, at["headsum"], *[("qkv_read", t) for t in tiles])
        add("headrstd", x, at["headrstd"], ("headsum", x))
        add("headscale", x, at["headscale"], ("headrstd", x))
        add("rope_pool", x, at["rope_pool"], ("headscale", x), ("tables", 0))
        add("rope", x, at["rope"], ("headscale", x), ("tables", 0), old("kT", p, x))
        add("rope_sum", x, at["rope_sum"], ("rope", x), ("rope_pool", x))
        for w, k in enumerate("qk"):
            add(k + "T", x, at[k + "T"], ("rope_sum", x), old("qT", x, w))
            add(k + "T_lead", x, at[k + "T_lead"], (k + "T", x), old("stack", (p, 1, 1), x), old("qT_lead", x, w))
            add(k + "T_rest", x, at[k + "T_rest"], (k + "T_lead", x))
            add(k + "T_low", x, at[k + "T_low"], (k + "T_rest", x), old("qT_low", x, w))
            add("stack", (x, w, 0), at[k + "T_lead"], (k + "T_lead", x),
                ("scores", banks[burst_end[first[NG * (x - 1)] - 1]]) if x >= 2 and w == 0 else None,
                old("ones", x // 2, w), old("zero", x, w == 0 and x < 2),
                old("stack", (x, 0, 1), w))
            add("stack", (x, w, 1), at[k + "T_low"], (k + "T_low", x), ("stack", (x, w, 0)))
    for n, (a, u) in enumerate(units):
        x = a // NG
        lo, hi = (first[a - AHEAD], first[a - AHEAD + 1]) if a >= AHEAD else (-8 + 4 * a, -5 + 4 * a)
        count = len(max_units_of(x % 2))
        key = lo + u * (hi - lo) / count
        add("max", (a, u), key, *[("stack", (y, w, 1)) for y in range(x - x % 2, x + 1) for w in range(2)],
            old("maxred", units[n - MAX_RING] if n >= MAX_RING else 0, n >= MAX_RING),
            old("max", units[n - 1], n))
        add("maxred", (a, u), key, ("max", (a, u)), old("maxred", units[n - 1], n), old("mneg", a - 1, u == 0 and a))
        if u == count - 1:
            add("mneg", a, hi, ("maxred", (a, u)), old("mturn", a - 1, a))
            add("mturn", a, hi, ("mneg", a))
            add("mcopy", a, hi, ("mturn", a), old("mrow", a - 2, a >= 2))
            add("mrow", a, hi, ("mcopy", a))
    for n, (s, i) in enumerate(banks):
        a, k = bursts[s]
        prev = banks[n - 1] if n else None
        reuse = next((q for q in range(len(bursts)) if burst_end[q] >= n - P_RING), None) if n >= P_RING else None
        add("scores", (s, i), s + i / 4, old("scores", prev, n), old("exp", banks[n - ST_RING] if n >= ST_RING else 0, n >= ST_RING),
            old("mrow", a, k == 0 and i == 0))
        add("exp", (s, i), s + i / 4, ("scores", (s, i)), old("exp", prev, n), old("pv", reuse, reuse is not None))
        if bursts_of(a // NG % 2)[k][i][1] is not None:
            add("mask", (s, i), s + i / 4, ("exp", (s, i)))
        if n == burst_end[s]:
            add("pv", s, s + 0.6, old("pv", s - 1, s), ("exp", (s, i)),
                *[("mask", (s, j)) for j in range(i + 1) if bursts_of(a // NG % 2)[k][j][1] is not None],
                old("leave", a - 1, k == 0 and a))
            if s + 1 == first[a + 1]:
                add("leave", a, s + 1, ("pv", s), old("oT", a - 1, a))
                add("oT", a, s + 1, ("leave", a))
                add("oT_read", a, s + 1, ("oT", a), old("onT", a // NG - 1, a >= NG and a % NG == 0), old("oT_read", a - 1, a))
    for x in range(NX):
        lo, hi = EPILOGUE_WINDOWS[x](first)
        names = ("onT onT_read proj proj_read norm2 x2T x2T_read gate gate_read gate_exp route1 route2 route3 "
                 "cT cT_read cstore cload").split()
        at = window(lo, hi, names)
        chain = {"onT": [("oT_read", NG * x + NG - 1)], "proj": [("weights2_read", 0)], "proj_read": [("xbo", x)],
                 "norm2": [old("x2T", x - 1, x)], "x2T_read": [old("moe", (x - 2, 2 * UNITS - 1), x >= 2)],
                 "cT_read": [old("cstore", x - 1, x), old("moe_y", (x - 1, 2 * UNITS - 1), x)],
                 "cload": [old("weight", (x - 1, 2 * UNITS - 1), x)]}
        for n, name in enumerate(names):
            add(name, x, at[name], old(names[n - 1], x, n), *chain.get(name, []))
        lo, hi = MOE_WINDOWS[x](first)
        for n in range(2 * UNITS):
            key = lo + n * (hi - lo) / (2 * UNITS)
            g = 2 * UNITS * x + n

            def back(kind, d):
                return old(kind, divmod(g - d, 2 * UNITS), g >= d)
            add("moe", (x, n), key, ("x2T_read", x), back("moe", 1))
            add("moe_act", (x, n), key, ("moe", (x, n)), back("moe_dve", MOE_RING), back("moe_act", 1))
            add("moe_dve", (x, n), key, ("moe_act", (x, n)), back("moe_y", MOE_RING), back("moe_dve", 1))
            shared = unit(n)[1] == PAIRS
            if not shared:
                add("weight", (x, n), key, ("moe_dve", (x, n)), ("cload", x), back("moe_y", MOE_RING))
            add("moe_y", (x, n), key, ("moe_dve" if shared else "weight", (x, n)), back("moe_y", 1),
                old("final", x - 1, n == 0 and x), old("cT_read", x, n == 2 * UNITS - 1))
        add("final", x, hi, ("moe_y", (x, 2 * UNITS - 1)))
        add("store", x, hi, ("final", x))

    def length(kind, arg):
        if kind in ("max", "maxred"):
            what, _, heads, keys = max_units_of(arg[0] // NG % 2)[arg[1]]
            cols = len(heads) * keys
            return (cols + P * len(heads) * (what == "diag")) / 2400 if kind == "max" else cols / 960 + .07
        if kind == "moe_y" and arg[1] == 2 * UNITS - 1:
            return 1.3
        if kind == "pv":
            return .92 if bursts[arg][1] < len(bursts_of(bursts[arg][0] // NG % 2)) - 1 else .5
        return LENGTHS[ENGINE[kind]][kind]

    users = {stage: [] for stage in needs}
    missing, ready_at = {}, {}
    for stage, after in needs.items():
        missing[stage] = len(after)
        for q in after:
            users[q].append(stage)
    ready = {engine: [] for engine in LENGTHS}
    for stage, m in missing.items():
        ready_at[stage] = {"weights": 8.0, "norm": 5.0}.get(stage[0], 0.0)
        if not m:
            ready[ENGINE[stage[0]]].append(stage)
    free_at = {engine: 0.0 for engine in LENGTHS}
    order, fills, bank_free = [], {}, {bank: 0.0 for bank in (WORK_BANK, MAX_BANK, MAX_BANK + 1)}
    unread, pending = {}, {"act": [], "dve": [], "experts": []}
    maxes = 0

    def bank_for(kind, now):
        if kind in FILLS_READ:
            allowed = [WORK_BANK] + ([MAX_BANK, MAX_BANK + 1] if maxes in (0, len(units)) and (
                not maxes or ("maxred", units[-1]) in done) else [])
            return next((q for q in allowed if q not in unread and bank_free[q] <= now), None)
        if kind == "max" and maxes < MAX_RING and MAX_BANK + maxes in unread:
            return None
        return 0

    done, now, work = {}, 0.0, {}
    while len(order) < len(needs):
        progress = False
        for engine in LENGTHS:
            if free_at[engine] > now:
                continue
            able = []
            for stage in ready[engine]:
                kind, arg = stage
                if ready_at[stage] > now:
                    continue
                if kind in READS and pending[READS[kind]][0] != stage:
                    continue
                if engine == "pe" and bank_for(kind, now) is None:
                    continue
                able.append((urgency[stage], stage[0], str(stage[1]), stage))
            if not able:
                continue
            stage = min(able)[3]
            kind, arg = stage
            ready[engine].remove(stage)
            took = length(kind, arg)
            if engine == "pe":
                tick = int(now / PE_TICK)
                work[tick] = work.get(tick, 0.0) + took * (2 if kind == "pv" else 1)
                if work.get(tick - 1, 0.0) < PE_BUSY:
                    took = min(2 * took, max(took, (tick + 1) * PE_TICK - now + took / 2))
            end = now + took + .03
            free_at[engine] = end
            order.append(stage)
            progress = True
            if kind == "max":
                maxes += 1
            if kind in FILLS_READ:
                fills[stage] = bank_for(kind, now)
                unread[fills[stage]] = (FILLS_READ[kind][0], arg)
                pending[FILLS_READ[kind][1]].append((FILLS_READ[kind][0], arg))
            if kind in READS:
                pending[READS[kind]].pop(0)
                for q in [q for q, reader in unread.items() if reader == stage]:
                    del unread[q]
                    bank_free[q] = end + SIGNAL
            done[stage] = end
            for q in users[stage]:
                missing[q] -= 1
                same = ENGINE[q[0]] == engine and kind not in DMA_DONE
                ready_at[q] = max(ready_at[q], (now + DMA_DONE[kind] if kind in DMA_DONE else end + SIGNAL * (not same)))
                if not missing[q]:
                    ready[ENGINE[q[0]]].append(q)
        if not progress:
            later = [t for t in list(free_at.values()) + list(bank_free.values()) +
                     [ready_at[q] for lst in ready.values() for q in lst] if t > now]
            now = min(later)
    return bursts, banks, units, order, fills, done


AHEAD = 2
PREP_WINDOWS = [lambda f: (-25, -12), lambda f: (-12, f[1]), lambda f: (f[2], f[5]), lambda f: (f[6], f[9])]
EPILOGUE_WINDOWS = [lambda f: (f[4] + 1, f[5]), lambda f: (f[8] + 1, f[10]), lambda f: (f[12] + 1, f[13]),
                    lambda f: (f[16], f[16] + 4)]
MOE_WINDOWS = [lambda f: (f[5], f[8]), lambda f: (f[10], f[13]), lambda f: (f[13], f[16]),
               lambda f: (f[16] + 3, f[16] + 12)]

BURSTS, BANK_LIST, UNIT_LIST, SCHEDULE, FILL_BANKS, PLANNED = plan()
BANKS = {key: n for n, key in enumerate(BANK_LIST)}
BANKS_TO = {s: max(n for (q, _), n in BANKS.items() if q == s) + 1 for s in range(len(BURSTS))}
MASKED_BANKS = [q for q in BANK_LIST if bursts_of(BURSTS[q[0]][0] // NG % 2)[BURSTS[q[0]][1]][q[1]][1] is not None]
MASKS_TO = {s: sum(q <= s for q, _ in MASKED_BANKS) for s in range(len(BURSTS))}
MAXES = {key: n for n, key in enumerate(UNIT_LIST)}
FILLS = list(FILL_BANKS)
FILL = {key: n for n, key in enumerate(FILLS)}
FILL_BANK = list(FILL_BANKS.values())
POS = {stage: n for n, stage in enumerate(SCHEDULE)}


def banks_before(a):
    return sum(BURSTS[s][0] < a for s, _ in BANKS)


def frees(reader, upto):
    return sum(FILLS_READ[FILLS[n][0]][1] == reader for n in range(upto))


def layer_kernel(nc, x, Wq, Wk, Wv, q_gamma, q_beta, k_gamma, k_beta, Wo, bo, gate_w, gate_b,
                 We1, be1, We2, be2, We3, be3, ws1, bs1, ws2, bs2, ws3, bs3,
                 c_ident, c_center, c_causal, c_rope, c_rank, out):
    x_v = x.rearrange("b (h t p) d -> (b h) p t d", p=P, t=TPC)
    out_v = out.rearrange("b (h t p) d -> (b h) p t d", p=P, t=TPC)
    combine_dram = nc.dram_tensor("combine_scratch", [NX, E, CH], F32, kind="Internal").ap()

    with ExitStack() as ctx:
        def sb(name, shape, dt=F32):
            return ctx.enter_context(nc.sbuf_tensor(name, shape, dt))

        def sem(name):
            return ctx.enter_context(nc.semaphore(name))

        psum = ctx.enter_context(nc.psum_tensor("psum", [P, 8, 512], F32))

        ident = sb("ident", [P, P])
        ident_bf = sb("ident_bf", [P, P], BF16)
        center = sb("center", [P, P])
        causal = sb("causal", [P, P])
        causal_bf = sb("causal_bf", [P, P], BF16)
        rope = sb("rope", [P, KT, 2, HD])
        rank = sb("rank", [P, E])
        w_raw = sb("w_raw", [P, 4, P])
        gate_raw = sb("gate_raw", [E, P])
        w_qkv = sb("w_qkv", [P, 3 * P])
        w_o = sb("w_o", [P, P + E])
        gb = sb("gb", [P, 4, HD])
        gb_rot = sb("gb_rot", [P, 4, HD])
        g_cos = sb("g_cos", [P, 2, KT, HD])
        g_sin = sb("g_sin", [P, 2, KT, HD])
        g_add = sb("g_add", [P, 2, KT, HD])
        g_tmp = sb("g_tmp", [P, 2, KT, HD])
        bo_b = sb("bo_b", [P, P])
        gate_bb = sb("gate_bb", [P, E])
        w1 = sb("w1", [P, UNITS, P])
        w3 = sb("w3", [P, UNITS, P])
        w2 = sb("w2", [P, UNITS, P])
        b1 = sb("b1", [P, UNITS])
        b1h = sb("b1h", [P, UNITS])
        b3 = sb("b3", [P, UNITS])
        b2 = sb("b2", [E + 1, P])
        xs = sb("xs", [P, NX, TPC, P])
        xn = sb("xn", [P, TPC, P])
        xn2 = sb("xn2", [P, TPC, P])
        xnT = sb("xnT", [P, CH])
        stats = sb("stats", [P, TPC, 6])
        mv = sb("mv", [P, TPC, 2])
        seed = sb("seed", [P, P], I32)
        nr = sb("nr", [P, 2, P])
        rstd = sb("rstd", [P, TPC])
        qk = sb("qk", [P, 2, TPC, H, HD])
        sq = sb("sq", [P, 2, TPC, H, HD])
        ssum = sb("ssum", [P, 2 * TPC * H])
        hvar = sb("hvar", [P, 2 * TPC * H])
        hrstd = sb("hrstd", [P, 2 * TPC * H])
        roped = sb("roped", [P, 2, TPC, 2, HD, H // 2])
        parts = sb("parts", [P, 2, 3, CH], BF16)
        resid = sb("resid", [P, 2, CH])
        q_st = sb("q_st", [P, 2, H // 2, 2, CH], BF16)
        k_st = sb("k_st", [P, B, H // 2, S], BF16)
        v_ones = sb("v_ones", [P, B, KT, H, VC])
        mx_full = sb("mx_full", [P, TPC, 2, 2])
        mx_diag = sb("mx_diag", [P, TPC, 2, 2])
        mx = sb("mx", [P, TPC * 2, 2])
        negmax = sb("negmax", [P, TPC * 2, 2, 2], BF16)
        maxT = sb("maxT", [8, 2, CH], BF16)
        probs = sb("probs", [P, P_RING, CH])
        o_raw = sb("o_raw", [P, CH])
        rden = sb("rden", [P, TPC, G, 1])
        o_norm = sb("o_norm", [P, TPC, P])
        o_normT = sb("o_normT", [P, CH])
        x2T = sb("x2T", [P, 2, CH])
        lg = sb("lg", [P, 12, TPC, E])
        gsm = sb("gsm", [P, 16, TPC, NGRP])
        pair_sums = sb("pair_sums", [P, TPC * NGRP, 6])
        red = sb("red", [P, 8, TPC])
        combT = sb("combT", [E + 1, CH])
        comb_b = sb("comb_b", [P, PAIRS, CH])
        mu = sb("mu", [P, MOE_RING, HALF])
        mt = sb("mt", [P, MOE_RING, HALF])
        mh = sb("mh", [P, MOE_RING, HALF])

        ld_x = [sem(f"ld_x{i}") for i in range(NX)]
        ld_attn = sem("ld_attn")
        ld_rope = sem("ld_rope")
        ld_moe = sem("ld_moe")
        ld_combine = sem("ld_combine")
        st_combine = sem("st_combine")
        stacked = [sem(f"stacked{i}") for i in range(NX)]
        maxrow_in = [sem(f"maxrow_in{i}") for i in range(2)]
        stored = sem("stored")
        scores_full = sem("scores_full")
        max_full = sem("max_full")
        work_full = sem("work_full")
        pv_done = sem("pv_done")
        y_done = sem("y_done")
        exp_done = sem("exp_done")
        o_ready = sem("o_ready")
        work_read_act = sem("work_read_act")
        part_hi = sem("part_hi")
        part_mid = sem("part_mid")
        gate_exp = sem("gate_exp")
        act_u = sem("act_u")
        act_t = sem("act_t")
        v_set = sem("v_set")
        k_set = sem("k_set")
        q_set = sem("q_set")
        masked = sem("masked")
        pool_chain = sem("pool_chain")
        rope_direct_ready = sem("rope_direct_ready")
        parts_lo = sem("parts_lo")
        xbo_ready = sem("xbo_ready")
        weighted = sem("weighted")
        consts = sem("consts")
        tables_ready = sem("tables_ready")
        rope_a = sem("rope_a")
        chain = sem("chain")
        max_free = sem("max_free")
        work_read_dve = sem("work_read_dve")
        xn_ready = sem("xn_ready")
        xn2_ready = sem("xn2_ready")
        roped_ready = sem("roped_ready")
        neg_ready = sem("neg_ready")
        comb_ready = sem("comb_ready")
        h_ready = sem("h_ready")
        h_used = sem("h_used")
        out_ready = sem("out_ready")

        N_ATTN, N_ROPE, N_MOE = 7, 6, 15

        def bank(n):
            return psum[:, n, :]

        def wbank(kind, arg):
            return bank(FILL_BANK[FILL[kind, arg]])

        def turned(kind, arg):
            return FILL[kind, arg] + 1

        block = ctx.enter_context(nc.Block())

        @block.sync
        def _(sp):
            for w, dst in ((Wq, 0), (Wk, 1), (Wv, 2), (Wo, 3)):
                sp.dma_start(w_raw[:, dst, :], w).then_inc(ld_attn, 16)
            sp.dma_start(ident[:, :], c_ident).then_inc(ld_attn, 16)
            sp.dma_start(center[:, :], c_center).then_inc(ld_attn, 16)
            sp.dma_start(gate_raw[:, :], gate_w).then_inc(ld_attn, 16)
            sp.dma_start(rope[:, :, :, :], c_rope).then_inc(ld_rope, 16)
            for n, v in enumerate((q_gamma, q_beta, k_gamma, k_beta)):
                sp.dma_start(gb[:, n, :], v.partition_broadcast(P)).then_inc(ld_rope, 16)
            sp.dma_start(bo_b[:, :], bo.partition_broadcast(P)).then_inc(ld_rope, 16)
            for i in range(1, NX):
                sp.dma_start(xs[:, i, :, :], x_v[i]).then_inc(ld_x[i], 16)
            sp.dma_start(causal[:, :], c_causal).then_inc(ld_moe, 16)
            sp.dma_start(rank[:, :], c_rank).then_inc(ld_moe, 16)
            sp.dma_start(gate_bb[:, :], gate_b.partition_broadcast(P)).then_inc(ld_moe, 16)
            for w, dst, shared in ((We1, w1, ws1), (We3, w3, ws3)):
                sp.dma_start(dst[:, 0:PAIRS, :].rearrange("d p (e i) -> d (p e) i", e=2),
                             w.rearrange("e d i -> d e i")).then_inc(ld_moe, 16)
                sp.dma_start(dst[:, PAIRS, :], shared).then_inc(ld_moe, 16)
            sp.dma_start(w2[:, 0:PAIRS, :], We2.rearrange("(p e) i d -> (e i) p d", e=2)).then_inc(ld_moe, 16)
            sp.dma_start(w2[:, PAIRS, :], ws2).then_inc(ld_moe, 16)
            for v, dst, shared in ((be1, b1, bs1), (be3, b3, bs3)):
                sp.dma_start(dst[:, 0:PAIRS], v.rearrange("(p e) i -> (e i) p", e=2),
                             allow_slow_non_contiguous=True).then_inc(ld_moe, 16)
                sp.dma_start(dst[:, PAIRS:UNITS], shared.rearrange("(i o) -> i o", o=1)).then_inc(ld_moe, 16)
            sp.dma_start(b2[0:E, :], be2).then_inc(ld_moe, 16)
            sp.dma_start(b2[E:E + 1, :], bs2.rearrange("(o d) -> o d", o=1)).then_inc(ld_moe, 16)

            def stack(x, which, lower):
                b, c = x // 2, x % 2
                terms = (TERMS_Q, TERMS_K)[which]
                if which == 0 and x >= 2 and not lower:
                    sp.wait_ge(scores_full, banks_before(NG * (x - 1)))
                if which == 0 and x < 2 and not lower:
                    sp.wait_ge(q_set, x + 1)
                if which == 1 and not lower:
                    sp.wait_ge(k_set, x // 2 + 1)
                for part in (1, 2) if lower else (0,):
                    if part == 0:
                        sp.wait_ge(part_hi, 2 * x + which + 1)
                    elif part == 1:
                        sp.wait_ge(parts_lo, 2 * x + which + 1)
                    for t in [t for t, p in enumerate(terms) if p == part]:
                        for par in range(2):
                            rows = slice(64 * par + 8 * t, 64 * par + 8 * t + 8)
                            sp.dma_start(k_st[rows, b, :, c * CH:(c + 1) * CH] if which else q_st[rows, x % 2, :, par, :],
                                         parts[64 * par:64 * par + 64, which, part, :]).then_inc(stacked[x], 16)

            for kind, arg in SCHEDULE:
                if kind == "stack":
                    stack(*arg)
                elif kind == "mrow":
                    x, g = arg // NG, arg % NG
                    b, c = x // 2, x % 2
                    sp.wait_ge(work_read_dve, frees("dve", FILL["mturn", arg] + 1))
                    for par in range(2):
                        sp.dma_start(q_st[KM:P, x % 2, 2 * g:2 * g + 2, par, :],
                                     maxT[4 * par:4 * par + 4, arg % 2, :]).then_inc(maxrow_in[arg % 2], 16)
                elif kind == "cstore":
                    x = arg
                    sp.wait_ge(work_read_dve, frees("dve", FILL["cT", x] + 1))
                    sp.dma_start(combine_dram[x], combT[0:E, :]).then_inc(st_combine, 16)
                elif kind == "cload":
                    x = arg
                    sp.wait_ge(st_combine, 16 * (x + 1))
                    if x >= 1:
                        sp.wait_ge(weighted, 2 * PAIRS * x)
                    for e in range(2):
                        src = combine_dram[x].rearrange("(m e) q -> e m q", e=2)[e]
                        sp.dma_start(comb_b[64 * e:64 * e + 64, :, :], src.partition_broadcast(64)).then_inc(ld_combine, 16)
                elif kind == "store":
                    sp.wait_ge(out_ready, arg + 1)
                    sp.dma_start(out_v[arg], xs[:, arg, :, :]).then_inc(stored, 16)
            sp.wait_ge(stored, 16 * NX)

        @block.tensor
        def _(pe):
            def wait_read(engine, n):
                reader = FILLS_READ[FILLS[n][0]][1]
                read = {"act": work_read_act, "dve": work_read_dve, "experts": h_ready}[reader]
                engine.wait_ge(read, frees(reader, n + 1))

            def fill(kind, arg):
                n = FILL[kind, arg]
                before = [m for m in range(n) if FILL_BANK[m] == FILL_BANK[n]]
                if before:
                    last = before[-1]
                    wait_read(pe, last)
                if FILL_BANK[n] != WORK_BANK and POS[kind, arg] > POS["max", UNIT_LIST[-1]]:
                    pe.wait_ge(max_free, len(MAXES))
                return bank(FILL_BANK[n])

            def weights():
                w = fill("weights", 0)
                pe.wait_ge(ld_attn, 16 * N_ATTN)
                pe.matmul(w[:, 0:P], w_raw[:, 0, :], center[:, :], start=True, stop=True)
                pe.matmul(w[:, P:2 * P], w_raw[:, 1, :], center[:, :], start=True, stop=True)
                pe.transpose(w[:, 2 * P:3 * P], w_raw[:, 2, :], ident[:, :]).then_inc(work_full, 1)

            def weights2():
                w = fill("weights2", 0)
                pe.transpose(w[:, 0:P], w_raw[:, 3, :], ident[:, :])
                pe.transpose(w[:, P:P + E], gate_raw[:, :], ident[0:E, 0:E]).then_inc(work_full, 1)

            def turn(kind, arg, src, tiles=TPC):
                w = fill(kind, arg)
                for t in range(tiles):
                    last = pe.transpose(w[:, t * P:(t + 1) * P], src(t), ident[:, :])
                last.then_inc(work_full, 1)

            def qkv(tile):
                x, t = tile // TPC, tile % TPC
                w = fill("qkv", tile)
                if tile == 0:
                    pe.wait_ge(work_read_act, 1)
                pe.wait_ge(work_read_act, frees("act", FILL["xT", x] + 1))
                pe.matmul(w[:, 0:3 * P], xnT[:, t * P:(t + 1) * P], w_qkv[:, :], start=True, stop=True
                          ).then_inc(work_full, 1)

            def maxima(a, u):
                x, g = a // NG, a % NG
                b, c = x // 2, x % 2
                n = MAXES[a, u]
                what, qt, heads, keys = max_units_of(c)[u]
                w = bank(MAX_BANK + n % MAX_RING)
                if n == 0:
                    pe.wait_ge(consts, 1)
                if n < MAX_RING:
                    here = [m for m in range(len(FILLS)) if FILL_BANK[m] == MAX_BANK + n and POS[FILLS[m]] < POS["max", (a, u)]]
                    if here:
                        wait_read(pe, here[-1])
                if n >= MAX_RING:
                    pe.wait_ge(max_free, n - MAX_RING + 1)
                if u == 0:
                    for y in range(2 * b, x + 1):
                        pe.wait_ge(stacked[y], 16 * 24)
                if what == "diag":
                    nh = len(heads)
                    v = w[:, 0:nh * keys].rearrange("p (h k) -> p h k", h=nh)[:, :, keys - P:keys]
                    pe.matmul(v, ident_bf[:, :], causal_bf[:, :].unsqueeze(1).broadcast_to([P, nh, P]),
                              start=True, stop=False, skip_group_check=True)
                k0 = c * CH if what == "diag" else 0
                for i, j in enumerate(heads):
                    par, m = j % 2, 2 * g + j // 2
                    q0 = qt * P
                    last = pe.matmul(w[:, i * keys:(i + 1) * keys], q_st[0:KM, x % 2, m, par, q0:q0 + P],
                                     k_st[0:KM, b, m, k0:k0 + keys],
                                     start=(what == "full"), stop=True, skip_group_check=True)
                last.then_inc(max_full, 1)

            def max_turn(a):
                w = fill("mturn", a)
                pe.wait_ge(neg_ready, a + 1)
                wb = w.bitcast(BF16)
                for qt in range(TPC):
                    src = negmax[:, 2 * qt:2 * qt + 2, :, :].rearrange("p a r m -> p (a r m)")
                    last = pe.transpose(wb[0:8, qt * P:(qt + 1) * P], src, ident_bf[:, :])
                last.then_inc(work_full, 1)

            def scores(s, i):
                a, k = BURSTS[s]
                x, g = a // NG, a % NG
                b, c = x // 2, x % 2
                n = BANKS[s, i]
                w = bank(ST_BANK + n % ST_RING)
                if n >= ST_RING:
                    pe.wait_ge(exp_done, n - ST_RING + 1)
                if k == 0 and i == 0:
                    pe.wait_ge(maxrow_in[a % 2], 32 * (a // 2 + 1))
                for j, kt, col, cols, q0 in bursts_of(c)[k][i][0]:
                    par, m = j % 2, 2 * g + j // 2
                    last = pe.matmul(w[:, col:col + cols], k_st[:, b, m, kt * P:(kt + 1) * P],
                                     q_st[:, x % 2, m, par, q0:q0 + cols],
                                     start=True, stop=True)
                last.then_inc(scores_full, 1)

            def pv(s):
                a, k = BURSTS[s]
                x, g = a // NG, a % NG
                b, c = x // 2, x % 2
                acc = bank(ACC_BANK)
                pe.wait_ge(exp_done, BANKS_TO[s])
                if MASKS_TO[s]:
                    pe.wait_ge(masked, MASKS_TO[s])
                if k == 0 and a >= 1:
                    pe.wait_ge(o_ready, a)
                todo = [(r, n) for i, (regions, _) in enumerate(bursts_of(c)[k]) for n in [BANKS[s, i]] for r in regions]
                todo.sort(key=lambda rn: (rn[0][1], rn[0][0]))
                for (j, kt, col, cols, q0), n in todo:
                    last = pe.matmul(acc[32 * j:32 * j + VC, q0:q0 + cols], v_ones[:, b, kt, G * g + j, :],
                                     probs[:, n % P_RING, col:col + cols], start=(kt == 0),
                                     stop=(k == len(bursts_of(c)) - 1), tile_position=(0, 32 * j),
                                     skip_group_check=True)
                last.then_inc(pv_done, 1)

            def project(x):
                w = fill("proj", x)
                pe.wait_ge(work_read_act, frees("act", FILL["onT", x] + 1))
                for t in range(TPC):
                    last = pe.matmul(w[:, t * P:(t + 1) * P], o_normT[:, t * P:(t + 1) * P], w_o[:, 0:P],
                                     start=True, stop=True)
                last.then_inc(work_full, 1)

            def router(x):
                w = fill("gate", x)
                pe.wait_ge(work_read_act, frees("act", FILL["x2T", x] + 1))
                for t in range(TPC):
                    last = pe.matmul(w[:, t * E:(t + 1) * E], x2T[:, x % 2, t * P:(t + 1) * P], w_o[:, P:P + E],
                                     start=True, stop=True)
                last.then_inc(work_full, 1)

            def combine_turn(x):
                w = fill("cT", x)
                pe.wait_ge(comb_ready, x + 1)
                for t in range(TPC):
                    last = pe.transpose(w[0:E, t * P:(t + 1) * P], lg[:, 11, t, :], ident[:, :])
                last.then_inc(work_full, 1)

            def moe(x, n):
                if n == 0 and x == 0:
                    pe.wait_ge(ld_moe, 16 * N_MOE)
                half, u = unit(n)
                w = fill("moe", (x, n))
                rhs = x2T[:, x % 2, half * HALF:(half + 1) * HALF]
                pe.matmul(w[:, 0:HALF], w1[:, u, :], rhs, start=True, stop=True)
                pe.matmul(w[:, HALF:CH], w3[:, u, :], rhs, start=True, stop=True).then_inc(work_full, 1)

            def moe_sum(x, n):
                half, u = unit(n)
                y = bank(Y_BANK)
                at = 2 * UNITS * x + n
                if n == 0 and x >= 1:
                    pe.wait_ge(out_ready, x)
                if u < PAIRS:
                    pe.wait_ge(weighted, PAIRS * (2 * x + half) + u + 1)
                else:
                    pe.wait_ge(h_ready, at + 1)
                for t in range(2):
                    tok = 2 * half + t
                    last = pe.matmul(y[:, tok * P:(tok + 1) * P], mh[:, at % MOE_RING, t * P:(t + 1) * P], w2[:, u, :],
                                     start=(n == 0 and t == 0), stop=False, skip_group_check=True)
                if n == 2 * UNITS - 1:
                    pe.wait_ge(work_read_dve, frees("dve", FILL["cT", x] + 1))
                    for t in range(TPC):
                        last = pe.matmul(y[:, t * P:(t + 1) * P], combT[:, t * P:(t + 1) * P], b2[:, :],
                                         start=False, stop=True, skip_group_check=True)
                last.then_inc(y_done, 1)

            for kind, arg in SCHEDULE:
                if kind == "weights":
                    weights()
                elif kind == "weights2":
                    weights2()
                elif kind == "xT":
                    pe.wait_ge(xn_ready, arg + 1)
                    turn(kind, arg, lambda t: xn[:, t, :])
                elif kind == "qkv":
                    qkv(arg)
                elif kind in ("qT", "kT"):
                    which = int(kind == "kT")
                    pe.wait_ge(roped_ready, arg + 1)
                    turn(kind, arg, lambda t, w=which: roped[:, w, t, :, :, :].rearrange("p r d m -> p (r d m)"))
                elif kind == "max":
                    maxima(*arg)
                elif kind == "mturn":
                    max_turn(arg)
                elif kind == "scores":
                    scores(*arg)
                elif kind == "pv":
                    pv(arg)
                elif kind == "oT":
                    pe.wait_ge(o_ready, arg + 1)
                    turn(kind, arg, lambda t: o_raw[:, t * P:(t + 1) * P])
                elif kind == "onT":
                    pe.wait_ge(work_read_dve, frees("dve", turned("oT", NG * arg + NG - 1)))
                    turn(kind, arg, lambda t: o_norm[:, t, :])
                elif kind == "proj":
                    project(arg)
                elif kind == "x2T":
                    pe.wait_ge(xn2_ready, arg + 1)
                    turn(kind, arg, lambda t: xn2[:, t, :])
                elif kind == "gate":
                    router(arg)
                elif kind == "cT":
                    combine_turn(arg)
                elif kind == "moe":
                    moe(*arg)
                elif kind == "moe_y":
                    moe_sum(*arg)

        @block.scalar
        def _(act):
            act.dma_start(xs[:, 0, :, :], x_v[0]).then_inc(ld_x[0], 16)

            def exp(s, i):
                n = BANKS[s, i]
                act.wait_ge(scores_full, n + 1)
                if n >= P_RING:
                    old = next(q for q in range(len(BURSTS)) if BANKS_TO[q] > n - P_RING)
                    act.wait_ge(pv_done, old + 1)
                act.activation(probs[:, n % P_RING, :], bank(ST_BANK + n % ST_RING), ACT.Exp,
                               scale=SCALE).then_inc(exp_done, 1)

            def keep(kind, arg, dst, cols):
                act.wait_ge(work_full, turned(kind, arg))
                act.copy(dst, wbank(kind, arg)[:, 0:cols]).then_inc(work_read_act, 1)

            def qkv(tile):
                x, t = tile // TPC, tile % TPC
                b, kt = x // 2, tile % KT
                act.wait_ge(work_full, turned("qkv", tile))
                w = wbank("qkv", tile)
                if x >= 1:
                    act.wait_ge(roped_ready, x)
                both = w[:, 0:2 * P].rearrange("p (w h d) -> p w h d", w=2, h=H)
                act.copy(qk[:, :, t, :, :], both)
                act.activation(sq[:, :, t, :, :], both, ACT.Square)
                if t == 0:
                    act.wait_ge(v_set, b + 1)
                act.copy(v_ones[:, b, kt, :, 0:HD], w[:, 2 * P:3 * P].rearrange("p (h d) -> p h d", h=H)
                         ).then_inc(work_read_act, 1)

            def leading_part(kind, x):
                which = int(kind == "kT")
                act.wait_ge(work_full, turned(kind, x))
                if x >= 1:
                    act.wait_ge(stacked[x - 1], 16 * 24)
                act.copy(parts[:, which, 0, :], wbank(kind, x)).then_inc(part_hi, 1)

            def moe(x, n):
                at, u = 2 * UNITS * x + n, unit(n)[1]
                act.wait_ge(work_full, turned("moe", (x, n)))
                if x == 0 and n == 0:
                    act.wait_ge(consts, 2)
                if at >= MOE_RING:
                    act.wait_ge(h_ready, at - MOE_RING + 1)
                act.activation(mu[:, at % MOE_RING, :], wbank("moe", (x, n))[:, 0:HALF], ACT.Identity,
                               bias=b1h[:, u:u + 1], scale=0.5).then_inc(act_u, 1)
                act.wait_ge(act_u, at + 1)
                act.activation(mt[:, at % MOE_RING, :], mu[:, at % MOE_RING, :], ACT.Tanh).then_inc(act_t, 1)

            def leave(a):
                act.wait_ge(pv_done, max(s for s, (q, _) in enumerate(BURSTS) if q == a) + 1)
                if a >= 1:
                    act.wait_ge(work_full, turned("oT", a - 1))
                act.copy(o_raw[:, :], bank(ACC_BANK)).then_inc(o_ready, 1)

            for kind, arg in SCHEDULE:
                if kind == "weights_read":
                    keep("weights", arg, w_qkv[:, :], 3 * P)
                elif kind == "weights2_read":
                    keep("weights2", arg, w_o[:, :], P + E)
                elif kind == "xT_read":
                    keep("xT", arg, xnT[:, :], CH)
                elif kind == "qkv_read":
                    qkv(arg)
                elif kind in ("qT_lead", "kT_lead"):
                    leading_part(kind[:2], arg)
                elif kind == "exp":
                    exp(*arg)
                elif kind == "leave":
                    leave(arg)
                elif kind == "onT_read":
                    keep("onT", arg, o_normT[:, :], CH)
                elif kind == "x2T_read":
                    keep("x2T", arg, x2T[:, arg % 2, :], CH)
                elif kind == "gate_exp":
                    act.wait_ge(work_read_dve, frees("dve", turned("gate", arg)))
                    act.activation(lg[:, 1, :, :], lg[:, 0, :, :], ACT.Exp).then_inc(gate_exp, 1)
                elif kind == "moe_act":
                    moe(*arg)

        @block.gpsimd
        def _(pool):
            links = [0]

            def link(ins):
                links[0] += 1
                ins.then_inc(pool_chain, 1)
                pool.wait_ge(pool_chain, links[0])

            def rope_direct(x):
                c = x % 2
                if x == 0:
                    pool.wait_ge(tables_ready, 1)
                pool.wait_ge(rope_a, x + 1)
                for w in range(2):
                    for tab, src, op in ((g_cos, sq, ALU.mult), (g_add, qk, ALU.add)):
                        t = tab[:, w, 4 * c:4 * c + 4, :].unsqueeze(2).broadcast_to([P, TPC, H, HD])
                        last = pool.tensor_tensor(qk[:, w, :, :, :], src[:, w, :, :, :], t, op)
                        if op == ALU.mult:
                            link(last)
                last.then_inc(rope_direct_ready, 1)

            def lower_parts(kind, x):
                which = int(kind == "kT")
                pool.wait_ge(part_mid, 2 * x + which + 1)
                pool.tensor_tensor(parts[:, which, 2, :], resid[:, which, :], parts[:, which, 1, :],
                                   ALU.subtract).then_inc(parts_lo, 1)

            for kind, arg in SCHEDULE:
                if kind == "ones":
                    pool.memset(v_ones[:, arg, :, :, :], 1.0).then_inc(v_set, 1)
                    pool.memset(k_st[:, arg, :, :].rearrange("p m q -> p (m q)").bitcast(F32), TWO_ONES).then_inc(k_set, 1)
                elif kind == "zero":
                    pool.memset(q_st[:, arg, :, :, :].rearrange("p m r q -> p (m r q)").bitcast(F32), 0.0).then_inc(q_set, 1)
                elif kind == "xbo":
                    if arg == 0:
                        pool.wait_ge(ld_rope, 16 * N_ROPE)
                    pool.wait_ge(xn_ready, arg + 1)
                    pool.tensor_tensor(xs[:, arg, :, :], xs[:, arg, :, :],
                                       bo_b[:, :].unsqueeze(1).broadcast_to([P, TPC, P]), ALU.add
                                       ).then_inc(xbo_ready, 1)
                elif kind == "rope_pool":
                    rope_direct(arg)
                elif kind in ("qT_low", "kT_low"):
                    lower_parts(kind[:2], arg)
                elif kind == "mask":
                    s, i = arg
                    a, k = BURSTS[s]
                    blocks, n = bursts_of(a // NG % 2)[k][i][1], BANKS[arg]
                    pool.wait_ge(exp_done, n + 1)
                    v = probs[:, n % P_RING, :].rearrange("p (r q) -> p r q", q=P)[:, blocks, :]
                    pool.affine_select(out=v, in_=v, compare_op=ALU.is_ge, fill=0.0, base=0,
                                       pattern=[[0, v.shape[1]], [1, P]], channel_multiplier=-1
                                       ).then_inc(masked, 1)
                elif kind == "weight":
                    x, n = arg
                    at, (half, u) = 2 * UNITS * x + n, unit(n)
                    if n == 1:
                        pool.wait_ge(ld_combine, 32 * (x + 1))
                    pool.wait_ge(h_ready, at + 1)
                    pool.tensor_tensor(mh[:, at % MOE_RING, :], mh[:, at % MOE_RING, :],
                                       comb_b[:, u, half * HALF:(half + 1) * HALF], ALU.mult).then_inc(weighted, 1)

        @block.vector
        def _(dve):
            links = [0]

            def link(ins):
                links[0] += 1
                ins.then_inc(chain, 1)
                dve.wait_ge(chain, links[0])

            def rsqrt(out, v, n):
                y, half, sq_v = seed[:, 0:n].bitcast(F32), nr[:, 0, 0:n], nr[:, 1, 0:n]
                link(dve.tensor_scalar(seed[:, 0:n], v.bitcast(I32), 1, None, ALU.logical_shift_right))
                link(dve.tensor_scalar(seed[:, 0:n], seed[:, 0:n], -1, RSQRT_SEED, ALU.mult, ALU.add))
                for step in range(3):
                    link(dve.scalar_tensor_tensor(out=half, in0=y, scalar=-0.5, in1=y, op0=ALU.mult, op1=ALU.mult))
                    link(dve.tensor_tensor(sq_v, half, v, ALU.mult))
                    last = dve.scalar_tensor_tensor(out=(y if step < 2 else out), in0=sq_v, scalar=1.5, in1=y,
                                                    op0=ALU.add, op1=ALU.mult)
                    link(last)

            def norm(kind, x):
                for t in range(TPC):
                    last = dve.bn_stats(stats[:, t, :], xs[:, x, t, :])
                link(last)
                for t in range(TPC):
                    last = dve.bn_aggr(mv[:, t, :], stats[:, t, :])
                link(last)
                link(dve.tensor_scalar(rstd[:, :], mv[:, :, 1], EPS, None, ALU.add))
                rsqrt(rstd[:, :], rstd[:, :], TPC)
                dst, ready = (xn, xn_ready) if kind == "norm" else (xn2, xn2_ready)
                if x >= 1:
                    dve.wait_ge(work_full, turned("xT" if kind == "norm" else "x2T", x - 1))
                for t in range(TPC):
                    last = dve.tensor_scalar(dst[:, t, :], xs[:, x, t, :], mv[:, t, 0:1], rstd[:, t:t + 1],
                                             ALU.subtract, ALU.mult)
                last.then_inc(ready, 1)

            def head_sums(x):
                dve.wait_ge(work_read_act, frees("act", turned("qkv", TPC * x + TPC - 1)))
                link(dve.tensor_reduce(ssum[:, :], sq[:, :, :, :, :].rearrange("p w t h d -> p (w t h) d"), AX.X,
                                       ALU.add))

            def head_rstd(x):
                link(dve.tensor_scalar(hvar[:, :], ssum[:, :], 1.0 / HD, EPS, ALU.mult, ALU.add))
                rsqrt(hrstd[:, :], hvar[:, :], 2 * TPC * H)

            def head_scale(x):
                dve.tensor_tensor(sq[:, :, :, :, :].rearrange("p w t h d -> p (w t h) d"),
                                  qk[:, :, :, :, :].rearrange("p w t h d -> p (w t h) d"),
                                  hrstd[:, :].unsqueeze(2).broadcast_to([P, 2 * TPC * H, HD]),
                                  ALU.mult).then_inc(rope_a, 1)

            def rope_rotated(x):
                c = x % 2
                dve.wait_ge(rope_a, x + 1)
                if x >= 1:
                    dve.wait_ge(work_full, turned("kT", x - 1))
                for w in range(2):
                    for j in range(2):
                        for par in range(2):
                            t = g_sin[:, w, 4 * c:4 * c + 4, 4 * j:4 * j + 4].unsqueeze(2).broadcast_to([P, TPC, H // 2, 4])
                            last = dve.tensor_tensor(by_head(w, par)[:, :, :, 4 * j:4 * j + 4],
                                                     sq[:, w, :, par::2, 1 - j::2], t, ALU.mult)
                link(last)

            def by_head(w, par):
                return roped[:, w, :, par, :, :].rearrange("p t d m -> p t m d")

            def rope_sum(x):
                dve.wait_ge(rope_direct_ready, x + 1)
                for w in range(2):
                    for par in range(2):
                        last = dve.tensor_tensor(by_head(w, par), qk[:, w, :, par::2, :], by_head(w, par), ALU.add)
                last.then_inc(roped_ready, 1)

            def remainder(kind, x):
                which = int(kind == "kT")
                dve.wait_ge(part_hi, 2 * x + which + 1)
                if x >= 1:
                    dve.wait_ge(parts_lo, 2 * x)
                dve.tensor_tensor(resid[:, which, :], wbank(kind, x), parts[:, which, 0, :],
                                  ALU.subtract).then_inc(work_read_dve, 1)
                dve.wait_ge(work_read_dve, frees("dve", turned(kind, x)))
                if x >= 1:
                    dve.wait_ge(stacked[x - 1], 16 * 24)
                dve.tensor_copy(parts[:, which, 1, :], resid[:, which, :]).then_inc(part_mid, 1)

            def maxima(a, u):
                n = MAXES[a, u]
                what, qt, heads, keys = max_units_of(a // NG % 2)[u]
                j, nh = heads[0], len(heads)
                w = bank(MAX_BANK + n % MAX_RING)[:, 0:nh * keys].rearrange("p (h k) -> p h k", h=nh)
                dst = mx_full if what == "full" else mx_diag
                if u == 0 and a >= 1:
                    dve.wait_ge(neg_ready, a)
                dve.wait_ge(max_full, n + 1)
                dve.tensor_reduce(dst[:, qt, j % 2, j // 2:j // 2 + nh], w, AX.X, ALU.max).then_inc(max_free, 1)

            def max_negate(a):
                dve.wait_ge(max_free, MAXES[a, len(max_units_of(a // NG % 2)) - 1] + 1)
                m = mx_diag[:, :, :, :].rearrange("p t r m -> p (t r) m")
                if a // NG % 2:
                    link(dve.tensor_tensor(mx[:, :, :], m, mx_full[:, :, :, :].rearrange("p t r m -> p (t r) m"), ALU.max))
                    m = mx[:, :, :]
                if a >= 1:
                    dve.wait_ge(work_full, turned("mturn", a - 1))
                link(dve.tensor_scalar(negmax[:, :, 0, :], m, -1.0, None, ALU.mult))
                dve.scalar_tensor_tensor(out=negmax[:, :, 1, :], in0=m, scalar=-1.0, in1=negmax[:, :, 0, :],
                                         op0=ALU.mult, op1=ALU.subtract).then_inc(neg_ready, 1)

            def max_copy(a):
                dve.wait_ge(work_full, turned("mturn", a))
                if a >= 2:
                    dve.wait_ge(maxrow_in[a % 2], 32 * (a // 2))
                dve.tensor_copy(maxT[:, a % 2, :], wbank("mturn", a).bitcast(BF16)[0:8, 0:CH]).then_inc(work_read_dve, 1)

            def normalise(a):
                g = a % NG
                dve.wait_ge(work_full, turned("oT", a))
                w = wbank("oT", a).rearrange("p (t j v) -> p t j v", t=TPC, j=G)
                link(dve.reciprocal(rden[:, :, :, :], w[:, :, :, HD:HD + 1]))
                dst = o_norm[:, :, G * HD * g:G * HD * (g + 1)].rearrange("p t (j d) -> p t j d", j=G)
                last = dve.tensor_tensor(dst, w[:, :, :, 0:HD], rden[:, :, :, :].broadcast_to([P, TPC, G, HD]), ALU.mult)
                last.then_inc(work_read_dve, 1)

            def two_largest(v, ranks, width, t, small, out_mask):
                link(dve.tensor_reduce(small[0], v, AX.X, ALU.max))
                for turn in range(2):
                    link(dve.tensor_tensor(t[0], v if turn == 0 else t[2], wide(small[0], width), ALU.is_equal))
                    link(dve.tensor_tensor(t[0], t[0], ranks, ALU.mult))
                    link(dve.tensor_reduce(small[1], t[0], AX.X, ALU.max))
                    link(dve.tensor_tensor(t[1 + 2 * turn], t[0], wide(small[1], width), ALU.is_equal))
                    if turn == 0:
                        link(dve.scalar_tensor_tensor(out=t[2], in0=t[1], scalar=3 * MASKED, in1=v,
                                                      op0=ALU.mult, op1=ALU.add))
                        link(dve.tensor_reduce(small[0], t[2], AX.X, ALU.max))
                link(dve.tensor_tensor(out_mask, t[1], t[3], ALU.add))

            def router(x):
                dve.wait_ge(work_full, turned("gate", x))
                w = wbank("gate", x)[:, 0:TPC * E].rearrange("p (t e) -> p t e", t=TPC)

                link(dve.tensor_reduce(red[:, 0, :], w, AX.X, ALU.max))
                dve.tensor_tensor(lg[:, 0, :, :], w, wide(red[:, 0, :]), ALU.subtract).then_inc(work_read_dve, 1)

            def grouped(m):
                return m.rearrange("p t (g e) -> p (t g) e", g=NGRP)

            def wide(m, width=E):
                return m.unsqueeze(2).broadcast_to([P, m.shape[1], width])

            def route1(x):
                dve.wait_ge(gate_exp, x + 1)
                link(dve.tensor_reduce(red[:, 1, :], lg[:, 1, :, :], AX.X, ALU.add))
                link(dve.reciprocal(red[:, 2, :], red[:, 1, :]))
                link(dve.tensor_tensor(lg[:, 2, :, :], lg[:, 1, :, :], wide(red[:, 2, :]), ALU.mult))
                link(dve.tensor_tensor(lg[:, 3, :, :], lg[:, 2, :, :],
                                       gate_bb[:, :].unsqueeze(1).broadcast_to([P, TPC, E]), ALU.add))
                s = grouped(lg[:, 3, :, :])
                dve.tensor_tensor(pair_sums[:, :, 0:3], s[:, :, 0:3], s[:, :, 1:4], ALU.add)
                dve.tensor_tensor(pair_sums[:, :, 3:5], s[:, :, 0:2], s[:, :, 2:4], ALU.add)
                link(dve.tensor_tensor(pair_sums[:, :, 5:6], s[:, :, 0:1], s[:, :, 3:4], ALU.add))
                link(dve.tensor_reduce(gsm[:, 0, :, :].rearrange("p t g -> p (t g)"), pair_sums[:, :, :], AX.X, ALU.max))

            def route2(x):
                two_largest(gsm[:, 0, :, :], rank[:, E - NGRP:E].unsqueeze(1).broadcast_to([P, TPC, NGRP]), NGRP,
                            [gsm[:, 1 + i, :, :] for i in range(4)], (red[:, 3, :], red[:, 4, :]), gsm[:, 5, :, :])
                link(dve.tensor_scalar(gsm[:, 6, :, :], gsm[:, 5, :, :], -MASKED, MASKED, ALU.mult, ALU.add))
                per = [gsm[:, i, :, :].rearrange("p t g -> p (t g)") for i in (5, 6)]
                link(dve.tensor_tensor(grouped(lg[:, 4, :, :]), grouped(lg[:, 3, :, :]), wide(per[0], E // NGRP), ALU.mult))
                link(dve.tensor_tensor(grouped(lg[:, 5, :, :]), grouped(lg[:, 4, :, :]), wide(per[1], E // NGRP), ALU.add))

            def route3(x):
                two_largest(lg[:, 5, :, :], rank[:, :].unsqueeze(1).broadcast_to([P, TPC, E]), E,
                            [lg[:, 6 + i, :, :] for i in range(4)], (red[:, 5, :], red[:, 6, :]), lg[:, 10, :, :])
                dve.tensor_tensor(lg[:, 11, :, :], lg[:, 2, :, :], lg[:, 10, :, :], ALU.mult).then_inc(comb_ready, 1)

            def combine_rows(x):
                dve.wait_ge(work_full, turned("cT", x))
                if x >= 1:
                    dve.wait_ge(st_combine, 16 * x)
                    dve.wait_ge(y_done, 2 * UNITS * x)
                dve.tensor_copy(combT[0:E, :], wbank("cT", x)[0:E, :]).then_inc(work_read_dve, 1)

            def moe(x, n):
                at, u = 2 * UNITS * x + n, unit(n)[1]
                dve.wait_ge(act_t, at + 1)
                dve.scalar_tensor_tensor(out=mt[:, at % MOE_RING, :], in0=mt[:, at % MOE_RING, :], scalar=1.0, in1=mu[:, at % MOE_RING, :],
                                         op0=ALU.add, op1=ALU.mult).then_inc(h_used, 1)
                dve.wait_ge(h_used, at + 1)
                if at >= MOE_RING:
                    dve.wait_ge(y_done, at - MOE_RING + 1)
                dve.scalar_tensor_tensor(out=mh[:, at % MOE_RING, :], in0=wbank("moe", (x, n))[:, HALF:CH],
                                         scalar=b3[:, u:u + 1], in1=mt[:, at % MOE_RING, :], op0=ALU.add, op1=ALU.mult
                                         ).then_inc(h_ready, 1)

            def tables():
                dve.wait_ge(ld_rope, 16 * N_ROPE)
                dve.tensor_copy(gb_rot[:, :, 0:4], gb[:, :, 1::2])
                link(dve.tensor_copy(gb_rot[:, :, 4:8], gb[:, :, 0::2]))
                for w in range(2):
                    def affine(m, i, w=w):
                        return m[:, 2 * w + i, :].unsqueeze(1).broadcast_to([P, KT, HD])
                    dve.tensor_tensor(g_cos[:, w, :, :], rope[:, :, 0, :], affine(gb, 0), ALU.mult)
                    dve.tensor_tensor(g_sin[:, w, :, :], rope[:, :, 1, :], affine(gb_rot, 0), ALU.mult)
                    dve.tensor_tensor(g_add[:, w, :, :], rope[:, :, 0, :], affine(gb, 1), ALU.mult)
                    link(dve.tensor_tensor(g_tmp[:, w, :, :], rope[:, :, 1, :], affine(gb_rot, 1), ALU.mult))
                dve.tensor_tensor(g_add[:, :, :, :], g_add[:, :, :, :], g_tmp[:, :, :, :], ALU.add).then_inc(tables_ready, 1)

            link(dve.memset(combT[:, :], 1.0))
            dve.memset(bank(ACC_BANK), 0.0)
            for kind, arg in SCHEDULE:
                if kind == "tables":
                    tables()
                elif kind == "norm":
                    dve.wait_ge(ld_x[arg], 16)
                    norm(kind, arg)
                elif kind == "norm2":
                    dve.wait_ge(work_read_dve, frees("dve", turned("proj", arg)))
                    norm(kind, arg)
                elif kind == "headsum":
                    head_sums(arg)
                elif kind == "headrstd":
                    head_rstd(arg)
                elif kind == "headscale":
                    head_scale(arg)
                elif kind == "rope":
                    rope_rotated(arg)
                elif kind == "rope_sum":
                    rope_sum(arg)
                elif kind in ("qT_rest", "kT_rest"):
                    remainder(kind[:2], arg)
                    if kind == "kT_rest" and arg == 0:
                        dve.wait_ge(ld_moe, 16 * N_MOE)
                        dve.wait_ge(ld_attn, 16 * N_ATTN)
                        dve.tensor_copy(ident_bf[:, :], ident[:, :])
                        dve.tensor_copy(causal_bf[:, :], causal[:, :]).then_inc(consts, 1)
                        dve.tensor_scalar(b1h[:, :], b1[:, :], 0.5, None, ALU.mult).then_inc(consts, 1)
                elif kind == "maxred":
                    maxima(*arg)
                elif kind == "mneg":
                    max_negate(arg)
                elif kind == "mcopy":
                    max_copy(arg)
                elif kind == "oT_read":
                    normalise(arg)
                elif kind == "proj_read":
                    dve.wait_ge(work_full, turned("proj", arg))
                    dve.wait_ge(xbo_ready, arg + 1)
                    dve.tensor_tensor(xs[:, arg, :, :], wbank("proj", arg).rearrange("p (t d) -> p t d", t=TPC),
                                      xs[:, arg, :, :], ALU.add).then_inc(work_read_dve, 1)
                elif kind == "gate_read":
                    router(arg)
                elif kind == "route1":
                    route1(arg)
                elif kind == "route2":
                    route2(arg)
                elif kind == "route3":
                    route3(arg)
                elif kind == "cT_read":
                    combine_rows(arg)
                elif kind == "moe_dve":
                    moe(*arg)
                elif kind == "final":
                    dve.wait_ge(y_done, 2 * UNITS * (arg + 1))
                    dve.tensor_tensor(xs[:, arg, :, :], bank(Y_BANK).rearrange("p (t d) -> p t d", t=TPC),
                                      xs[:, arg, :, :], ALU.add).then_inc(out_ready, 1)
    return nc


_INS = ["x", "Wq", "Wk", "Wv", "q_gamma", "q_beta", "k_gamma", "k_beta", "Wo", "bo"]
_FFN = ["gate_w", "gate_b", "We1", "be1", "We2", "be2", "We3", "be3", "ws1", "bs1", "ws2", "bs2", "ws3", "bs3"]


def shape_constants():
    f = np.float32
    ident = np.eye(P, dtype=f)
    center = (ident - np.kron(np.eye(H, dtype=f), np.full((HD, HD), 1.0 / HD, f))).astype(f)
    q, k = np.arange(P)[:, None], np.arange(P)[None, :]
    causal = np.where(k > q, f(MASKED), f(0)).astype(f)
    di = np.arange(0, HD, 2, dtype=f) / f(HD)
    theta = np.arange(S, dtype=f)[:, None] * np.exp(-di * f(np.log(10000.0)))
    cos, sin = (np.repeat(fn(theta.astype(f)), 2, axis=1).astype(f) for fn in (np.cos, np.sin))
    sin[:, 0:HD // 2] *= -1
    rope = np.stack([cos, sin], axis=1).reshape(KT, P, 2, HD).transpose(1, 0, 2, 3)
    rank = np.broadcast_to(np.arange(E, 0, -1, dtype=f), (P, E))
    return {"c_ident": ident, "c_center": center, "c_causal": causal, "c_rope": rope, "c_rank": rank}


def kernel(**inputs):
    import concourse.bacc as _bacc
    from concourse.bass_utils import run_bass_kernel_spmd as _run

    nc = _bacc.Bacc("TRN2", target_bir_lowering=False, num_devices=1)
    given = {n: inputs["L0_attn_" + n] for n in _INS} | {n: inputs["L0_ffn_" + n] for n in _FFN} | shape_constants()
    arrays, args = {}, []
    for name, a in given.items():
        a = np.ascontiguousarray(a)
        arrays["in_" + name] = a
        args.append(nc.dram_tensor("in_" + name, a.shape, mybir.dt.from_np(a.dtype), kind="ExternalInput").ap())
    out = nc.dram_tensor("out_0", (B, S, D), F32, kind="ExternalOutput").ap()
    layer_kernel(nc, *args, out)
    r = _run(nc, [arrays], core_ids=[0])
    return r.results[0]["out_0"]
```

```python
from contextlib import ExitStack

import numpy as np
import concourse.bass as bass
from concourse import mybir

F32 = mybir.dt.float32
BF16 = mybir.dt.bfloat16
I32 = mybir.dt.int32
ALU = mybir.AluOpType
ACT = mybir.ActivationFunctionType
AX = mybir.AxisListType

P = 128
B, S, D = 2, 1024, 128
H, HD = 16, 8
E, INTER, NGRP = 16, 64, 4
CH = 512
NX = B * S // CH
TPC = CH // P
KT = S // P
G = 4
NG = H // G
NA = NX * NG
PAIRS = E // 2
UNITS = PAIRS + 1
HALF = CH // 2
BIAS_STEP = 2
SCALE = float(HD) ** -0.5
EPS = 1e-5
TERMS_Q = [0, 0, 1, 1, 0, 2]
TERMS_K = [0, 1, 0, 1, 2, 0]
N_STACK = 3 * len(TERMS_Q)
N_STACK_POOL = sum(part > 0 for part in TERMS_K)
KM = P - 2
VC = 16
MASKED = -1e30
RSQRT_SEED = 0x5F3759DF
TWO_ONES = float(np.array([0x3F803F80], np.uint32).view(np.float32)[0])
ST_RING, P_RING, MOE_RING = 3, 10, 4
ST_BANK, ACC_BANK, WORK_BANKS, Y_BANK = 0, 3, (4, 5, 6), 7


def bursts_of(c):
    out = [[([(j, kt, 0, CH, 0)], None) for j in range(G)] for kt in range(4 * c)]
    out.append([([(j, 4 * c, 0, CH, 0)], slice(0, 1)) for j in range(G)])
    out.append([([(j, 4 * c + 1, 0, 384, 128), (j, 4 * c + 3, 384, 128, 384)], slice(0, 4, 3)) for j in range(G)])
    out.append([([(j, 4 * c + 2, 0, 256, 256), (j + 2, 4 * c + 2, 256, 256, 256)], slice(0, 4, 2)) for j in range(2)])
    return out


def max_units_of(c):
    units = [("full", qt, [j], 512) for qt in range(TPC) for j in range(G)] if c else []
    for qt in range(TPC):
        keys = P * (qt + 1)
        for j in range(2):
            units += [("diag", qt, [j, j + 2], keys)] if qt < 2 else [("diag", qt, [j], keys), ("diag", qt, [j + 2], keys)]
    return units


def unit(n):
    return (n, PAIRS) if n < 2 else divmod(n - 2, PAIRS)


FILLS_READ = {"weights": ("weights_read", "act"), "weights2": ("weights2_read", "act"), "xT": ("xT_read", "act"),
              "qkv": ("qkv_read", "act"), "qT": ("qT_rest", "dve"), "kT": ("kT_rest", "dve"),
              "mturn": ("mcopy", "dve"), "oT": ("oT_read", "dve"), "onT": ("onT_read", "act"),
              "proj": ("proj_read", "dve"), "x2T": ("x2T_read", "act"), "gate": ("gate_read", "dve"),
              "cT": ("cT_read", "act"), "moe": ("moe_u", "experts"), "max": ("maxred", "maxima")}
READS = {stage: reader for stage, reader in FILLS_READ.values()}
LENGTHS = {
    "pe": {"weights": 1.06, "weights2": .3, "xT": .44, "qkv": .65, "qT": .44, "kT": .44, "scores": .22, "mturn": .25,
           "pv": .92, "oT": .44, "onT": .44, "proj": .87, "x2T": .44, "gate": .87, "cT": .44, "moe": .86,
           "moe_y": .45, "max": .25},
    "act": {"norm_apply": 1.6, "norm2_apply": 1.6, "weights_read": .4, "weights2_read": .2, "xT_read": .5,
            "qkv_read": .72, "qT_lead": .5, "kT_lead": .5, "exp": .49, "leave": .5, "onT_read": .5, "x2T_read": .5,
            "gate_exp": .2, "cT_read": .5, "moe_u": .6, "moe_t": .28},
    "dve": {"norm": 3.9, "tables": 1.85, "headsum": 1.15, "headrstd": 3.65, "headscale": 1.15, "rope": 1.35,
            "rope_sum": 1.35, "qT_rest": 1.1, "kT_rest": 1.1, "maxred": .6, "mneg": .5, "mcopy": .35, "oT_read": .5,
            "proj_read": .6, "norm2": 3.9, "gate_read": .4, "route1": 1.65, "route2": 3.2, "route3": 3.3,
            "gated": .36, "weight_dve": .4, "final": .6},
    "pool": {"ones": 5.2, "zero": 6.9, "xbo": 1.3, "rope_pool": 4.9, "qT_low": 1.2, "kT_low": 1.2, "mask": .35,
             "weight": .75, "stack_pool": 3.2, "moe_h": .75},
    "sp": {"stack": 3.9, "mrow": .65, "cstore": .6, "cload": 1.2, "store": .6},
}
ENGINE = {kind: engine for engine, kinds in LENGTHS.items() for kind in kinds}
DMA_DONE = {"stack": 6.1, "stack_pool": 8.5, "mrow": 2.6, "cstore": 2.3, "cload": 4.7,
            "store": 3.0}
PE_TICK, PE_BUSY = 3.413, 1.3
SIGNAL = 0.12


def plan():
    bursts = [(a, k) for a in range(NA) for k in range(len(bursts_of(a // NG % 2)))]
    first = {a: min(s for s, (q, _) in enumerate(bursts) if q == a) for a in range(NA)}
    first[NA] = len(bursts)
    banks = [(s, i) for s, (a, k) in enumerate(bursts) for i in range(len(bursts_of(a // NG % 2)[k]))]
    units = [(a, u) for a in range(NA) for u in range(len(max_units_of(a // NG % 2)))]
    burst_end = {s: max(n for n, (q, _) in enumerate(banks) if q == s) for s in range(len(bursts))}
    needs, urgency = {}, {}

    def add(kind, arg, key, *after):
        assert (kind, arg) not in needs
        needs[kind, arg] = [q for q in after if q is not None]
        urgency[kind, arg] = key

    def stacked_last(x, which):
        return ("stack", (x, which, 1)) if (x, which) != (0, 1) else ("stack_pool", 0)

    def old(kind, arg, ok):
        return (kind, arg) if ok else None

    add("weights", 0, -30)
    add("weights_read", 0, -30, ("weights", 0))
    add("weights2", 0, -29, ("weights", 0))
    add("weights2_read", 0, -29, ("weights2", 0))
    add("tables", 0, -20, ("norm", 0))
    add("ones", 0, -40)
    add("zero", 0, -39)
    add("zero", 1, -12, ("xbo", 0), ("ones", 0))
    add("ones", 1, -11, ("kT_low", 0))

    def window(lo, hi, what):
        return {stage: lo + n * (hi - lo) / len(what) for n, stage in enumerate(what)}

    for x in range(NX):
        lo, hi = PREP_WINDOWS[x]
        tiles = range(TPC * x, TPC * x + TPC)
        names = (["norm", "norm_apply", "xbo", "xT", "xT_read"] + [n for t in tiles for n in (("qkv", t), ("qkv_read", t))] +
                 ["headsum", "headrstd", "headscale", "rope_pool", "rope", "rope_sum", "qT", "qT_lead", "qT_rest",
                  "qT_low", "kT", "kT_lead", "kT_rest", "kT_low"])
        at = window(lo, hi, names)
        p = x - 1
        add("norm", x, at["norm"], old("norm_apply", p, x >= 2), old("kT_rest", x - 2, x >= 2))
        applied = "norm_apply" if x else "norm"
        if x:
            add("norm_apply", x, at["norm_apply"], ("norm", x), old("xT", p, x))
        add("xbo", x, at["xbo"] + 3, (applied, x))
        add("xT", x, at["xT"], (applied, x), ("weights", 0))
        add("xT_read", x, at["xT_read"], ("xT", x), old("qkv", TPC * x - 1, x))
        for t in tiles:
            add("qkv", t, at["qkv", t], ("xT_read", x), ("weights_read", 0), old("qkv", t - 1, t))
            add("qkv_read", t, at["qkv_read", t], ("qkv", t), ("ones", x // 2), old("rope_sum", p, x))
        add("headsum", x, at["headsum"], *[("qkv_read", t) for t in tiles])
        add("headrstd", x, at["headrstd"], ("headsum", x))
        add("headscale", x, at["headscale"], ("headrstd", x))
        add("rope_pool", x, at["rope_pool"], ("headscale", x), ("tables", 0))
        add("rope", x, at["rope"], ("headscale", x), ("tables", 0), old("kT", p, x))
        add("rope_sum", x, at["rope_sum"], ("rope", x), ("rope_pool", x))
        for w, k in enumerate("qk"):
            add(k + "T", x, at[k + "T"], ("rope_sum", x), old("qT", x, w))
            add(k + "T_lead", x, at[k + "T_lead"], (k + "T", x), stacked_last(p, 1) if x else None, old("qT_lead", x, w))
            add(k + "T_rest", x, at[k + "T_rest"], (k + "T_lead", x))
            add(k + "T_low", x, at[k + "T_low"], (k + "T_rest", x), old("qT_low", x, w))
            add("stack", (x, w, 0), at[k + "T_lead"], (k + "T_lead", x),
                ("scores", banks[burst_end[first[NG * (x - 1)] - 1]]) if x >= 2 and w == 0 else None,
                old("ones", x // 2, w), old("zero", x, w == 0 and x < 2),
                old("stack", (x, 0, 1), w))
            if (x, w) == (0, 1):
                add("stack_pool", 0, -40, ("kT_low", 0), ("ones", 0))
            else:
                add("stack", (x, w, 1), at[k + "T_low"], (k + "T_low", x), ("stack", (x, w, 0)))
    for n, (a, u) in enumerate(units):
        x = a // NG
        lo, hi = MAX_WINDOWS[a]
        count = len(max_units_of(x % 2))
        key = lo + u * (hi - lo) / count
        add("max", (a, u), key, *[stacked_last(y, w) for y in range(x - x % 2, x + 1) for w in range(2)],
            old("max", units[n - 1], n))
        add("maxred", (a, u), key, ("max", (a, u)), old("maxred", units[n - 1], n), old("mneg", a - 1, u == 0 and a))
        if u == count - 1:
            add("mneg", a, hi, ("maxred", (a, u)), old("mturn", a - 1, a))
            add("mturn", a, hi, ("mneg", a))
            add("mcopy", a, hi, ("mturn", a), old("mrow", a - 2, a >= 2))
            add("mrow", a, hi, ("mcopy", a))
    for n, (s, i) in enumerate(banks):
        a, k = bursts[s]
        prev = banks[n - 1] if n else None
        reuse = next((q for q in range(len(bursts)) if burst_end[q] >= n - P_RING), None) if n >= P_RING else None
        add("scores", (s, i), s + i / 4, old("scores", prev, n), old("exp", banks[n - ST_RING] if n >= ST_RING else 0, n >= ST_RING),
            old("mrow", a, k == 0 and i == 0))
        add("exp", (s, i), s + i / 4, ("scores", (s, i)), old("exp", prev, n), old("pv", reuse, reuse is not None))
        if bursts_of(a // NG % 2)[k][i][1] is not None:
            add("mask", (s, i), s + i / 4, ("exp", (s, i)))
        if n == burst_end[s]:
            add("pv", s, s + PV_LAG, old("pv", s - 1, s), ("exp", (s, i)),
                *[("mask", (s, j)) for j in range(i + 1) if bursts_of(a // NG % 2)[k][j][1] is not None],
                old("leave", a - 1, k == 0 and a))
            if s + 1 == first[a + 1]:
                add("leave", a, s + 1, ("pv", s), old("oT", a - 1, a))
                add("oT", a, s + 1, ("leave", a))
                add("oT_read", a, s + 1, ("oT", a), old("onT", a // NG - 1, a >= NG and a % NG == 0), old("oT_read", a - 1, a))
    for x in range(NX):
        lo, hi = EPILOGUE_WINDOWS[x]
        names = ("onT onT_read proj proj_read norm2 norm2_apply x2T x2T_read gate gate_read gate_exp route1 route2 route3 "
                 "cT cT_read cstore").split()
        at = window(lo, hi, names)
        chain = {"onT": [("oT_read", NG * x + NG - 1)], "proj": [("weights2_read", 0)], "proj_read": [("xbo", x)],
                 "norm2": [old("norm2_apply", x - 1, x)], "norm2_apply": [old("x2T", x - 1, x)], "x2T_read": [old("moe", (x - 2, 2 * UNITS - 1), x >= 2)],
                 "cT_read": [old("cstore", x - 1, x), old("moe_y", (x - 1, BIAS_STEP), x)],
                 }
        for n, name in enumerate(names):
            add(name, x, at[name], old(names[n - 1], x, n), *chain.get(name, []))
        for half in range(2):
            add("cload", (x, half), at["cstore"], ("cstore", x), old("cload", (x, 0), half),
                old(WEIGHT_OF[x - 1], (x - 1, 2 + PAIRS * half + PAIRS - 1), x))
        lo, hi = MOE_WINDOWS[x]
        for n in range(2 * UNITS):
            key = lo + n * (hi - lo) / (2 * UNITS)
            g = 2 * UNITS * x + n

            def back(kind, d):
                return old(kind, divmod(g - d, 2 * UNITS), g >= d)
            add("moe", (x, n), key, ("x2T_read", x), back("moe", 1))
            pair = unit(n)[1] < PAIRS
            add("moe_u", (x, n), key, ("moe", (x, n)), back("moe_h", MOE_RING), back("moe_u", 1))
            add("moe_t", (x, n), key, ("moe_u", (x, n)), back("moe_y", MOE_RING), back("moe_t", 1))
            if pair:
                add(WEIGHT_OF[x], (x, n), key, ("moe_u", (x, n)), ("cload", (x, unit(n)[0])))
            add("gated", (x, n), key, ("moe_t", (x, n)), back("gated", 1))
            add("moe_h", (x, n), key, ("gated", (x, n)), back("moe_h", 1), (WEIGHT_OF[x], (x, n)) if pair else None)
            add("moe_y", (x, n), key, ("moe_h", (x, n)), back("moe_y", 1),
                old("final", x - 1, n == 0 and x), old("cT_read", x, n == BIAS_STEP))
        add("final", x, hi, ("moe_y", (x, 2 * UNITS - 1)))
        add("store", x, hi, ("final", x))

    def length(kind, arg):
        if kind in ("max", "maxred"):
            what, _, heads, keys = max_units_of(arg[0] // NG % 2)[arg[1]]
            cols = len(heads) * keys
            return (cols + P * len(heads) * (what == "diag")) / 2400 if kind == "max" else cols / 960 + .07
        if kind == "moe_y" and arg[1] == BIAS_STEP:
            return 1.3
        if kind in ("rope", "rope_pool") and arg == 0:
            return {"rope": 2.9, "rope_pool": 2.5}[kind]
        if kind == "norm" and arg == 0:
            return 4.8
        if kind == "stack" and arg[1]:
            return 1.95
        if kind == "pv":
            return .92 if bursts[arg][1] < len(bursts_of(bursts[arg][0] // NG % 2)) - 1 else .5
        return LENGTHS[ENGINE[kind]][kind]

    users = {stage: [] for stage in needs}
    missing, ready_at = {}, {}
    for stage, after in needs.items():
        missing[stage] = len(after)
        for q in after:
            users[q].append(stage)
    ready = {engine: [] for engine in LENGTHS}
    for stage, m in missing.items():
        ready_at[stage] = {"weights": 8.0, "norm": 5.0}.get(stage[0], 0.0)
        if not m:
            ready[ENGINE[stage[0]]].append(stage)
    free_at = {engine: 0.0 for engine in LENGTHS}
    order, fills, bank_free = [], {}, {bank: 0.0 for bank in WORK_BANKS + (Y_BANK,)}
    unread, pending = {}, {reader: [] for _, reader in FILLS_READ.values()}

    def is_free(bank, now):
        return bank not in unread and bank_free[bank] <= now

    def bank_for(kind, arg, now):
        if kind in FILLS_READ:
            return next((q for q in WORK_BANKS + (Y_BANK,) if is_free(q, now)), None)
        if kind == "moe_y" and arg[1] == 0 and not is_free(Y_BANK, now):
            return None
        return 0

    now, work = 0.0, {}
    while len(order) < len(needs):
        progress = False
        for engine in LENGTHS:
            if free_at[engine] > now:
                continue
            able = []
            for stage in ready[engine]:
                kind, arg = stage
                if ready_at[stage] > now:
                    continue
                if kind in READS and pending[READS[kind]][0] != stage:
                    continue
                if engine == "pe" and bank_for(kind, arg, now) is None:
                    continue
                able.append((urgency[stage], stage[0], str(stage[1]), stage))
            if not able:
                continue
            stage = min(able)[3]
            kind, arg = stage
            ready[engine].remove(stage)
            took = length(kind, arg)
            if engine == "pe":
                tick = int(now / PE_TICK)
                work[tick] = work.get(tick, 0.0) + took * (2 if kind == "pv" else 1)
                if work.get(tick - 1, 0.0) < PE_BUSY:
                    took = min(2 * took, max(took, (tick + 1) * PE_TICK - now + took / 2))
            end = now + took + .03
            free_at[engine] = end
            order.append(stage)
            progress = True
            if kind == "moe_y" and arg[1] == 0:
                unread[Y_BANK] = ("final", arg[0])
            if kind == "final":
                del unread[Y_BANK]
                bank_free[Y_BANK] = end + SIGNAL
            if kind in FILLS_READ:
                fills[stage] = bank_for(kind, arg, now)
                unread[fills[stage]] = (FILLS_READ[kind][0], arg)
                pending[FILLS_READ[kind][1]].append((FILLS_READ[kind][0], arg))
            if kind in READS:
                pending[READS[kind]].pop(0)
                for q in [q for q, reader in unread.items() if reader == stage]:
                    del unread[q]
                    bank_free[q] = end + SIGNAL
            for q in users[stage]:
                missing[q] -= 1
                same = ENGINE[q[0]] == engine
                if kind in DMA_DONE and q[0] != kind:
                    at = now + took - LENGTHS[engine][kind] + DMA_DONE[kind]
                else:
                    at = end + SIGNAL * (not same)
                ready_at[q] = max(ready_at[q], at)
                if not missing[q]:
                    ready[ENGINE[q[0]]].append(q)
        if not progress:
            later = [t for t in list(free_at.values()) + list(bank_free.values()) +
                     [ready_at[q] for lst in ready.values() for q in lst] if t > now]
            now = min(later)
    return bursts, banks, units, order, fills


PREP_WINDOWS = ((-41.1, -27.3), (-21.6, 2.1), (16, 26.4), (20.4, 36.8))
EPILOGUE_WINDOWS = ((11.9, 20.4), (35.3, 45.2), (53.4, 88.6), (55.9, 70.6))
MOE_WINDOWS = ((12.6, 47.1), (43.6, 52.2), (82.7, 84.5), (97.9, 98.3))
PV_LAG = 2.85
WEIGHT_OF = ("weight", "weight", "weight", "weight_dve")
MAX_WINDOWS = (
    (-21.2, -6.1), (-2.7, -2.2), (-21, -19.2), (1.5, 2), (5.1, 10), (12.8, 13.3), (10.5, 17.5), (16.7, 22.9),
    (18.8, 32.7), (32, 35.1), (39.5, 41.5), (41.3, 43.7), (45.6, 47.2), (47.5, 50.3), (40.4, 57.5), (57.5, 64.5))

BURSTS, BANK_LIST, UNIT_LIST, SCHEDULE, FILL_BANKS = plan()
BANKS = {key: n for n, key in enumerate(BANK_LIST)}
BANKS_TO = {s: max(n for (q, _), n in BANKS.items() if q == s) + 1 for s in range(len(BURSTS))}
MASKED_BANKS = [q for q in BANK_LIST if bursts_of(BURSTS[q[0]][0] // NG % 2)[BURSTS[q[0]][1]][q[1]][1] is not None]
MASKS_TO = {s: sum(q <= s for q, _ in MASKED_BANKS) for s in range(len(BURSTS))}
MAXES = {key: n for n, key in enumerate(UNIT_LIST)}
FILLS = list(FILL_BANKS)
FILL = {key: n for n, key in enumerate(FILLS)}
FILL_BANK = list(FILL_BANKS.values())
POS = {stage: n for n, stage in enumerate(SCHEDULE)}


def banks_before(a):
    return sum(BURSTS[s][0] < a for s, _ in BANKS)


def frees(reader, upto):
    return sum(FILLS_READ[kind][1] == reader for kind, _ in FILLS[:upto])


def layer_kernel(nc, x, Wq, Wk, Wv, q_gamma, q_beta, k_gamma, k_beta, Wo, bo, gate_w, gate_b,
                 We1, be1, We2, be2, We3, be3, ws1, bs1, ws2, bs2, ws3, bs3,
                 c_ident, c_center, c_causal, c_rope, c_rank, out):
    x_v = x.rearrange("b (h t p) d -> (b h) p t d", p=P, t=TPC)
    out_v = out.rearrange("b (h t p) d -> (b h) p t d", p=P, t=TPC)
    combine_dram = nc.dram_tensor("combine_scratch", [NX, E, CH], F32, kind="Internal").ap()

    with ExitStack() as ctx:
        def sb(name, shape, dt=F32):
            return ctx.enter_context(nc.sbuf_tensor(name, shape, dt))

        def sem(name):
            return ctx.enter_context(nc.semaphore(name))

        psum = ctx.enter_context(nc.psum_tensor("psum", [P, 8, 512], F32))

        ident = sb("ident", [P, P])
        ident_bf = sb("ident_bf", [P, P], BF16)
        center = sb("center", [P, P])
        causal = sb("causal", [P, P])
        causal_bf = sb("causal_bf", [P, P], BF16)
        rope = sb("rope", [P, KT, 2, HD])
        rank = sb("rank", [P, E])
        w_raw = sb("w_raw", [P, 4, P])
        gate_raw = sb("gate_raw", [E, P])
        w_qkv = sb("w_qkv", [P, 3 * P])
        w_o = sb("w_o", [P, P + E])
        gb = sb("gb", [P, 4, HD])
        gb_rot = sb("gb_rot", [P, 4, HD])
        g_cos = sb("g_cos", [P, 2, KT, HD])
        g_sin = sb("g_sin", [P, 2, KT, HD])
        g_add = sb("g_add", [P, 2, KT, HD])
        bo_b = sb("bo_b", [P, P])
        gate_bb = sb("gate_bb", [P, E])
        w1 = sb("w1", [P, UNITS, P])
        w3 = sb("w3", [P, UNITS, P])
        w2 = sb("w2", [P, UNITS, P])
        b1 = sb("b1", [P, UNITS])
        b1h = sb("b1h", [P, UNITS])
        ones_col = sb("ones_col", [P, 1])
        b3 = sb("b3", [P, UNITS])
        b2 = sb("b2", [E + 1, P])
        xs = sb("xs", [P, NX, TPC, P])
        xn = sb("xn", [P, TPC, P])
        xnT = sb("xnT", [P, CH])
        stats = sb("stats", [P, TPC, 6])
        mean_var = sb("mean_var", [P, TPC, 2])
        seed = sb("seed", [P, P], I32)
        nr = sb("nr", [P, 2, P])
        rstd = sb("rstd", [P, 2, TPC])
        shift = sb("shift", [P, 2, TPC])
        qk = sb("qk", [P, 2, TPC, H, HD])
        sq = sb("sq", [P, 2, TPC, H, HD])
        ssum = sb("ssum", [P, 2 * TPC * H])
        hvar = sb("hvar", [P, 2 * TPC * H])
        hrstd = sb("hrstd", [P, 2 * TPC * H])
        roped = sb("roped", [P, 2, TPC, 2, HD, H // 2])
        parts = sb("parts", [P, 2, 3, CH], BF16)
        resid = sb("resid", [P, 2, CH])
        g_tmp = resid[:, 0, 0:2 * KT * HD].rearrange("p (w t d) -> p w t d", w=2, t=KT)
        q_st = sb("q_st", [P, 2, H // 2, 2, CH], BF16)
        k_st = sb("k_st", [P, B, H // 2, S], BF16)
        v_ones = sb("v_ones", [P, B, KT, H, VC])
        mx_full = sb("mx_full", [P, TPC, 2, 2])
        mx_diag = sb("mx_diag", [P, TPC, 2, 2])
        mx = sb("mx", [P, TPC, G])
        negmax = sb("negmax", [P, TPC, 2, 2, 2], BF16)
        maxT = sb("maxT", [8, 2, CH], BF16)
        probs = sb("probs", [P, P_RING, CH])
        o_raw = sb("o_raw", [P, CH])
        rden = sb("rden", [P, TPC, G, 1])
        o_norm = sb("o_norm", [P, TPC, P])
        o_normT = sb("o_normT", [P, CH])
        x2T = sb("x2T", [P, 2, CH])
        lg = sb("lg", [P, 12, TPC, E])
        gsm = sb("gsm", [P, 16, TPC, NGRP])
        pair_sums = sb("pair_sums", [P, TPC * NGRP, 6])
        red = sb("red", [P, 8, TPC])
        combT = sb("combT", [E + 1, CH])
        comb_b = sb("comb_b", [P, 2, PAIRS, HALF])
        mu = sb("mu", [P, MOE_RING, HALF])
        mv = sb("mv", [P, MOE_RING, HALF])
        mh = sb("mh", [P, MOE_RING, HALF])

        ld_x = [sem(f"ld_x{i}") for i in range(NX)]
        ld_attn = sem("ld_attn")
        ld_rope = sem("ld_rope")
        ld_moe = sem("ld_moe")
        ld_combine = [sem(f"ld_combine{half}") for half in range(2)]
        st_combine = sem("st_combine")
        stacked = [sem(f"stacked{i}") for i in range(NX)]
        stacked_pool = sem("stacked_pool")
        maxrow_in = [sem(f"maxrow_in{i}") for i in range(2)]
        stored = sem("stored")
        scores_full = sem("scores_full")
        work_full = sem("work_full")
        pv_done = sem("pv_done")
        y_done = sem("y_done")
        exp_done = sem("exp_done")
        o_ready = sem("o_ready")
        work_read_act = sem("work_read_act")
        part_hi = sem("part_hi")
        part_mid = sem("part_mid")
        gate_exp = sem("gate_exp")
        act_u = sem("act_u")
        act_t = sem("act_t")
        v_set = sem("v_set")
        k_set = sem("k_set")
        q_set = sem("q_set")
        masked = sem("masked")
        pool_chain = sem("pool_chain")
        rope_direct_ready = sem("rope_direct_ready")
        parts_lo = sem("parts_lo")
        xbo_ready = sem("xbo_ready")
        weighted = sem("weighted")
        h_ready = sem("h_ready")
        consts = sem("consts")
        tables_ready = sem("tables_ready")
        rope_a = sem("rope_a")
        chain = sem("chain")
        max_free = sem("max_free")
        work_read_dve = sem("work_read_dve")
        xn_ready = sem("xn_ready")
        xn2_ready = sem("xn2_ready")
        norm_ready = sem("norm_ready")
        norm2_ready = sem("norm2_ready")
        roped_ready = sem("roped_ready")
        neg_ready = sem("neg_ready")
        comb_ready = sem("comb_ready")
        gated = sem("gated")
        out_ready = sem("out_ready")

        N_ATTN, N_ROPE, N_MOE = 7, 6, 15

        def bank(n):
            return psum[:, n, :]

        def wbank(kind, arg):
            return bank(FILL_BANK[FILL[kind, arg]])

        def turned(kind, arg):
            return FILL[kind, arg] + 1

        def direct_table(table, w, c):
            return table[:, w, 4 * c:4 * c + 4, :].unsqueeze(2).broadcast_to([P, TPC, H, HD])

        def weight(engine, x, n):
            at, (half, u) = 2 * UNITS * x + n, unit(n)
            if u == 0:
                engine.wait_ge(ld_combine[half], 32 * (x + 1))
            engine.wait_ge(act_u, at + 1)
            engine.tensor_tensor(mv[:, at % MOE_RING, :], mv[:, at % MOE_RING, :], comb_b[:, half, u, :],
                                 ALU.mult).then_inc(weighted, 1)

        def stack(engine, x, which, lower, done):
            b, c = x // 2, x % 2
            terms = (TERMS_Q, TERMS_K)[which]
            if which == 0 and x >= 2 and not lower:
                engine.wait_ge(scores_full, banks_before(NG * (x - 1)))
            if which == 0 and x < 2 and not lower:
                engine.wait_ge(q_set, x + 1)
            if which == 1 and not lower:
                engine.wait_ge(k_set, x // 2 + 1)
            for part in (1, 2) if lower else (0,):
                if part == 0:
                    engine.wait_ge(part_hi, 2 * x + which + 1)
                elif part == 1:
                    engine.wait_ge(parts_lo, 2 * x + which + 1)
                for t in [t for t, p in enumerate(terms) if p == part]:
                    if which:
                        engine.dma_start(k_st[16 * t:16 * t + 16, b, :, c * CH:(c + 1) * CH],
                                     parts[:, which, part, :]).then_inc(done, 16)
                        continue
                    for par in range(2):
                        row = 16 * t + 8 * par
                        engine.dma_start(q_st[row:row + 8, x % 2, :, par, :],
                                     parts[64 * par:64 * par + 64, which, part, :]).then_inc(done, 16)

        def wait_stacked(engine, x):
            engine.wait_ge(stacked[x], 16 * (N_STACK if x else N_STACK - N_STACK_POOL))
            if x == 0:
                engine.wait_ge(stacked_pool, 16 * N_STACK_POOL)

        block = ctx.enter_context(nc.Block())

        @block.sync
        def _(sp):
            for w, dst in ((Wq, 0), (Wk, 1), (Wv, 2), (Wo, 3)):
                sp.dma_start(w_raw[:, dst, :], w).then_inc(ld_attn, 16)
            sp.dma_start(ident[:, :], c_ident).then_inc(ld_attn, 16)
            sp.dma_start(center[:, :], c_center).then_inc(ld_attn, 16)
            sp.dma_start(gate_raw[:, :], gate_w).then_inc(ld_attn, 16)
            sp.dma_start(rope[:, :, :, :], c_rope).then_inc(ld_rope, 16)
            for n, v in enumerate((q_gamma, q_beta, k_gamma, k_beta)):
                sp.dma_start(gb[:, n, :], v.partition_broadcast(P)).then_inc(ld_rope, 16)
            sp.dma_start(bo_b[:, :], bo.partition_broadcast(P)).then_inc(ld_rope, 16)
            for i in range(1, NX):
                sp.dma_start(xs[:, i, :, :], x_v[i]).then_inc(ld_x[i], 16)
            sp.dma_start(causal[:, :], c_causal).then_inc(ld_moe, 16)
            sp.dma_start(rank[:, :], c_rank).then_inc(ld_moe, 16)
            sp.dma_start(gate_bb[:, :], gate_b.partition_broadcast(P)).then_inc(ld_moe, 16)
            for w, dst, shared in ((We1, w1, ws1), (We3, w3, ws3)):
                sp.dma_start(dst[:, 0:PAIRS, :].rearrange("d p (e i) -> d (p e) i", e=2),
                             w.rearrange("e d i -> d e i")).then_inc(ld_moe, 16)
                sp.dma_start(dst[:, PAIRS, :], shared).then_inc(ld_moe, 16)
            sp.dma_start(w2[:, 0:PAIRS, :], We2.rearrange("(p e) i d -> (e i) p d", e=2)).then_inc(ld_moe, 16)
            sp.dma_start(w2[:, PAIRS, :], ws2).then_inc(ld_moe, 16)
            for v, dst, shared in ((be1, b1, bs1), (be3, b3, bs3)):
                sp.dma_start(dst[:, 0:PAIRS], v.rearrange("(p e) i -> (e i) p", e=2),
                             allow_slow_non_contiguous=True).then_inc(ld_moe, 16)
                sp.dma_start(dst[:, PAIRS:UNITS], shared.rearrange("(i o) -> i o", o=1)).then_inc(ld_moe, 16)
            sp.dma_start(b2[0:E, :], be2).then_inc(ld_moe, 16)
            sp.dma_start(b2[E:E + 1, :], bs2.rearrange("(o d) -> o d", o=1)).then_inc(ld_moe, 16)

            for kind, arg in SCHEDULE:
                if kind == "stack":
                    stack(sp, *arg, stacked[arg[0]])
                elif kind == "mrow":
                    x, g = arg // NG, arg % NG
                    b, c = x // 2, x % 2
                    sp.wait_ge(work_read_dve, frees("dve", FILL["mturn", arg] + 1))
                    sp.dma_start(q_st[KM:P, x % 2, 2 * g:2 * g + 2, :, :],
                                 maxT[:, arg % 2, :]).then_inc(maxrow_in[arg % 2], 16)
                elif kind == "cstore":
                    x = arg
                    sp.wait_ge(work_read_act, frees("act", turned("cT", x)))
                    sp.dma_start(combine_dram[x], combT[0:E, :]).then_inc(st_combine, 16)
                elif kind == "cload":
                    x, half = arg
                    sp.wait_ge(st_combine, 16 * (x + 1))
                    if x >= 1:
                        sp.wait_ge(weighted, PAIRS * (2 * x + half - 1))
                    for e in range(2):
                        src = combine_dram[x].rearrange("(m e) q -> e m q", e=2)[e][:, half * HALF:(half + 1) * HALF]
                        sp.dma_start(comb_b[64 * e:64 * e + 64, half, :, :], src.partition_broadcast(64)
                                     ).then_inc(ld_combine[half], 16)
                elif kind == "store":
                    sp.wait_ge(out_ready, arg + 1)
                    sp.dma_start(out_v[arg], xs[:, arg, :, :]).then_inc(stored, 16)
            sp.wait_ge(stored, 16 * NX)

        @block.tensor
        def _(pe):
            reads = {"act": work_read_act, "dve": work_read_dve, "experts": act_u, "maxima": max_free}

            def wait_read(bank, before):
                earlier = [m for m in range(len(FILLS)) if FILL_BANK[m] == bank and POS[FILLS[m]] < before]
                if earlier:
                    reader = FILLS_READ[FILLS[earlier[-1]][0]][1]
                    pe.wait_ge(reads[reader], frees(reader, earlier[-1] + 1))
                results = [x for x in range(NX) if POS["final", x] < before]
                if bank == Y_BANK and results:
                    pe.wait_ge(out_ready, results[-1] + 1)

            def fill(kind, arg):
                wait_read(FILL_BANK[FILL[kind, arg]], POS[kind, arg])
                return bank(FILL_BANK[FILL[kind, arg]])

            def weights():
                w = fill("weights", 0)
                pe.wait_ge(ld_attn, 16 * N_ATTN)
                pe.matmul(w[:, 0:P], w_raw[:, 0, :], center[:, :], start=True, stop=True)
                pe.matmul(w[:, P:2 * P], w_raw[:, 1, :], center[:, :], start=True, stop=True)
                pe.transpose(w[:, 2 * P:3 * P], w_raw[:, 2, :], ident[:, :]).then_inc(work_full, 1)

            def weights2():
                w = fill("weights2", 0)
                pe.transpose(w[:, 0:P], w_raw[:, 3, :], ident[:, :])
                pe.transpose(w[:, P:P + E], gate_raw[:, :], ident[0:E, 0:E]).then_inc(work_full, 1)

            def turn(kind, arg, src, tiles=TPC):
                w = fill(kind, arg)
                for t in range(tiles):
                    last = pe.transpose(w[:, t * P:(t + 1) * P], src(t), ident[:, :])
                last.then_inc(work_full, 1)

            def qkv(tile):
                x, t = tile // TPC, tile % TPC
                w = fill("qkv", tile)
                if tile == 0:
                    pe.wait_ge(work_read_act, 1)
                pe.wait_ge(work_read_act, frees("act", FILL["xT", x] + 1))
                pe.matmul(w[:, 0:3 * P], xnT[:, t * P:(t + 1) * P], w_qkv[:, :], start=True, stop=True
                          ).then_inc(work_full, 1)

            def maxima(a, u):
                x, g = a // NG, a % NG
                b, c = x // 2, x % 2
                n = MAXES[a, u]
                what, qt, heads, keys = max_units_of(c)[u]
                w = fill("max", (a, u))
                if n == 0:
                    pe.wait_ge(consts, 1)
                if u == 0:
                    for y in range(2 * b, x + 1):
                        wait_stacked(pe, y)
                if what == "diag":
                    nh = len(heads)
                    v = w[:, 0:nh * keys].rearrange("p (h k) -> p h k", h=nh)[:, :, keys - P:keys]
                    pe.matmul(v, ident_bf[:, :], causal_bf[:, :].unsqueeze(1).broadcast_to([P, nh, P]),
                              start=True, stop=False, skip_group_check=True)
                k0 = c * CH if what == "diag" else 0
                for i, j in enumerate(heads):
                    par, m = j % 2, 2 * g + j // 2
                    q0 = qt * P
                    last = pe.matmul(w[:, i * keys:(i + 1) * keys], q_st[0:KM, x % 2, m, par, q0:q0 + P],
                                     k_st[0:KM, b, m, k0:k0 + keys],
                                     start=(what == "full"), stop=True, skip_group_check=True)
                last.then_inc(work_full, 1)

            def max_turn(a):
                w = fill("mturn", a)
                pe.wait_ge(neg_ready, a + 1)
                wb = w.bitcast(BF16)
                for qt in range(TPC):
                    src = negmax[:, qt, :, :, :].rearrange("p r m a -> p (r m a)")
                    last = pe.transpose(wb[0:8, qt * P:(qt + 1) * P], src, ident_bf[:, :])
                last.then_inc(work_full, 1)

            def scores(s, i):
                a, k = BURSTS[s]
                x, g = a // NG, a % NG
                b, c = x // 2, x % 2
                n = BANKS[s, i]
                w = bank(ST_BANK + n % ST_RING)
                if n >= ST_RING:
                    pe.wait_ge(exp_done, n - ST_RING + 1)
                if k == 0 and i == 0:
                    pe.wait_ge(maxrow_in[a % 2], 16 * (a // 2 + 1))
                for j, kt, col, cols, q0 in bursts_of(c)[k][i][0]:
                    par, m = j % 2, 2 * g + j // 2
                    last = pe.matmul(w[:, col:col + cols], k_st[:, b, m, kt * P:(kt + 1) * P],
                                     q_st[:, x % 2, m, par, q0:q0 + cols],
                                     start=True, stop=True)
                last.then_inc(scores_full, 1)

            def pv(s):
                a, k = BURSTS[s]
                x, g = a // NG, a % NG
                b, c = x // 2, x % 2
                acc = bank(ACC_BANK)
                pe.wait_ge(exp_done, BANKS_TO[s])
                if MASKS_TO[s]:
                    pe.wait_ge(masked, MASKS_TO[s])
                if k == 0 and a >= 1:
                    pe.wait_ge(o_ready, a)
                todo = [(r, n) for i, (regions, _) in enumerate(bursts_of(c)[k]) for n in [BANKS[s, i]] for r in regions]
                todo.sort(key=lambda rn: (rn[0][1], rn[0][0]))
                for (j, kt, col, cols, q0), n in todo:
                    last = pe.matmul(acc[32 * j:32 * j + VC, q0:q0 + cols], v_ones[:, b, kt, G * g + j, :],
                                     probs[:, n % P_RING, col:col + cols], start=(kt == 0),
                                     stop=(k == len(bursts_of(c)) - 1), tile_position=(0, 32 * j),
                                     skip_group_check=True)
                last.then_inc(pv_done, 1)

            def project(x):
                w = fill("proj", x)
                pe.wait_ge(work_read_act, frees("act", FILL["onT", x] + 1))
                for t in range(TPC):
                    last = pe.matmul(w[:, t * P:(t + 1) * P], o_normT[:, t * P:(t + 1) * P], w_o[:, 0:P],
                                     start=True, stop=True)
                last.then_inc(work_full, 1)

            def router(x):
                w = fill("gate", x)
                pe.wait_ge(work_read_act, frees("act", FILL["x2T", x] + 1))
                for t in range(TPC):
                    last = pe.matmul(w[:, t * E:(t + 1) * E], x2T[:, x % 2, t * P:(t + 1) * P], w_o[:, P:P + E],
                                     start=True, stop=True)
                last.then_inc(work_full, 1)

            def combine_turn(x):
                w = fill("cT", x)
                pe.wait_ge(comb_ready, x + 1)
                for t in range(TPC):
                    last = pe.transpose(w[0:E, t * P:(t + 1) * P], lg[:, 11, t, :], ident[:, :])
                last.then_inc(work_full, 1)

            def moe(x, n):
                if n == 0 and x == 0:
                    pe.wait_ge(ld_moe, 16 * N_MOE)
                half, u = unit(n)
                w = fill("moe", (x, n))
                if n == 0:
                    pe.wait_ge(work_read_act, frees("act", turned("x2T", x)))
                rhs = x2T[:, x % 2, half * HALF:(half + 1) * HALF]
                pe.matmul(w[:, 0:HALF], w1[:, u, :], rhs, start=True, stop=True)
                pe.matmul(w[:, HALF:CH], w3[:, u, :], rhs, start=True, stop=True).then_inc(work_full, 1)

            def moe_sum(x, n):
                half, u = unit(n)
                y = bank(Y_BANK)
                at = 2 * UNITS * x + n
                if n == 0:
                    wait_read(Y_BANK, POS["moe_y", (x, n)])
                pe.wait_ge(h_ready, at + 1)
                for t in range(2):
                    tok = 2 * half + t
                    last = pe.matmul(y[:, tok * P:(tok + 1) * P], mh[:, at % MOE_RING, t * P:(t + 1) * P], w2[:, u, :],
                                     start=(n == 0 and t == 0), stop=(n == 2 * UNITS - 1), skip_group_check=True)
                if n == BIAS_STEP:
                    pe.wait_ge(work_read_act, frees("act", turned("cT", x)))
                    for t in range(TPC):
                        last = pe.matmul(y[:, t * P:(t + 1) * P], combT[:, t * P:(t + 1) * P], b2[:, :],
                                         start=False, stop=False, skip_group_check=True)
                last.then_inc(y_done, 1)

            for kind, arg in SCHEDULE:
                if kind == "weights":
                    weights()
                elif kind == "weights2":
                    weights2()
                elif kind == "xT":
                    pe.wait_ge(xn_ready, arg + 1)
                    turn(kind, arg, lambda t: xn[:, t, :])
                elif kind == "qkv":
                    qkv(arg)
                elif kind in ("qT", "kT"):
                    which = int(kind == "kT")
                    pe.wait_ge(roped_ready, arg + 1)
                    turn(kind, arg, lambda t, w=which: roped[:, w, t, :, :, :].rearrange("p r d m -> p (r d m)"))
                elif kind == "max":
                    maxima(*arg)
                elif kind == "mturn":
                    max_turn(arg)
                elif kind == "scores":
                    scores(*arg)
                elif kind == "pv":
                    pv(arg)
                elif kind == "oT":
                    pe.wait_ge(o_ready, arg + 1)
                    turn(kind, arg, lambda t: o_raw[:, t * P:(t + 1) * P])
                elif kind == "onT":
                    pe.wait_ge(work_read_dve, frees("dve", turned("oT", NG * arg + NG - 1)))
                    turn(kind, arg, lambda t: o_norm[:, t, :])
                elif kind == "proj":
                    project(arg)
                elif kind == "x2T":
                    pe.wait_ge(xn2_ready, arg + 1)
                    turn(kind, arg, lambda t: w_raw[:, t, :])
                elif kind == "gate":
                    router(arg)
                elif kind == "cT":
                    combine_turn(arg)
                elif kind == "moe":
                    moe(*arg)
                elif kind == "moe_y":
                    moe_sum(*arg)

        @block.scalar
        def _(act):
            act.dma_start(xs[:, 0, :, :], x_v[0]).then_inc(ld_x[0], 16)

            def exp(s, i):
                n = BANKS[s, i]
                act.wait_ge(scores_full, n + 1)
                if n >= P_RING:
                    old = next(q for q in range(len(BURSTS)) if BANKS_TO[q] > n - P_RING)
                    act.wait_ge(pv_done, old + 1)
                act.activation(probs[:, n % P_RING, :], bank(ST_BANK + n % ST_RING), ACT.Exp,
                               scale=SCALE).then_inc(exp_done, 1)

            def keep(kind, arg, dst, cols):
                act.wait_ge(work_full, turned(kind, arg))
                act.copy(dst, wbank(kind, arg)[:, 0:cols]).then_inc(work_read_act, 1)

            def qkv(tile):
                x, t = tile // TPC, tile % TPC
                b, kt = x // 2, tile % KT
                act.wait_ge(work_full, turned("qkv", tile))
                w = wbank("qkv", tile)
                if x >= 1:
                    act.wait_ge(roped_ready, x)
                both = w[:, 0:2 * P].rearrange("p (w h d) -> p w h d", w=2, h=H)
                act.copy(qk[:, :, t, :, :], both)
                act.activation(sq[:, :, t, :, :], both, ACT.Square)
                if t == 0:
                    act.wait_ge(v_set, b + 1)
                act.copy(v_ones[:, b, kt, :, 0:HD], w[:, 2 * P:3 * P].rearrange("p (h d) -> p h d", h=H)
                         ).then_inc(work_read_act, 1)

            def leading_part(kind, x):
                which = int(kind == "kT")
                act.wait_ge(work_full, turned(kind, x))
                if x >= 1:
                    wait_stacked(act, x - 1)
                act.copy(parts[:, which, 0, :], wbank(kind, x)).then_inc(part_hi, 1)

            def moe(x, n):
                at, u = 2 * UNITS * x + n, unit(n)[1]
                act.wait_ge(work_full, turned("moe", (x, n)))
                if x == 0 and n == 0:
                    act.wait_ge(consts, 3)
                if at >= MOE_RING:
                    act.wait_ge(h_ready, at - MOE_RING + 1)
                act.activation(mu[:, at % MOE_RING, :], wbank("moe", (x, n))[:, 0:HALF], ACT.Identity,
                               bias=b1h[:, u:u + 1], scale=0.5)
                act.activation(mv[:, at % MOE_RING, :], wbank("moe", (x, n))[:, HALF:CH], ACT.Identity,
                               bias=b3[:, u:u + 1]).then_inc(act_u, 1)

            def moe_tanh(x, n):
                at = 2 * UNITS * x + n
                act.wait_ge(act_u, at + 1)
                if at >= MOE_RING:
                    act.wait_ge(y_done, at - MOE_RING + 1)
                act.activation(mh[:, at % MOE_RING, :], mu[:, at % MOE_RING, :], ACT.Tanh).then_inc(act_t, 1)

            def normalised(kind, x):
                which = int(kind == "norm2_apply")
                dst, ready = ((xn, xn_ready), (w_raw, xn2_ready))[which]
                act.wait_ge((norm_ready, norm2_ready)[which], x + which)
                if x >= 1:
                    act.wait_ge(work_full, turned(("xT", "x2T")[which], x - 1))
                elif which:
                    act.wait_ge(work_full, turned("weights2", 0))
                for t in range(TPC):
                    last = act.activation(dst[:, t, :], xs[:, x, t, :], ACT.Identity,
                                          bias=shift[:, which, t:t + 1], scale=rstd[:, which, t:t + 1])
                last.then_inc(ready, 1)

            def leave(a):
                act.wait_ge(pv_done, max(s for s, (q, _) in enumerate(BURSTS) if q == a) + 1)
                if a >= 1:
                    act.wait_ge(work_full, turned("oT", a - 1))
                act.copy(o_raw[:, :], bank(ACC_BANK)).then_inc(o_ready, 1)

            for kind, arg in SCHEDULE:
                if kind in ("norm_apply", "norm2_apply"):
                    normalised(kind, arg)
                elif kind == "weights_read":
                    keep("weights", arg, w_qkv[:, :], 3 * P)
                elif kind == "weights2_read":
                    keep("weights2", arg, w_o[:, :], P + E)
                elif kind == "xT_read":
                    keep("xT", arg, xnT[:, :], CH)
                elif kind == "qkv_read":
                    qkv(arg)
                elif kind in ("qT_lead", "kT_lead"):
                    leading_part(kind[:2], arg)
                elif kind == "exp":
                    exp(*arg)
                elif kind == "leave":
                    leave(arg)
                elif kind == "onT_read":
                    keep("onT", arg, o_normT[:, :], CH)
                elif kind == "x2T_read":
                    keep("x2T", arg, x2T[:, arg % 2, :], CH)
                elif kind == "cT_read":
                    act.wait_ge(work_full, turned("cT", arg))
                    if arg == 0:
                        act.wait_ge(consts, 3)
                    else:
                        act.wait_ge(st_combine, 16 * arg)
                        act.wait_ge(y_done, 2 * UNITS * (arg - 1) + BIAS_STEP + 1)
                    act.copy(combT[0:E, :], wbank("cT", arg)[0:E, :]).then_inc(work_read_act, 1)
                elif kind == "gate_exp":
                    act.wait_ge(work_read_dve, frees("dve", turned("gate", arg)))
                    act.activation(lg[:, 1, :, :], lg[:, 0, :, :], ACT.Exp).then_inc(gate_exp, 1)
                elif kind == "moe_u":
                    moe(*arg)
                elif kind == "moe_t":
                    moe_tanh(*arg)

        @block.gpsimd
        def _(pool):
            links = [0]

            def link(ins):
                links[0] += 1
                ins.then_inc(pool_chain, 1)
                pool.wait_ge(pool_chain, links[0])

            def rope_direct(x):
                c = x % 2
                if x == 0:
                    pool.wait_ge(tables_ready, 1)
                pool.wait_ge(rope_a, x + 1)
                for w in range(1 if x == 0 else 2):
                    for tab, src, op in ((g_cos, sq, ALU.mult), (g_add, qk, ALU.add)):
                        last = pool.tensor_tensor(qk[:, w, :, :, :], src[:, w, :, :, :], direct_table(tab, w, c), op)
                        if op == ALU.mult:
                            link(last)
                last.then_inc(rope_direct_ready, 1)

            def lower_parts(kind, x):
                which = int(kind == "kT")
                pool.wait_ge(part_mid, 2 * x + which + 1)
                pool.tensor_tensor(parts[:, which, 2, :], resid[:, which, :], parts[:, which, 1, :],
                                   ALU.subtract).then_inc(parts_lo, 1)

            for kind, arg in SCHEDULE:
                if kind == "stack_pool":
                    stack(pool, 0, 1, True, stacked_pool)
                elif kind == "ones":
                    pool.memset(v_ones[:, arg, :, :, :], 1.0).then_inc(v_set, 1)
                    pool.memset(k_st[:, arg, :, :].rearrange("p m q -> p (m q)").bitcast(F32), TWO_ONES).then_inc(k_set, 1)
                elif kind == "zero":
                    pool.memset(q_st[:, arg, :, :, :].rearrange("p m r q -> p (m r q)").bitcast(F32), 0.0).then_inc(q_set, 1)
                elif kind == "xbo":
                    if arg == 0:
                        pool.wait_ge(ld_rope, 16 * N_ROPE)
                    pool.wait_ge(xn_ready, arg + 1)
                    pool.tensor_tensor(xs[:, arg, :, :], xs[:, arg, :, :],
                                       bo_b[:, :].unsqueeze(1).broadcast_to([P, TPC, P]), ALU.add
                                       ).then_inc(xbo_ready, 1)
                elif kind == "rope_pool":
                    rope_direct(arg)
                elif kind in ("qT_low", "kT_low"):
                    lower_parts(kind[:2], arg)
                elif kind == "mask":
                    s, i = arg
                    a, k = BURSTS[s]
                    blocks, n = bursts_of(a // NG % 2)[k][i][1], BANKS[arg]
                    pool.wait_ge(exp_done, n + 1)
                    v = probs[:, n % P_RING, :].rearrange("p (r q) -> p r q", q=P)[:, blocks, :]
                    pool.affine_select(out=v, in_=v, compare_op=ALU.is_ge, fill=0.0, base=0,
                                       pattern=[[0, v.shape[1]], [1, P]], channel_multiplier=-1
                                       ).then_inc(masked, 1)
                elif kind == "weight":
                    weight(pool, *arg)
                elif kind == "moe_h":
                    x, n = arg
                    at, (half, u) = 2 * UNITS * x + n, unit(n)
                    pool.wait_ge(gated, at + 1)
                    if u < PAIRS:
                        pool.wait_ge(weighted, PAIRS * (2 * x + half) + u + 1)
                    pool.tensor_tensor(mh[:, at % MOE_RING, :], mh[:, at % MOE_RING, :], mv[:, at % MOE_RING, :],
                                       ALU.mult).then_inc(h_ready, 1)

        @block.vector
        def _(dve):
            links = [0]

            def link(ins):
                links[0] += 1
                ins.then_inc(chain, 1)
                dve.wait_ge(chain, links[0])

            def rsqrt(out, v, n):
                y, half, sq_v = seed[:, 0:n].bitcast(F32), nr[:, 0, 0:n], nr[:, 1, 0:n]
                link(dve.tensor_scalar(seed[:, 0:n], v.bitcast(I32), 1, None, ALU.logical_shift_right))
                link(dve.tensor_scalar(seed[:, 0:n], seed[:, 0:n], -1, RSQRT_SEED, ALU.mult, ALU.add))
                for step in range(3):
                    link(dve.scalar_tensor_tensor(out=half, in0=y, scalar=-0.5, in1=y, op0=ALU.mult, op1=ALU.mult))
                    link(dve.tensor_tensor(sq_v, half, v, ALU.mult))
                    last = dve.scalar_tensor_tensor(out=(y if step < 2 else out), in0=sq_v, scalar=1.5, in1=y,
                                                    op0=ALU.add, op1=ALU.mult)
                    link(last)

            def norm(kind, x):
                for t in range(TPC):
                    last = dve.bn_stats(stats[:, t, :], xs[:, x, t, :])
                link(last)
                for t in range(TPC):
                    last = dve.bn_aggr(mean_var[:, t, :], stats[:, t, :])
                link(last)
                which = int(kind == "norm2")
                if x >= 1:
                    dve.wait_ge((xn_ready, xn2_ready)[which], x)
                r = rstd[:, which, :]
                link(dve.tensor_scalar(r, mean_var[:, :, 1], EPS, None, ALU.add))
                rsqrt(r, r, TPC)
                if (kind, x) == ("norm", 0):
                    for t in range(TPC):
                        last = dve.tensor_scalar(xn[:, t, :], xs[:, x, t, :], mean_var[:, t, 0:1],
                                                 rstd[:, 0, t:t + 1], ALU.subtract, ALU.mult)
                    last.then_inc(xn_ready, 1)
                    return
                dve.scalar_tensor_tensor(out=shift[:, which, :], in0=mean_var[:, :, 0], scalar=-1.0, in1=r,
                                         op0=ALU.mult, op1=ALU.mult).then_inc((norm_ready, norm2_ready)[which], 1)

            def head_sums(x):
                dve.wait_ge(work_read_act, frees("act", turned("qkv", TPC * x + TPC - 1)))
                link(dve.tensor_reduce(ssum[:, :], sq[:, :, :, :, :].rearrange("p w t h d -> p (w t h) d"), AX.X,
                                       ALU.add))

            def head_rstd(x):
                link(dve.tensor_scalar(hvar[:, :], ssum[:, :], 1.0 / HD, EPS, ALU.mult, ALU.add))
                rsqrt(hrstd[:, :], hvar[:, :], 2 * TPC * H)

            def head_scale(x):
                dve.tensor_tensor(sq[:, :, :, :, :].rearrange("p w t h d -> p (w t h) d"),
                                  qk[:, :, :, :, :].rearrange("p w t h d -> p (w t h) d"),
                                  hrstd[:, :].unsqueeze(2).broadcast_to([P, 2 * TPC * H, HD]),
                                  ALU.mult).then_inc(rope_a, 1)

            def rope_rotated(x):
                c = x % 2
                dve.wait_ge(rope_a, x + 1)
                if x == 0:
                    dve.wait_ge(tables_ready, 1)
                if x >= 1:
                    dve.wait_ge(work_full, turned("kT", x - 1))
                for w in range(2):
                    for j in range(2):
                        for par in range(2):
                            t = g_sin[:, w, 4 * c:4 * c + 4, 4 * j:4 * j + 4].unsqueeze(2).broadcast_to([P, TPC, H // 2, 4])
                            last = dve.tensor_tensor(by_head(w, par)[:, :, :, 4 * j:4 * j + 4],
                                                     sq[:, w, :, par::2, 1 - j::2], t, ALU.mult)
                link(last)
                if x == 0:
                    link(dve.tensor_tensor(qk[:, 1, :, :, :], sq[:, 1, :, :, :], direct_table(g_cos, 1, c), ALU.mult))
                    link(dve.tensor_tensor(qk[:, 1, :, :, :], qk[:, 1, :, :, :], direct_table(g_add, 1, c), ALU.add))

            def by_head(w, par):
                return roped[:, w, :, par, :, :].rearrange("p t d m -> p t m d")

            def rope_sum(x):
                dve.wait_ge(rope_direct_ready, x + 1)
                for w in range(2):
                    for par in range(2):
                        last = dve.tensor_tensor(by_head(w, par), qk[:, w, :, par::2, :], by_head(w, par), ALU.add)
                last.then_inc(roped_ready, 1)

            def remainder(kind, x):
                which = int(kind == "kT")
                dve.wait_ge(part_hi, 2 * x + which + 1)
                if x >= 1:
                    dve.wait_ge(parts_lo, 2 * x)
                dve.tensor_tensor(resid[:, which, :], wbank(kind, x), parts[:, which, 0, :],
                                  ALU.subtract).then_inc(work_read_dve, 1)
                dve.wait_ge(work_read_dve, frees("dve", turned(kind, x)))
                if x >= 1:
                    wait_stacked(dve, x - 1)
                dve.tensor_copy(parts[:, which, 1, :], resid[:, which, :]).then_inc(part_mid, 1)

            def maxima(a, u):
                what, qt, heads, keys = max_units_of(a // NG % 2)[u]
                j, nh = heads[0], len(heads)
                w = wbank("max", (a, u))[:, 0:nh * keys].rearrange("p (h k) -> p h k", h=nh)
                dst = mx_full if what == "full" else mx_diag
                if u == 0 and a >= 1:
                    dve.wait_ge(neg_ready, a)
                dve.wait_ge(work_full, turned("max", (a, u)))
                dve.tensor_reduce(dst[:, qt, j // 2:j // 2 + nh, j % 2], w, AX.X, ALU.max).then_inc(max_free, 1)

            def max_negate(a):
                dve.wait_ge(max_free, MAXES[a, len(max_units_of(a // NG % 2)) - 1] + 1)
                m = mx_diag[:, :, :, :].rearrange("p t m a -> p t (m a)")
                if a // NG % 2:
                    link(dve.tensor_tensor(mx[:, :, :], m, mx_full[:, :, :, :].rearrange("p t m a -> p t (m a)"), ALU.max))
                    m = mx[:, :, :]
                if a >= 1:
                    dve.wait_ge(work_full, turned("mturn", a - 1))
                hi, lo = [negmax[:, :, r, :, :].rearrange("p t m a -> p t (m a)") for r in range(2)]
                link(dve.tensor_scalar(hi, m, -1.0, None, ALU.mult))
                dve.scalar_tensor_tensor(out=lo, in0=m, scalar=-1.0, in1=hi,
                                         op0=ALU.mult, op1=ALU.subtract).then_inc(neg_ready, 1)

            def max_copy(a):
                dve.wait_ge(work_full, turned("mturn", a))
                if a >= 2:
                    dve.wait_ge(maxrow_in[a % 2], 16 * (a // 2))
                dve.tensor_copy(maxT[:, a % 2, :], wbank("mturn", a).bitcast(BF16)[0:8, 0:CH]).then_inc(work_read_dve, 1)

            def normalise(a):
                g = a % NG
                dve.wait_ge(work_full, turned("oT", a))
                w = wbank("oT", a).rearrange("p (t j v) -> p t j v", t=TPC, j=G)
                link(dve.reciprocal(rden[:, :, :, :], w[:, :, :, HD:HD + 1]))
                dst = o_norm[:, :, G * HD * g:G * HD * (g + 1)].rearrange("p t (j d) -> p t j d", j=G)
                last = dve.tensor_tensor(dst, w[:, :, :, 0:HD], rden[:, :, :, :].broadcast_to([P, TPC, G, HD]), ALU.mult)
                last.then_inc(work_read_dve, 1)

            def two_largest(v, ranks, width, t, small, out_mask):
                link(dve.tensor_reduce(small[0], v, AX.X, ALU.max))
                for turn in range(2):
                    link(dve.tensor_tensor(t[0], v if turn == 0 else t[2], wide(small[0], width), ALU.is_equal))
                    link(dve.tensor_tensor(t[0], t[0], ranks, ALU.mult))
                    link(dve.tensor_reduce(small[1], t[0], AX.X, ALU.max))
                    link(dve.tensor_tensor(t[1 + 2 * turn], t[0], wide(small[1], width), ALU.is_equal))
                    if turn == 0:
                        link(dve.scalar_tensor_tensor(out=t[2], in0=t[1], scalar=3 * MASKED, in1=v,
                                                      op0=ALU.mult, op1=ALU.add))
                        link(dve.tensor_reduce(small[0], t[2], AX.X, ALU.max))
                link(dve.tensor_tensor(out_mask, t[1], t[3], ALU.add))

            def router(x):
                dve.wait_ge(work_full, turned("gate", x))
                w = wbank("gate", x)[:, 0:TPC * E].rearrange("p (t e) -> p t e", t=TPC)

                link(dve.tensor_reduce(red[:, 0, :], w, AX.X, ALU.max))
                dve.tensor_tensor(lg[:, 0, :, :], w, wide(red[:, 0, :]), ALU.subtract).then_inc(work_read_dve, 1)

            def grouped(m):
                return m.rearrange("p t (g e) -> p (t g) e", g=NGRP)

            def wide(m, width=E):
                return m.unsqueeze(2).broadcast_to([P, m.shape[1], width])

            def route1(x):
                dve.wait_ge(gate_exp, x + 1)
                link(dve.tensor_reduce(red[:, 1, :], lg[:, 1, :, :], AX.X, ALU.add))
                link(dve.reciprocal(red[:, 2, :], red[:, 1, :]))
                link(dve.tensor_tensor(lg[:, 2, :, :], lg[:, 1, :, :], wide(red[:, 2, :]), ALU.mult))
                link(dve.tensor_tensor(lg[:, 3, :, :], lg[:, 2, :, :],
                                       gate_bb[:, :].unsqueeze(1).broadcast_to([P, TPC, E]), ALU.add))
                s = grouped(lg[:, 3, :, :])
                dve.tensor_tensor(pair_sums[:, :, 0:3], s[:, :, 0:3], s[:, :, 1:4], ALU.add)
                dve.tensor_tensor(pair_sums[:, :, 3:5], s[:, :, 0:2], s[:, :, 2:4], ALU.add)
                link(dve.tensor_tensor(pair_sums[:, :, 5:6], s[:, :, 0:1], s[:, :, 3:4], ALU.add))
                link(dve.tensor_reduce(gsm[:, 0, :, :].rearrange("p t g -> p (t g)"), pair_sums[:, :, :], AX.X, ALU.max))

            def route2(x):
                two_largest(gsm[:, 0, :, :], rank[:, E - NGRP:E].unsqueeze(1).broadcast_to([P, TPC, NGRP]), NGRP,
                            [gsm[:, 1 + i, :, :] for i in range(4)], (red[:, 3, :], red[:, 4, :]), gsm[:, 5, :, :])
                link(dve.tensor_scalar(gsm[:, 6, :, :], gsm[:, 5, :, :], -MASKED, MASKED, ALU.mult, ALU.add))
                per = [gsm[:, i, :, :].rearrange("p t g -> p (t g)") for i in (5, 6)]
                link(dve.tensor_tensor(grouped(lg[:, 4, :, :]), grouped(lg[:, 3, :, :]), wide(per[0], E // NGRP), ALU.mult))
                link(dve.tensor_tensor(grouped(lg[:, 5, :, :]), grouped(lg[:, 4, :, :]), wide(per[1], E // NGRP), ALU.add))

            def route3(x):
                two_largest(lg[:, 5, :, :], rank[:, :].unsqueeze(1).broadcast_to([P, TPC, E]), E,
                            [lg[:, 6 + i, :, :] for i in range(4)], (red[:, 5, :], red[:, 6, :]), lg[:, 10, :, :])
                dve.tensor_tensor(lg[:, 11, :, :], lg[:, 2, :, :], lg[:, 10, :, :], ALU.mult).then_inc(comb_ready, 1)

            def gate_unit(x, n):
                at = 2 * UNITS * x + n
                dve.wait_ge(act_t, at + 1)
                dve.scalar_tensor_tensor(out=mh[:, at % MOE_RING, :], in0=mh[:, at % MOE_RING, :], scalar=1.0,
                                         in1=mu[:, at % MOE_RING, :], op0=ALU.add, op1=ALU.mult).then_inc(gated, 1)

            def tables():
                dve.wait_ge(ld_rope, 16 * N_ROPE)
                dve.tensor_copy(gb_rot[:, :, 0:4], gb[:, :, 1::2])
                link(dve.tensor_copy(gb_rot[:, :, 4:8], gb[:, :, 0::2]))
                for w in range(2):
                    def affine(m, i, w=w):
                        return m[:, 2 * w + i, :].unsqueeze(1).broadcast_to([P, KT, HD])
                    dve.tensor_tensor(g_cos[:, w, :, :], rope[:, :, 0, :], affine(gb, 0), ALU.mult)
                    dve.tensor_tensor(g_sin[:, w, :, :], rope[:, :, 1, :], affine(gb_rot, 0), ALU.mult)
                    dve.tensor_tensor(g_add[:, w, :, :], rope[:, :, 0, :], affine(gb, 1), ALU.mult)
                    link(dve.tensor_tensor(g_tmp[:, w, :, :], rope[:, :, 1, :], affine(gb_rot, 1), ALU.mult))
                dve.tensor_tensor(g_add[:, :, :, :], g_add[:, :, :, :], g_tmp[:, :, :, :], ALU.add).then_inc(tables_ready, 1)

            link(dve.memset(combT[:, :], 1.0))
            dve.memset(bank(ACC_BANK), 0.0)
            for kind, arg in SCHEDULE:
                if kind == "tables":
                    tables()
                elif kind == "norm":
                    dve.wait_ge(ld_x[arg], 16)
                    norm(kind, arg)
                elif kind == "norm2":
                    dve.wait_ge(work_read_dve, frees("dve", turned("proj", arg)))
                    norm(kind, arg)
                elif kind == "headsum":
                    head_sums(arg)
                elif kind == "headrstd":
                    head_rstd(arg)
                elif kind == "headscale":
                    head_scale(arg)
                elif kind == "rope":
                    rope_rotated(arg)
                elif kind == "rope_sum":
                    rope_sum(arg)
                elif kind in ("qT_rest", "kT_rest"):
                    remainder(kind[:2], arg)
                    if kind == "kT_rest" and arg == 0:
                        dve.wait_ge(ld_moe, 16 * N_MOE)
                        dve.wait_ge(ld_attn, 16 * N_ATTN)
                        dve.tensor_copy(ident_bf[:, :], ident[:, :])
                        dve.tensor_copy(causal_bf[:, :], causal[:, :]).then_inc(consts, 1)
                        dve.memset(ones_col[:, :], 1.0).then_inc(consts, 1)
                        dve.tensor_scalar(b1h[:, :], b1[:, :], 0.5, None, ALU.mult).then_inc(consts, 1)
                elif kind == "maxred":
                    maxima(*arg)
                elif kind == "mneg":
                    max_negate(arg)
                elif kind == "mcopy":
                    max_copy(arg)
                elif kind == "oT_read":
                    normalise(arg)
                elif kind == "proj_read":
                    dve.wait_ge(work_full, turned("proj", arg))
                    dve.wait_ge(xbo_ready, arg + 1)
                    dve.tensor_tensor(xs[:, arg, :, :], wbank("proj", arg).rearrange("p (t d) -> p t d", t=TPC),
                                      xs[:, arg, :, :], ALU.add).then_inc(work_read_dve, 1)
                elif kind == "gate_read":
                    router(arg)
                elif kind == "route1":
                    route1(arg)
                elif kind == "route2":
                    route2(arg)
                elif kind == "route3":
                    route3(arg)
                elif kind == "weight_dve":
                    weight(dve, *arg)
                elif kind == "gated":
                    gate_unit(*arg)
                elif kind == "final":
                    dve.wait_ge(y_done, 2 * UNITS * (arg + 1))
                    dve.tensor_tensor(xs[:, arg, :, :], bank(Y_BANK).rearrange("p (t d) -> p t d", t=TPC),
                                      xs[:, arg, :, :], ALU.add).then_inc(out_ready, 1)
    return nc


_INS = ["x", "Wq", "Wk", "Wv", "q_gamma", "q_beta", "k_gamma", "k_beta", "Wo", "bo"]
_FFN = ["gate_w", "gate_b", "We1", "be1", "We2", "be2", "We3", "be3", "ws1", "bs1", "ws2", "bs2", "ws3", "bs3"]


def shape_constants():
    f = np.float32
    ident = np.eye(P, dtype=f)
    center = (ident - np.kron(np.eye(H, dtype=f), np.full((HD, HD), 1.0 / HD, f))).astype(f)
    q, k = np.arange(P)[:, None], np.arange(P)[None, :]
    causal = np.where(k > q, f(MASKED), f(0)).astype(f)
    di = np.arange(0, HD, 2, dtype=f) / f(HD)
    theta = np.arange(S, dtype=f)[:, None] * np.exp(-di * f(np.log(10000.0)))
    cos, sin = (np.repeat(fn(theta.astype(f)), 2, axis=1).astype(f) for fn in (np.cos, np.sin))
    sin[:, 0:HD // 2] *= -1
    rope = np.stack([cos, sin], axis=1).reshape(KT, P, 2, HD).transpose(1, 0, 2, 3)
    rank = np.broadcast_to(np.arange(E, 0, -1, dtype=f), (P, E))
    return {"c_ident": ident, "c_center": center, "c_causal": causal, "c_rope": rope, "c_rank": rank}


def kernel(**inputs):
    import concourse.bacc as _bacc
    from concourse.bass_utils import run_bass_kernel_spmd as _run

    nc = _bacc.Bacc("TRN2", target_bir_lowering=False, num_devices=1)
    given = {n: inputs["L0_attn_" + n] for n in _INS} | {n: inputs["L0_ffn_" + n] for n in _FFN} | shape_constants()
    arrays, args = {}, []
    for name, a in given.items():
        a = np.ascontiguousarray(a)
        arrays["in_" + name] = a
        args.append(nc.dram_tensor("in_" + name, a.shape, mybir.dt.from_np(a.dtype), kind="ExternalInput").ap())
    out = nc.dram_tensor("out_0", (B, S, D), F32, kind="ExternalOutput").ap()
    layer_kernel(nc, *args, out)
    r = _run(nc, [arrays], core_ids=[0])
    return r.results[0]["out_0"]
```
